# Optimizing a Trainium2 kernel written in Bass

```python
import numpy as np
import jax
import jax.numpy as jnp

def _softmax(x, axis=-1):
    return jax.nn.softmax(x, axis=axis)

def _gelu(x):
    return jax.nn.gelu(x, approximate=True)

def _silu(x):
    return jax.nn.silu(x)

def _sigmoid(x):
    return jax.nn.sigmoid(x)

def _layernorm(x, axis=-1, eps=1e-05):
    m = jnp.mean(x, axis=axis, keepdims=True)
    v = jnp.var(x, axis=axis, keepdims=True)
    return (x - m) / jnp.sqrt(v + eps)

def _scatter_add(tgt, idx, src, axis=0):
    return tgt.at[idx].add(src)

def _segment_sum(src, seg, n):
    return jax.ops.segment_sum(src, seg, n)
kernel_name = 'mk_hybrid_d1_jaxref_r8_b66715'

def setup_inputs(seed: int=0):
    np.random.seed(seed)
    _w = jnp.asarray

    def _L0_attn_a_setup():
        import jax, jax.numpy as jnp
        import numpy as np
        B, L, DM = (2, 256, 256)
        EXPAND, D_STATE, D_CONV, H, CS = (2, 128, 4, 32, 32)
        D_INNER = EXPAND * DM
        HD = D_INNER // H
        N = D_STATE
        PROJ = 2 * D_INNER + 2 * H * N + H
        key = jax.random.key(seed)
        ks = jax.random.split(key, 8)
        x = jax.random.normal(ks[0], (B, L, DM), jnp.float32)
        W_in = jax.random.normal(ks[1], (PROJ, DM), jnp.float32) * 0.02
        conv_w = jax.random.normal(ks[2], (D_INNER, 1, D_CONV), jnp.float32) * 0.2
        conv_b = jnp.zeros((D_INNER,), jnp.float32)
        A_log = jnp.full((H,), jnp.log(2.0), jnp.float32)
        D_param = jnp.ones((D_INNER,), jnp.float32)
        dt_bias = jnp.zeros((H,), jnp.float32)
        W_out = jax.random.normal(ks[3], (DM, D_INNER), jnp.float32) * 0.02
        return {'x': x, 'W_in': W_in, 'conv_w': conv_w, 'conv_b': conv_b, 'A_log': A_log, 'D_param': D_param, 'dt_bias': dt_bias, 'W_out': W_out}
    _L0_attn_a_in = _L0_attn_a_setup()

    def _L0_attn_b_setup():
        import jax, jax.numpy as jnp
        import numpy as np
        from jax import lax
        H = 256
        HK = 16
        KD = 128
        HV = 32
        DV = 128
        CK = 4
        VEFF = HV // HK * DV

        def _causal_group_conv(x, w, b):
            xc = jnp.transpose(x, (0, 2, 1))
            xc = jnp.pad(xc, ((0, 0), (0, 0), (CK - 1, 0)))
            y = lax.conv_general_dilated(xc, w, window_strides=(1,), padding='VALID', dimension_numbers=('NCH', 'OIH', 'NCH'), feature_group_count=HK)
            y = y + b[None, :, None]
            return jnp.transpose(y, (0, 2, 1))

        def _reference_tuple_inner(hidden_states, Wq, Wk, Wv, Wo, Wq_conv, bq_conv, Wk_conv, bk_conv, Wg, bg, Wb, bb):
            B, S, _ = hidden_states.shape
            q = hidden_states @ Wq.T
            k = hidden_states @ Wk.T
            v = hidden_states @ Wv.T
            q = jax.nn.silu(_causal_group_conv(q, Wq_conv, bq_conv))
            k = jax.nn.silu(_causal_group_conv(k, Wk_conv, bk_conv))
            gate = jax.nn.sigmoid(hidden_states @ Wg.T + bg)
            beta = jax.nn.sigmoid(hidden_states @ Wb.T + bb)
            q = q.reshape(B, S, HK, KD)
            k = k.reshape(B, S, HK, KD)
            v = v.reshape(B, S, HK, VEFF)
            qT = jnp.transpose(q, (1, 0, 2, 3))
            kT = jnp.transpose(k, (1, 0, 2, 3))
            vT = jnp.transpose(v, (1, 0, 2, 3))
            bT = jnp.transpose(beta, (1, 0, 2))
            gT = jnp.transpose(gate, (1, 0, 2))
            S0 = jnp.zeros((B, HK, KD, VEFF), hidden_states.dtype)

            def step(St, xs):
                qt, kt, vt, bt, gt = xs
                St = bt[:, :, None, None] * St + kt[..., None] * vt[:, :, None, :]
                ot = jnp.einsum('bhk,bhkv->bhv', qt, St) * gt[..., None]
                return (St, ot)
            Sf, outs = lax.scan(step, S0, (qT, kT, vT, bT, gT))
            out = jnp.transpose(outs, (1, 0, 2, 3)).reshape(B, S, HV * DV)
            out = out @ Wo.T
            return (out, Sf)
        key = jax.random.key(seed)
        ks = jax.random.split(key, 13)
        sc = 0.02
        n = lambda k, sh: jax.random.normal(k, sh, jnp.float32) * sc
        return {'hidden_states': jax.random.normal(ks[0], (1, 256, H), jnp.float32), 'Wq': n(ks[1], (HK * KD, H)), 'Wk': n(ks[2], (HK * KD, H)), 'Wv': n(ks[3], (HV * DV, H)), 'Wo': n(ks[4], (H, HV * DV)), 'Wq_conv': n(ks[5], (HK * KD, KD, CK)), 'bq_conv': n(ks[6], (HK * KD,)), 'Wk_conv': n(ks[7], (HK * KD, KD, CK)), 'bk_conv': n(ks[8], (HK * KD,)), 'Wg': n(ks[9], (HK, H)), 'bg': n(ks[10], (HK,)), 'Wb': n(ks[11], (HK, H)), 'bb': n(ks[12], (HK,))}
    _L0_attn_b_in = _L0_attn_b_setup()

    def _L0_ffn_setup():
        import jax, jax.numpy as jnp
        import numpy as np
        TOP_K = 4

        def _silu_and_mul(gu):
            g, u = jnp.split(gu, 2, axis=-1)
            return jax.nn.silu(g) * u
        key = jax.random.key(seed)
        ks = jax.random.split(key, 7)
        H, E, I, Is = (256, 16, 176, 704)
        s = 0.02
        return {'hidden_states': jax.random.normal(ks[0], (4, 128, H), dtype=jnp.float32), 'gate_w': jax.random.normal(ks[1], (E, H), dtype=jnp.float32) * s, 'sgate_w': jax.random.normal(ks[2], (1, H), dtype=jnp.float32) * s, 'w13': jax.random.normal(ks[3], (E, 2 * I, H), dtype=jnp.float32) * s, 'w2': jax.random.normal(ks[4], (E, H, I), dtype=jnp.float32) * s, 'shared_gate_up_w': jax.random.normal(ks[5], (2 * Is, H), dtype=jnp.float32) * s, 'shared_down_w': jax.random.normal(ks[6], (H, Is), dtype=jnp.float32) * s}
    _L0_ffn_in = _L0_ffn_setup()
    _d = {'L0_attn_a_x': _L0_attn_a_in['x'], 'L0_attn_a_W_in': _L0_attn_a_in['W_in'], 'L0_attn_a_conv_w': _L0_attn_a_in['conv_w'], 'L0_attn_a_conv_b': _L0_attn_a_in['conv_b'], 'L0_attn_a_A_log': _L0_attn_a_in['A_log'], 'L0_attn_a_D_param': _L0_attn_a_in['D_param'], 'L0_attn_a_dt_bias': _L0_attn_a_in['dt_bias'], 'L0_attn_a_W_out': _L0_attn_a_in['W_out'], 'L0_attn_b_Wq': _L0_attn_b_in['Wq'], 'L0_attn_b_Wk': _L0_attn_b_in['Wk'], 'L0_attn_b_Wv': _L0_attn_b_in['Wv'], 'L0_attn_b_Wo': _L0_attn_b_in['Wo'], 'L0_attn_b_Wq_conv': _L0_attn_b_in['Wq_conv'], 'L0_attn_b_bq_conv': _L0_attn_b_in['bq_conv'], 'L0_attn_b_Wk_conv': _L0_attn_b_in['Wk_conv'], 'L0_attn_b_bk_conv': _L0_attn_b_in['bk_conv'], 'L0_attn_b_Wg': _L0_attn_b_in['Wg'], 'L0_attn_b_bg': _L0_attn_b_in['bg'], 'L0_attn_b_Wb': _L0_attn_b_in['Wb'], 'L0_attn_b_bb': _L0_attn_b_in['bb'], 'L0_ffn_gate_w': _L0_ffn_in['gate_w'], 'L0_ffn_sgate_w': _L0_ffn_in['sgate_w'], 'L0_ffn_w13': _L0_ffn_in['w13'], 'L0_ffn_w2': _L0_ffn_in['w2'], 'L0_ffn_shared_gate_up_w': _L0_ffn_in['shared_gate_up_w'], 'L0_ffn_shared_down_w': _L0_ffn_in['shared_down_w']}
    _x0 = _d['L0_attn_a_x']
    _d['L0_attn_a_x'] = jax.random.normal(jax.random.fold_in(jax.random.key(seed), 1), (4, 256, 256), dtype=_x0.dtype)
    del _x0
    return _d

def reference(L0_attn_a_x, L0_attn_a_W_in, L0_attn_a_conv_w, L0_attn_a_conv_b, L0_attn_a_A_log, L0_attn_a_D_param, L0_attn_a_dt_bias, L0_attn_a_W_out, L0_attn_b_Wq, L0_attn_b_Wk, L0_attn_b_Wv, L0_attn_b_Wo, L0_attn_b_Wq_conv, L0_attn_b_bq_conv, L0_attn_b_Wk_conv, L0_attn_b_bk_conv, L0_attn_b_Wg, L0_attn_b_bg, L0_attn_b_Wb, L0_attn_b_bb, L0_ffn_gate_w, L0_ffn_sgate_w, L0_ffn_w13, L0_ffn_w2, L0_ffn_shared_gate_up_w, L0_ffn_shared_down_w):

    def _L0_attn_a_ref(x, W_in, conv_w, conv_b, A_log, D_param, dt_bias, W_out):
        import jax, jax.numpy as jnp
        import numpy as np
        B, L, DM = (2, 256, 256)
        EXPAND, D_STATE, D_CONV, H, CS = (2, 128, 4, 32, 32)
        D_INNER = EXPAND * DM
        HD = D_INNER // H
        N = D_STATE
        PROJ = 2 * D_INNER + 2 * H * N + H
        b, l, _ = x.shape
        proj = x @ W_in.T
        val, gate, Bp, Cp, dt = jnp.split(proj, [D_INNER, 2 * D_INNER, 2 * D_INNER + H * N, 2 * D_INNER + 2 * H * N], axis=-1)
        vc = jax.lax.conv_general_dilated(val.transpose(0, 2, 1), conv_w, (1,), [(D_CONV - 1, 0)], dimension_numbers=('NCH', 'OIH', 'NCH'), feature_group_count=D_INNER)
        val = jax.nn.silu(vc.transpose(0, 2, 1) + conv_b)
        val = val.reshape(b, l, H, HD)
        Bp = Bp.reshape(b, l, H, N)
        Cp = Cp.reshape(b, l, H, N)
        dt = jax.nn.softplus(dt + dt_bias)
        ld = dt * -jnp.exp(A_log)
        nC = l // CS
        mask = jnp.tril(jnp.ones((CS, CS), bool))
        Dh = D_param.reshape(1, H, 1, HD)

        def chunk(h, inp):
            val_c, B_c, C_c, ld_c = inp
            cum = jnp.cumsum(ld_c, axis=1)
            cumh = cum.transpose(0, 2, 1)
            diff = jnp.where(mask, cumh[:, :, :, None] - cumh[:, :, None, :], -jnp.inf)
            CB = jnp.einsum('blhn,bmhn->bhlm', C_c, B_c)
            M = CB * jnp.exp(diff)
            val_ch = val_c.transpose(0, 2, 1, 3)
            Y = M @ val_ch + jnp.einsum('blhn,bhdn,blh->bhld', C_c, h, jnp.exp(cum)) + Dh * val_ch
            last = cum[:, -1, :]
            h_new = jnp.exp(last)[:, :, None, None] * h + jnp.einsum('blhd,blhn,blh->bhdn', val_c, B_c, jnp.exp(last[:, None, :] - cum))
            return (h_new, Y)
        inps = tuple((jnp.moveaxis(a.reshape(b, nC, CS, *a.shape[2:]), 1, 0) for a in (val, Bp, Cp, ld)))
        h0 = jnp.zeros((b, H, HD, N), jnp.float32)
        _, Ys = jax.lax.scan(chunk, h0, inps)
        Y = Ys.transpose(1, 0, 3, 2, 4).reshape(b, l, D_INNER)
        Y = Y * jax.nn.silu(gate)
        return Y @ W_out.T

    def _L0_attn_b_ref(hidden_states, Wq, Wk, Wv, Wo, Wq_conv, bq_conv, Wk_conv, bk_conv, Wg, bg, Wb, bb):
        import jax, jax.numpy as jnp
        import numpy as np
        from jax import lax
        H = 256
        HK = 16
        KD = 128
        HV = 32
        DV = 128
        CK = 4
        VEFF = HV // HK * DV

        def _causal_group_conv(x, w, b):
            xc = jnp.transpose(x, (0, 2, 1))
            xc = jnp.pad(xc, ((0, 0), (0, 0), (CK - 1, 0)))
            y = lax.conv_general_dilated(xc, w, window_strides=(1,), padding='VALID', dimension_numbers=('NCH', 'OIH', 'NCH'), feature_group_count=HK)
            y = y + b[None, :, None]
            return jnp.transpose(y, (0, 2, 1))

        def _reference_tuple_inner(hidden_states, Wq, Wk, Wv, Wo, Wq_conv, bq_conv, Wk_conv, bk_conv, Wg, bg, Wb, bb):
            B, S, _ = hidden_states.shape
            q = hidden_states @ Wq.T
            k = hidden_states @ Wk.T
            v = hidden_states @ Wv.T
            q = jax.nn.silu(_causal_group_conv(q, Wq_conv, bq_conv))
            k = jax.nn.silu(_causal_group_conv(k, Wk_conv, bk_conv))
            gate = jax.nn.sigmoid(hidden_states @ Wg.T + bg)
            beta = jax.nn.sigmoid(hidden_states @ Wb.T + bb)
            q = q.reshape(B, S, HK, KD)
            k = k.reshape(B, S, HK, KD)
            v = v.reshape(B, S, HK, VEFF)
            qT = jnp.transpose(q, (1, 0, 2, 3))
            kT = jnp.transpose(k, (1, 0, 2, 3))
            vT = jnp.transpose(v, (1, 0, 2, 3))
            bT = jnp.transpose(beta, (1, 0, 2))
            gT = jnp.transpose(gate, (1, 0, 2))
            S0 = jnp.zeros((B, HK, KD, VEFF), hidden_states.dtype)

            def step(St, xs):
                qt, kt, vt, bt, gt = xs
                St = bt[:, :, None, None] * St + kt[..., None] * vt[:, :, None, :]
                ot = jnp.einsum('bhk,bhkv->bhv', qt, St) * gt[..., None]
                return (St, ot)
            Sf, outs = lax.scan(step, S0, (qT, kT, vT, bT, gT))
            out = jnp.transpose(outs, (1, 0, 2, 3)).reshape(B, S, HV * DV)
            out = out @ Wo.T
            return (out, Sf)
        return _reference_tuple_inner(hidden_states, Wq, Wk, Wv, Wo, Wq_conv, bq_conv, Wk_conv, bk_conv, Wg, bg, Wb, bb)[0]

    def _L0_ffn_ref(hidden_states, gate_w, sgate_w, w13, w2, shared_gate_up_w, shared_down_w):
        import jax, jax.numpy as jnp
        import numpy as np
        TOP_K = 4

        def _silu_and_mul(gu):
            g, u = jnp.split(gu, 2, axis=-1)
            return jax.nn.silu(g) * u
        B, S, H = hidden_states.shape
        x = hidden_states.reshape(-1, H)
        E = gate_w.shape[0]
        shared = _silu_and_mul(x @ shared_gate_up_w.T) @ shared_down_w.T
        shared = shared * jax.nn.sigmoid(x @ sgate_w.T)
        router_logits = x @ gate_w.T
        routing_weights = jax.nn.softmax(router_logits.astype(jnp.float32), axis=-1)
        topk_w, topk_ids = jax.lax.top_k(routing_weights, TOP_K)

        def body(acc, ew):
            w13_e, w2_e, e = ew
            coef = jnp.sum(jnp.where(topk_ids == e, topk_w, 0.0), axis=-1)
            h = _silu_and_mul(x @ w13_e.T)
            acc = acc + (h @ w2_e.T).astype(jnp.float32) * coef[:, None]
            return (acc, None)
        init = jnp.zeros((x.shape[0], H), dtype=jnp.float32)
        sparse_out, _ = jax.lax.scan(body, init, (w13, w2, jnp.arange(E)))
        out = shared + sparse_out.astype(x.dtype)
        return out.reshape(B, S, H)
    x = L0_attn_a_x
    x = x + _L0_attn_a_ref(_layernorm(x, axis=-1), L0_attn_a_W_in, L0_attn_a_conv_w, L0_attn_a_conv_b, L0_attn_a_A_log, L0_attn_a_D_param, L0_attn_a_dt_bias, L0_attn_a_W_out)
    x = x + _L0_ffn_ref(_layernorm(x, axis=-1), L0_ffn_gate_w, L0_ffn_sgate_w, L0_ffn_w13, L0_ffn_w2, L0_ffn_shared_gate_up_w, L0_ffn_shared_down_w)
    x = x + _L0_attn_b_ref(_layernorm(x, axis=-1), L0_attn_b_Wq, L0_attn_b_Wk, L0_attn_b_Wv, L0_attn_b_Wo, L0_attn_b_Wq_conv, L0_attn_b_bq_conv, L0_attn_b_Wk_conv, L0_attn_b_bk_conv, L0_attn_b_Wg, L0_attn_b_bg, L0_attn_b_Wb, L0_attn_b_bb)
    x = x + _L0_ffn_ref(_layernorm(x, axis=-1), L0_ffn_gate_w, L0_ffn_sgate_w, L0_ffn_w13, L0_ffn_w2, L0_ffn_shared_gate_up_w, L0_ffn_shared_down_w)
    return x

_drawn_inputs = setup_inputs


def setup_inputs(seed=0):
    import zlib

    import numpy as np

    out = dict(_drawn_inputs(seed))
    spreads = {'L0_attn_a_conv_b': (0.0, 0.8),
     'L0_attn_a_A_log': (0.6931471824645996, 0.6),
     'L0_attn_a_D_param': (1.0, 0.6),
     'L0_attn_a_dt_bias': (0.0, 0.8)}
    factors = {'L0_attn_a_W_in': 4.567,
     'L0_attn_a_conv_w': 4.758,
     'L0_attn_a_W_out': 3.854,
     'L0_attn_b_Wq': 3.734,
     'L0_attn_b_Wk': 3.667,
     'L0_attn_b_Wv': 3.616,
     'L0_attn_b_Wo': 3.618,
     'L0_attn_b_Wq_conv': 3.681,
     'L0_attn_b_bq_conv': 8.0,
     'L0_attn_b_Wk_conv': 3.619,
     'L0_attn_b_bk_conv': 8.0,
     'L0_attn_b_Wg': 8.0,
     'L0_attn_b_bg': 8.0,
     'L0_attn_b_Wb': 8.0,
     'L0_attn_b_bb': 8.0,
     'L0_ffn_gate_w': 8.0,
     'L0_ffn_sgate_w': 64.0,
     'L0_ffn_w13': 8.0,
     'L0_ffn_w2': 8.0,
     'L0_ffn_shared_gate_up_w': 8.0,
     'L0_ffn_shared_down_w': 8.0}
    for name, (base, spread) in spreads.items():
        noise = np.random.default_rng([zlib.crc32(name.encode()), seed]).standard_normal(out[name].shape)
        drawn = base * np.exp(spread * noise) if base else spread * noise
        out[name] = jnp.asarray(drawn.astype(out[name].dtype))
    for name, factor in factors.items():
        out[name] = (out[name] * factor).astype(out[name].dtype)
    return out
```

```python
from contextlib import ExitStack

import numpy as np

import concourse.bass as bass
from concourse import mybir

F32 = mybir.dt.float32
FR = mybir.dt.float32r
BF16 = mybir.dt.bfloat16
ALU = mybir.AluOpType
ACT = mybir.ActivationFunctionType
AX_X = mybir.AxisListType.X

P = 128
BATCH, SEQ, DM = 4, 256, 256
TOKENS = BATCH * SEQ
KT = DM // P
CHUNK = 512
CHUNKS = TOKENS // CHUNK
BLOCKS = TOKENS // P
EPS = 1e-5
MASKED = -1e30

A_HEADS, A_STATE, A_HD, A_TAPS = 32, 128, 16, 4
A_INNER = A_HEADS * A_HD
A_TILES = A_INNER // P
A_GROUP = P // A_HD
UNITS = A_GROUP * BATCH
OUT_UNIT = 8
PADDED = SEQ + A_TAPS - 1

B_HEADS, B_KD, B_V, B_TAPS = 16, 128, 256, 4
B_VT = B_V // P

EXPERTS, TOP_K, E_HIDDEN, S_HIDDEN = 16, 4, 176, 704
ROWS_E = P // EXPERTS
R_TILES = E_HIDDEN // ROWS_E
S_TILES = -(-S_HIDDEN // P)
F_TILES = S_TILES + R_TILES
LOGITS = 32

QKW, VW, CONVW, WOW = KT * 2 * P, KT * B_V, 2 * B_TAPS * P, B_VT * DM
TRI = 3 * P

N_CONST = 2 * P + 32 + EXPERTS * EXPERTS
N_APAR = A_TILES * (A_TAPS + 2) + 2
N_BPAR = 2


def build_layer(nc, xT, consts, a_vg, a_dt, a_heads, a_wo, a_par, ffn_w, router_w, b_qk, b_v, b_conv, b_wo,
                b_bg, b_par, out):
    ctx = ExitStack()
    with ctx:
        sems = {}

        def sem(name):
            if name not in sems:
                sems[name] = ctx.enter_context(nc.semaphore(name))
            return sems[name]

        def sb(stack, name, shape, dt=F32):
            return stack.enter_context(nc.sbuf_tensor(name, shape, dt))

        def pair(stack, name, shape):
            return sb(stack, name + "_hi", shape, FR), sb(stack, name + "_lo", shape, FR)

        x = sb(ctx, "x", [P, KT, TOKENS])
        xn = pair(ctx, "xn", [P, KT, TOKENS])
        const = sb(ctx, "const", [P, N_CONST])
        ident = const[:, 0:P]
        tri = const[:, 2 * P + 32:N_CONST].rearrange("p (e j) -> p e j", e=EXPERTS)
        ident_b = sb(ctx, "ident_b", [P, P], BF16)
        mask_b = sb(ctx, "mask_b", [P, 2, P], BF16)
        rows_b = sb(ctx, "rows_b", [P, 32], BF16)
        mean_w = sb(ctx, "mean_w", [P, P])
        zero_w = sb(ctx, "zero_w", [P, P], BF16)
        zero_x = sb(ctx, "zero_x", [P, CHUNK], BF16)
        ps = ctx.enter_context(nc.psum_tensor("ps", [P, 8, CHUNK], F32))

        pro = ExitStack()
        ln_xc = sb(pro, "ln_xc", [P, KT, TOKENS])
        ln_sq = sb(pro, "ln_sq", [P, KT, TOKENS])
        ln_v = sb(pro, "ln_v", [P, TOKENS])
        ln_r = sb(pro, "ln_r", [P, TOKENS])
        ln_t = sb(pro, "ln_t", [P, TOKENS])
        pro.close()

        ma = ExitStack()
        valz = pair(ma, "valz", [P, A_GROUP, BLOCKS, P])
        bc_at = ExitStack()
        bmat = [pair(bc_at, f"bmat{p}", [P, TOKENS]) for p in range(2)]
        cmat = [pair(bc_at, f"cmat{p}", [P, TOKENS]) for p in range(2)]
        bc_at.close()
        pro = ExitStack()
        a_vg_raw = sb(pro, "a_vg_raw", [P, A_TILES, KT, 2, P])
        a_vg_w = pair(pro, "a_vg_w", [P, A_TILES, KT, 2, P])
        a_dt_raw = sb(pro, "a_dt_raw", [P, KT, P])
        a_dt_w = pair(pro, "a_dt_w", [P, KT, P])
        pro.close()
        ma2 = ExitStack()
        bc_hold = sb(ma2, "bc_hold", [P, 8 * TOKENS])
        valT = sb(ma2, "valT", [P, A_TILES, TOKENS])
        gateT = sb(ma2, "gateT", [P, A_TILES, TOKENS])
        e_a = sb(ma2, "e_a", [P, 2, TRI])
        m_a = sb(ma2, "m_a", [P, 2, TRI])
        ms_a = pair(ma2, "ms_a", [P, 3, TRI])
        aw_raw = sb(ma2, "aw_raw", [P, 2, KT, 2, P])
        aw = pair(ma2, "aw", [P, 2, KT, 2, P])
        awo_raw = sb(ma2, "awo_raw", [P, DM])
        awo = pair(ma2, "awo", [P, DM])
        yT = sb(ma2, "yT", [P, TOKENS])
        ys = pair(ma2, "ys", [P, TOKENS])
        stage = sb(ma2, "stage", [P, TOKENS])
        pieces_a = sb(ma2, "pieces_a", [P, BATCH, TRI], BF16)
        ncum_a = sb(ma2, "ncum_a", [P, BLOCKS, 32])
        apar = sb(ma2, "apar", [P, N_APAR])
        neg_a = sb(ma2, "neg_a", [P, 1])
        ma2.close()
        ma.close()
        tmp = ExitStack()
        sb(tmp, "valz_hi_hold", [P, A_GROUP * BLOCKS * P])
        vpad = sb(tmp, "vpad", [P, A_TILES, BATCH, PADDED])
        vacc = sb(tmp, "vacc", [P, BATCH, SEQ])
        dec_z = sb(tmp, "dec_z", [P, TOKENS])
        dec_e = sb(tmp, "dec_e", [P, TOKENS])
        tmp.close()
        a_conv_w = apar[:, 0:A_TILES * A_TAPS].rearrange("p (t j) -> p t j", j=A_TAPS)
        a_conv_b = apar[:, A_TILES * A_TAPS:A_TILES * (A_TAPS + 1)]
        a_d = apar[:, A_TILES * (A_TAPS + 1):A_TILES * (A_TAPS + 2)]
        a_log = apar[:, N_APAR - 2:N_APAR - 1]
        a_dt_b = apar[:, N_APAR - 1:N_APAR]

        mb = ExitStack()
        sb(mb, "ln_hold_b", [P, 7 * TOKENS])
        qpad = pair(mb, "qpad", [P, 2, BATCH, PADDED])
        qk = [pair(mb, f"qk{p}", [P, 2, TOKENS]) for p in range(2)]
        qf = sb(mb, "qf", [P, 2, CHUNK])
        vtok = [pair(mb, f"vtok{p}", [P, BLOCKS, B_V]) for p in range(2)]
        pro = ExitStack()
        wbg_raw = sb(pro, "wbg_raw", [P, KT, 2, P])
        wbg = pair(pro, "wbg", [P, KT, 2, P])
        pro.close()
        oT = pair(mb, "oT", [P, B_VT, TOKENS])
        e_b = sb(mb, "e_b", [P, 2, TRI])
        m_b = sb(mb, "m_b", [P, 2, TRI])
        ms_b = pair(mb, "ms_b", [P, 2, TRI])
        wqk_raw = sb(mb, "wqk_raw", [P, KT, 2, P])
        wqk = pair(mb, "wqk", [P, KT, 2, P])
        wv_raw = sb(mb, "wv_raw", [P, KT, B_V])
        wv = pair(mb, "wv", [P, KT, B_V])
        wconv_raw_all = sb(mb, "wconv_raw", [P, CONVW + 2])
        wconv_raw = wconv_raw_all[:, 0:CONVW].rearrange("p (s j m) -> p s j m", s=2, j=B_TAPS)
        conv_bias = sb(mb, "conv_bias", [P, 2])
        wconv = pair(mb, "wconv", [P, 2, B_TAPS, P])
        wo_raw = sb(mb, "wo_raw", [P, B_VT, DM])
        wo = pair(mb, "wo", [P, B_VT, DM])
        pieces_b = sb(mb, "pieces_b", [P, BATCH, TRI], BF16)
        ncum_b = sb(mb, "ncum_b", [P, BLOCKS, 32])
        bpar = sb(mb, "bpar", [P, N_BPAR])
        mb.close()
        tmp = ExitStack()
        dec_b = [sb(tmp, f"dec_b{i}", [P, TOKENS]) for i in range(6)]
        tmp.close()

        mf = ExitStack()
        sb(mf, "ln_hold_f", [P, 7 * TOKENS])
        fw_raw = sb(mf, "fw_raw", [P, 2, KT * 2 * P + DM])
        fgu = pair(mf, "fgu", [P, 2, KT, 2, P])
        fd = pair(mf, "fd", [P, 2, DM])
        f_s = sb(mf, "f_s", [P, CHUNKS, CHUNK])
        f_sc = sb(mf, "f_sc", [P, CHUNKS, CHUNK])
        f_h = sb(mf, "f_h", [P, CHUNKS, CHUNK])
        fh = pair(mf, "fh", [P, 2, TOKENS])
        coef_r = sb(mf, "coef_r", [P, TOKENS])
        coef_s = sb(mf, "coef_s", [P, TOKENS])
        rw_raw = sb(mf, "rw_raw", [P, KT, LOGITS])
        rw = pair(mf, "rw", [P, KT, LOGITS])
        lg = sb(mf, "lg", [P, BLOCKS, LOGITS])
        pr = sb(mf, "pr", [P, BLOCKS, EXPERTS])
        r_mx = sb(mf, "r_mx", [P, BLOCKS])
        r_sum = sb(mf, "r_sum", [P, BLOCKS])
        r_gate = sb(mf, "r_gate", [P, BLOCKS])
        r_gt = sb(mf, "r_gt", [P, BLOCKS, EXPERTS, EXPERTS])
        r_eq = sb(mf, "r_eq", [P, BLOCKS, EXPERTS, EXPERTS])
        r_rank = sb(mf, "r_rank", [P, BLOCKS, EXPERTS])
        cexp = sb(mf, "cexp", [P, BLOCKS, EXPERTS, ROWS_E])
        sexp = sb(mf, "sexp", [P, BLOCKS, P])
        mf.close()

        def f32(ap):
            return ap.bitcast(F32)

        def mm3(o, w, v, first, last=True):
            nc.tensor.matmul(o, w[0], v[0], start=first, stop=False, skip_group_check=True)
            nc.tensor.matmul(o, w[0], v[1], start=False, stop=False, skip_group_check=True)
            return nc.tensor.matmul(o, w[1], v[0], start=False, stop=last, skip_group_check=True)

        def at(t, *idx):
            return tuple(v[idx] for v in t)

        def half_view(ap):
            return ap.rearrange("p (h n) -> p h n", n=P)

        def halves(t):
            return tuple(half_view(v) for v in t)

        def first_m(ap):
            return half_view(ap[:, 0:TRI])[:, 0:3:2, :]

        def cols(c):
            return slice(c * CHUNK, (c + 1) * CHUNK)

        def counter(eng, name, start=0):
            n = [start]

            def step(ins):
                n[0] += 1
                ins.then_inc(sem(name), 1)
                eng.wait_ge(sem(name), n[0])
            return step

        X_FINAL = {0: lambda c: 16, 1: lambda c: 4 * A_TILES + 2 * c + 2, 2: lambda c: 2 * c + 2,
                   3: lambda c: 4 * B_HEADS + 2 * c + 2, 4: lambda c: 2 * c + 2}

        def x_final(eng, n, c):
            eng.wait_ge(sem(f"x_updated{n}"), X_FINAL[n](c))

        def mean_bank(n):
            return 6 if n % 2 else 0

        def norm_pe(pe, n):
            pe.wait_ge(sem("consts_made"), 1)
            for c in range(CHUNKS):
                x_final(pe, n, c)
                for k in range(KT):
                    ins = nc.tensor.matmul(ps[:, mean_bank(n) + c, :], mean_w[:], x[:, k, cols(c)], start=k == 0, stop=k == KT - 1)
                ins.then_inc(sem("ln_mean"), 1)
            for c in range(CHUNKS):
                pe.wait_ge(sem("ln_sq"), CHUNKS * n + c + 1)
                for k in range(KT):
                    ins = nc.tensor.matmul(ps[:, 2 + c, :], mean_w[:], ln_sq[:, k, cols(c)], start=k == 0, stop=k == KT - 1)
                ins.then_inc(sem("ln_var"), 1)

        def norm_act(act, n):
            for c in range(CHUNKS):
                act.wait_ge(sem("ln_xc"), CHUNKS * n + c + 1)
                nc.scalar.activation(ln_sq[:, :, cols(c)], ln_xc[:, :, cols(c)], ACT.Square).then_inc(sem("ln_sq"), 1)
            for c in range(CHUNKS):
                act.wait_ge(sem("ln_v"), CHUNKS * n + c + 1)
                nc.scalar.activation(ln_t[:, cols(c)], ln_v[:, cols(c)], ACT.Sqrt).then_inc(sem("ln_std"), 1)
            for c in range(CHUNKS):
                act.wait_ge(sem("ln_xn"), CHUNKS * n + c + 1)
                nc.scalar.copy(xn[0][:, :, cols(c)], ln_xc[:, :, cols(c)]).then_inc(sem("ln_hi"), 1)

        def norm_dve(dve, n):
            step = counter(dve, "ln_step", 5 * CHUNKS * n)
            for c in range(CHUNKS):
                dve.wait_ge(sem("ln_mean"), CHUNKS * n + c + 1)
                mean = ps[:, mean_bank(n) + c, None, :].broadcast_to([P, KT, CHUNK])
                nc.vector.tensor_tensor(ln_xc[:, :, cols(c)], x[:, :, cols(c)], mean,
                                        ALU.subtract).then_inc(sem("ln_xc"), 1)
            for c in range(CHUNKS):
                dve.wait_ge(sem("ln_var"), CHUNKS * n + c + 1)
                nc.vector.tensor_scalar(ln_v[:, cols(c)], ps[:, 2 + c, :], EPS, None, ALU.add).then_inc(sem("ln_v"), 1)
            for c in range(CHUNKS):
                r, t, v = ln_r[:, cols(c)], ln_t[:, cols(c)], ln_v[:, cols(c)]
                dve.wait_ge(sem("ln_std"), CHUNKS * n + c + 1)
                step(nc.vector.reciprocal(r, t))
                step(nc.vector.tensor_tensor(t, r, r, ALU.mult))
                step(nc.vector.tensor_tensor(t, t, v, ALU.mult))
                step(nc.vector.tensor_scalar(t, t, -0.5, 1.5, ALU.mult, ALU.add))
                step(nc.vector.tensor_tensor(r, r, t, ALU.mult))
                rb = ln_r[:, None, cols(c)].broadcast_to([P, KT, CHUNK])
                nc.vector.tensor_tensor(ln_xc[:, :, cols(c)], ln_xc[:, :, cols(c)], rb,
                                        ALU.mult).then_inc(sem("ln_xn"), 1)
            for c in range(CHUNKS):
                dve.wait_ge(sem("ln_hi"), CHUNKS * n + c + 1)
                nc.vector.tensor_tensor(xn[1][:, :, cols(c)], ln_xc[:, :, cols(c)], f32(xn[0][:, :, cols(c)]),
                                        ALU.subtract).then_inc(sem("ln_done"), 1)

        def normed(eng, n):
            eng.wait_ge(sem("ln_done"), CHUNKS * n + CHUNKS)

        def split_hi(dst, src, hi_sem):
            return nc.scalar.copy(dst[0], src).then_inc(sem(hi_sem), 1)

        def split_lo(pool, dst, src, hi_sem, count, done_sem):
            pool.wait_ge(sem(hi_sem), count)
            return nc.gpsimd.tensor_tensor(dst[1], src, f32(dst[0]), ALU.subtract).then_inc(sem(done_sem), 1)

        def a_pe(pe):
            normed(pe, 0)
            pe.wait_ge(sem("a_pro_w"), 2)
            n = 0
            for t in range(-1, A_TILES):
                for s in range(1 if t < 0 else 2):
                    for c in range(CHUNKS):
                        if n >= 8:
                            pe.wait_ge(sem("a_pro_read"), n - 7)
                        for k in range(KT):
                            w = at(a_dt_w, slice(None), k) if t < 0 else at(a_vg_w, slice(None), t, k, s)
                            ins = mm3(ps[:, n % 8, :], w, at(xn, slice(None), k, cols(c)), k == 0, k == KT - 1)
                        ins.then_inc(sem("a_pro_done"), 1)
                        n += 1
            pe.wait_ge(sem("a_cum"), 1)
            pe.wait_ge(sem("a_pro_read"), n)
            for i in range(BLOCKS):
                ins = nc.tensor.transpose(ps[:, 2, i * 32:(i + 1) * 32], dec_e[0:32, i * P:(i + 1) * P], ident[0:32, 0:32])
            ins.then_inc(sem("a_cumT"), 1)
            pe.wait_ge(sem("a_ncum"), 1)
            a_project_pe(pe, 0, 0, 0)
            a_project_pe(pe, 0, 0, 1)
            a_project_pe(pe, 0, 0, 2)
            a_project_pe(pe, 0, 0, 3)
            pe.wait_ge(sem("a_pieces"), 6)
            with pe.Fori(0, A_TILES - 1) as g:
                a_group_pe(pe, g, False)
            a_group_pe(pe, A_TILES - 1, True)
            for n in range(4):
                if n >= 2:
                    pe.wait_ge(sem("x_updated1"), 4 * A_TILES + n - 1)
                a_out_pe(pe, A_TILES, n, n % 2)

        def a_project_pe(pe, h, parity, q):
            s, c = q // 2, q % 2
            if q == 0:
                pe.wait_ge(sem("aw_split"), h + 1)
            if not (isinstance(h, int) and h == 0 and q < 2):
                pe.wait_ge(sem("bc_split"), 4 * h + q - 1)
            for k in range(KT):
                ins = mm3(ps[:, c, :], at(aw, slice(None), parity, k, s), at(xn, slice(None), k, cols(c)),
                          k == 0, k == KT - 1)
            ins.then_inc(sem("a_p_done"), 1)

        def a_out_pe(pe, g, n, bank):
            c, m = n // KT, n % KT
            if n == 0:
                pe.wait_ge(sem("ys_split"), 2 * g + 2)
                pe.wait_ge(sem("awo_split"), g + 1)
            mm3(ps[:, bank, :], at(awo, slice(None), slice(m * P, (m + 1) * P)), at(ys, slice(None), cols(c)),
                True).then_inc(sem("a_wo_done"), 1)

        def a_state_pe(pe, g, u):
            j, b = u // BATCH, u % BATCH
            p, l0 = j % 2, b * SEQ
            if u >= 2:
                pe.wait_ge(sem("a_m_done"), UNITS * g + u - 1)
            if b % 2 == 0:
                pe.wait_ge(sem("bc_split"), UNITS * g + 4 * j + 3 + b // 2)
            d, s = ps[:, 2 + u % 2, :], ps[:, 4 + u % 2, :]
            lhs = rows_b[:, bass.ds(g * A_GROUP + j, 1)].broadcast_to([P, P])
            nc.tensor.matmul(d[:, 0:TRI], lhs, pieces_a[:, b, :], start=True, stop=False, skip_group_check=True)
            nc.tensor.matmul(d[:, 0:2 * P], ident_b[:], mask_b[:].rearrange("p d n -> p (d n)"), start=False, stop=True, skip_group_check=True)
            mm3(first_m(s), at(bmat[p], slice(None), slice(l0, l0 + P)), halves(at(cmat[p], slice(None), slice(l0, l0 + SEQ))), True, False)
            mm3(s[:, P:2 * P], at(bmat[p], slice(None), slice(l0 + P, l0 + SEQ)),
                at(cmat[p], slice(None), slice(l0 + P, l0 + SEQ)), False).then_inc(sem("a_s_done"), 1)

        def a_value_pe(pe, g, u):
            j, b = u // BATCH, u % BATCH
            pe.wait_ge(sem("a_m_split"), UNITS * g + u + 1)
            if u == 0:
                pe.wait_ge(sem("valz_split"), 2 * g + 2)
                pe.wait_ge(sem("y_read"), 2 * g + 2)
            o, l0, t = ps[:, 6 + b // 2, :], (b % 2) * SEQ, 2 * b
            ms = at(ms_a, slice(None), u % 3)
            mm3(half_view(o[:, l0:l0 + SEQ]), at(valz, slice(None), j, t), tuple(first_m(v) for v in ms),
                j == 0 and b % 2 == 0, False)
            mm3(o[:, l0 + P:l0 + SEQ], at(valz, slice(None), j, t + 1), at(ms, slice(None), slice(P, 2 * P)),
                False, j == A_GROUP - 1).then_inc(sem("a_y_done"), 1)

        def a_group_pe(pe, g, last):
            pe.wait_ge(sem("stage_ready"), g + 1)
            pe.wait_ge(sem("bc_split"), UNITS * g + BATCH)
            for i in range(BLOCKS):
                ins = nc.tensor.transpose(ps[:, i // 4, (i % 4) * P:(i % 4 + 1) * P], stage[:, i * P:(i + 1) * P], ident)
                if i % 4 == 3:
                    ins.then_inc(sem("val_T"), 1)
            for u in range(UNITS):
                a_state_pe(pe, g, u)
                if u < 2:
                    pe.wait_ge(sem("valz_split"), 2 * g + u + 1)
                n = u - OUT_UNIT
                if 0 < n <= 4:
                    pe.wait_ge(sem("x_updated1"), 4 * g + n)
                if not (last and u >= UNITS - BATCH):
                    a_project_pe(pe, g * A_GROUP + u // BATCH + 1, (u // BATCH + 1) % 2, u % BATCH)
                if 0 <= n < 4:
                    pe.wait_ge(sem("bc_split"), UNITS * g + BATCH + u)
                    a_out_pe(pe, g, n, (u + 1) % 2)
                if u >= 2:
                    a_value_pe(pe, g, u - 2)
            a_value_pe(pe, g, UNITS - 2)
            a_value_pe(pe, g, UNITS - 1)

        def a_act(act):
            act.wait_ge(sem("a_params"), 16)
            act.wait_ge(sem("a_pro_loaded"), 32)
            split_hi(at(a_dt_w, slice(None)), a_dt_raw[:], "a_pro_hi")
            split_hi(at(a_vg_w, slice(None)), a_vg_raw[:], "a_pro_hi")
            for h in range(2):
                act.wait_ge(sem(f"aw_loaded{h}"), 16)
                split_hi(at(aw, slice(None), h), aw_raw[:, h], "aw_hi")
            act.wait_ge(sem("awo_loaded"), 16)
            split_hi(at(awo, slice(None)), awo_raw[:], "awo_hi")
            n = 0
            for c in range(CHUNKS):
                act.wait_ge(sem("a_pro_done"), n + 1)
                nc.scalar.activation(dec_z[:, cols(c)], ps[:, n, :], ACT.Identity, bias=a_dt_b).then_inc(sem("a_pro_read"), 1)
                n += 1
            act.wait_ge(sem("a_abs"), 1)
            nc.scalar.activation(dec_e[:], dec_e[:], ACT.Exp, scale=-1.0).then_inc(sem("a_exp"), 1)
            act.wait_ge(sem("a_exp"), 1)
            nc.scalar.activation(dec_e[:], dec_e[:], ACT.Ln, bias=1.0).then_inc(sem("a_ln"), 1)
            nc.scalar.activation(neg_a[:], a_log, ACT.Exp).then_inc(sem("a_ln"), 1)
            act.wait_ge(sem("vpad_zero"), 1)
            for t in range(A_TILES):
                for s in range(2):
                    for c in range(CHUNKS):
                        act.wait_ge(sem("a_pro_done"), n + 1)
                        if s == 0:
                            nc.scalar.copy(vpad[:, t, 2 * c:2 * c + 2, A_TAPS - 1:PADDED],
                                           ps[:, n % 8, :].rearrange("p (b l) -> p b l", l=SEQ)).then_inc(sem("a_pro_read"), 1)
                        else:
                            nc.scalar.activation(gateT[:, t, cols(c)], ps[:, n % 8, :], ACT.Silu).then_inc(sem("a_pro_read"), 1)
                        n += 1
            for t in range(A_TILES):
                act.wait_ge(sem("a_conv"), t + 1)
                nc.scalar.activation(valT[:, t, :].rearrange("p (b l) -> p b l", l=SEQ), vacc[:], ACT.Silu,
                                     bias=a_conv_b[:, t:t + 1]).then_inc(sem("a_val"), 1)
            act.wait_ge(sem("a_cumT"), 1)
            nc.scalar.mul(ncum_a[:], ps[:, 2, 0:BLOCKS * 32].rearrange("p (i h) -> p i h", h=32), -1.0).then_inc(sem("a_ncum"), 1)
            act.wait_ge(sem("a_ncum"), 1)
            act.wait_ge(sem("valz_zero"), 3)
            for q in range(4):
                a_project_act(act, 0, 0, q)
            with act.Fori(0, A_TILES - 1) as g:
                a_group_act(act, g, False)
            a_group_act(act, A_TILES - 1, True)

        def a_project_act(act, h, parity, q):
            s, c = q // 2, q % 2
            act.wait_ge(sem("a_p_done"), 4 * h + q + 1)
            nc.scalar.copy((bmat, cmat)[s][parity][0][:, cols(c)], ps[:, c, :]).then_inc(sem("bc_hi"), 1)

        def a_group_act(act, g, last):
            for c in range(2):
                act.wait_ge(sem("val_T"), 2 * g + c + 1)
                nc.scalar.copy(valz_diagonal(valz[0], c), val_blocks(c)).then_inc(sem("valz_hi"), 1)
            for u in range(UNITS):
                j, b = u // BATCH, u % BATCH
                h = g * A_GROUP + j
                d = ps[:, 2 + u % 2, :]
                act.wait_ge(sem("a_s_done"), UNITS * g + u + 1)
                act.wait_ge(sem("a_ncum"), 1)
                nc.scalar.activation(first_m(e_a[:, u % 2]), first_m(d), ACT.Exp, bias=ncum_a[:, 2 * b, bass.ds(h, 1)])
                nc.scalar.activation(e_a[:, u % 2, P:2 * P], d[:, P:2 * P], ACT.Exp,
                                     bias=ncum_a[:, 2 * b + 1, bass.ds(h, 1)]).then_inc(sem("a_e_done"), 1)
                if not (last and u >= UNITS - BATCH):
                    a_project_act(act, h + 1, (j + 1) % 2, b)
                act.wait_ge(sem("a_m_done"), UNITS * g + u + 1)
                split_hi(at(ms_a, slice(None), u % 3), m_a[:, u % 2, :], "a_m_hi")
                if b == 1 and not (last and j >= A_GROUP - 2):
                    act.wait_ge(sem(f"aw_loaded{j % 2}"), 8 * h + 32 - 8 * (j % 2))
                    split_hi(at(aw, slice(None), j % 2), aw_raw[:, j % 2], "aw_hi")
                if u == OUT_UNIT + 8:
                    act.wait_ge(sem("awo_loaded"), 16 * g + 32)
                    split_hi(at(awo, slice(None)), awo_raw[:], "awo_hi")
            for c in range(CHUNKS):
                act.wait_ge(sem("y_gated"), 2 * g + c + 1)
                split_hi(at(ys, slice(None), cols(c)), yT[:, cols(c)], "ys_hi")

        def val_blocks(c):
            return ps[:, c, :].rearrange("p (i j d) -> p i j d", j=A_GROUP, d=A_HD)

        def valz_diagonal(z, c):
            flat = z[:].rearrange("p j i m -> p (j i m)")
            step = BLOCKS * P + A_HD
            ap = flat[:, 4 * c * P:4 * c * P + A_HD]
            return bass.AP(ap.tensor, ap.offset, [list(ap.ap[0]), [P, 4], [step, A_GROUP], [1, A_HD]])

        def a_dve(dve):
            step = counter(dve, "a_dve_step")
            dve.wait_ge(sem("a_params"), 16)
            dve.wait_ge(sem("a_pro_read"), CHUNKS)
            nc.vector.scalar_tensor_tensor(dec_e[:], dec_z[:], -1.0, dec_z[:], ALU.mult, ALU.max).then_inc(sem("a_abs"), 1)
            nc.vector.memset(vpad[:, :, :, 0:A_TAPS - 1], 0.0).then_inc(sem("vpad_zero"), 1)
            dve.wait_ge(sem("a_ln"), 2)
            step(nc.vector.scalar_tensor_tensor(dec_e[:], dec_z[:], 0.0, dec_e[:], ALU.max, ALU.add))
            step(nc.vector.tensor_scalar(dec_z[:], dec_e[:], neg_a[:], -1.0, ALU.mult, ALU.mult))
            step(nc.vector.memset(yT[:], 1.0))
            step(nc.vector.memset(yT[:, 0:TOKENS:SEQ], 0.0))
            nc.vector.tensor_tensor_scan(dec_e[:], yT[:], dec_z[:], 0.0, ALU.mult, ALU.add).then_inc(sem("a_cum"), 1)
            dve.wait_ge(sem("a_cum"), 1)
            split_pieces(dve, step, pieces_a, dec_e, dec_z, stage, "a_pieces")
            for t in range(A_TILES):
                dve.wait_ge(sem("a_pro_read"), CHUNKS + 4 * t + 2)
                if t:
                    dve.wait_ge(sem("a_val"), t)
                step(nc.vector.tensor_scalar(vacc[:], vpad[:, t, :, 0:SEQ], a_conv_w[:, t, 0:1], None, ALU.mult))
                for j in range(1, A_TAPS):
                    ins = nc.vector.scalar_tensor_tensor(vacc[:], vpad[:, t, :, j:j + SEQ], a_conv_w[:, t, j:j + 1],
                                                         vacc[:], ALU.mult, ALU.add)
                    if j < A_TAPS - 1:
                        step(ins)
                ins.then_inc(sem("a_conv"), 1)
            nc.vector.memset(f32(ys[0][:]), 0.0).then_inc(sem("ys_split"), 1)
            nc.vector.memset(f32(ys[1][:]), 0.0).then_inc(sem("ys_split"), 1)
            nc.vector.memset(yT[:, 0:1], 0.0).then_inc(sem("y_read"), 2)
            dve.wait_ge(sem("a_val"), A_TILES)
            nc.vector.memset(f32(valz[1][:, 0:A_GROUP // 2]), 0.0).then_inc(sem("valz_zero"), 1)
            nc.vector.tensor_copy(stage[:], valT[:, 0, :]).then_inc(sem("stage_ready"), 1)
            for q in range(4):
                a_project_dve(dve, 0, 0, q)
            dve.wait_ge(sem("valz_zero"), 3)
            with dve.Fori(0, A_TILES - 1) as g:
                a_group_dve(dve, g, False)
            a_group_dve(dve, A_TILES - 1, True)
            for n in range(4):
                a_out_dve(dve, A_TILES, n, n % 2)

        def split_pieces(dve, step, dst, v, t, hold, done):
            hb = hold[:].bitcast(BF16)
            p1, p2 = hb[:, 0:TOKENS], hb[:, TOKENS:2 * TOKENS]

            def place(rows, src):
                src = src[rows].rearrange("p (b l) -> p b l", l=SEQ)
                nc.vector.tensor_copy(dst[rows, :, 0:SEQ], src).then_inc(sem(done), 1)
                nc.vector.tensor_copy(dst[rows, :, SEQ:TRI], src[:, :, P:SEQ]).then_inc(sem(done), 1)
            step(nc.vector.memset(dst[:], 0.0))
            step(nc.vector.tensor_copy(p1, v[:]))
            place(slice(0, 32), p1)
            step(nc.vector.tensor_tensor(t[:], v[:], p1, ALU.subtract))
            step(nc.vector.tensor_copy(p2, t[:]))
            place(slice(32, 64), p2)
            step(nc.vector.tensor_tensor(t[:], t[:], p2, ALU.subtract))
            place(slice(64, 96), t[:])

        def a_project_dve(dve, h, parity, q):
            s, c = q // 2, q % 2
            m = (bmat, cmat)[s][parity]
            dve.wait_ge(sem("bc_hi"), 4 * h + q + 1)
            nc.vector.tensor_tensor(m[1][:, cols(c)], ps[:, c, :], f32(m[0][:, cols(c)]),
                                    ALU.subtract).then_inc(sem("bc_split"), 1)

        def a_out_dve(dve, g, n, bank):
            c, m = n // KT, n % KT
            dve.wait_ge(sem("a_wo_done"), 4 * g + n + 1)
            nc.vector.tensor_tensor(x[:, m, cols(c)], x[:, m, cols(c)], ps[:, bank, :], ALU.add).then_inc(sem("x_updated1"), 1)

        def a_group_dve(dve, g, last):
            for c in range(2):
                dve.wait_ge(sem("valz_hi"), 2 * g + c + 1)
                nc.vector.tensor_tensor(valz_diagonal(valz[1], c), val_blocks(c), f32(valz_diagonal(valz[0], c)),
                                        ALU.subtract).then_inc(sem("valz_split"), 1)
            for u in range(UNITS):
                j, b = u // BATCH, u % BATCH
                dve.wait_ge(sem("a_e_done"), UNITS * g + u + 1)
                if u >= 2:
                    dve.wait_ge(sem("a_m_split"), UNITS * g + u - 1)
                nc.vector.tensor_tensor(m_a[:, u % 2, :], ps[:, 4 + u % 2, 0:TRI], e_a[:, u % 2, :],
                                        ALU.mult).then_inc(sem("a_m_done"), 1)
                if not (last and u >= UNITS - BATCH):
                    a_project_dve(dve, g * A_GROUP + j + 1, (j + 1) % 2, b)
                if 0 <= u - OUT_UNIT < 4:
                    a_out_dve(dve, g, u - OUT_UNIT, (u + 1) % 2)
                if u == OUT_UNIT - 2 and not last:
                    nc.vector.tensor_copy(stage[:], group_tile(valT, g + 1, 0, TOKENS)).then_inc(sem("stage_ready"), 1)
            for c in range(CHUNKS):
                dve.wait_ge(sem("a_y_done"), UNITS * g + UNITS)
                nc.vector.scalar_tensor_tensor(yT[:, cols(c)], group_tile(valT, g, c * CHUNK, CHUNK), a_d[:, bass.ds(g, 1)],
                                               ps[:, 6 + c, :], ALU.mult, ALU.add).then_inc(sem("y_read"), 1)
            for c in range(CHUNKS):
                dve.wait_ge(sem("y_read"), 2 * g + 2 + c + 1)
                nc.vector.tensor_tensor(yT[:, cols(c)], yT[:, cols(c)], group_tile(gateT, g, c * CHUNK, CHUNK),
                                        ALU.mult).then_inc(sem("y_gated"), 1)
            for c in range(CHUNKS):
                dve.wait_ge(sem("ys_hi"), 2 * g + c + 1)
                nc.vector.tensor_tensor(ys[1][:, cols(c)], yT[:, cols(c)], f32(ys[0][:, cols(c)]),
                                        ALU.subtract).then_inc(sem("ys_split"), 1)

        def group_tile(t, g, first, n):
            return t[:].rearrange("p t n -> p (t n)")[:, bass.ds(g * TOKENS + first, n)]

        def a_pool(pool):
            split_lo(pool, at(a_dt_w, slice(None)), a_dt_raw[:], "a_pro_hi", 1, "a_pro_w")
            split_lo(pool, at(a_vg_w, slice(None)), a_vg_raw[:], "a_pro_hi", 2, "a_pro_w")
            for h in range(2):
                split_lo(pool, at(aw, slice(None), h), aw_raw[:, h], "aw_hi", h + 1, "aw_split")
            split_lo(pool, at(awo, slice(None)), awo_raw[:], "awo_hi", 1, "awo_split")
            normed(pool, 0)
            nc.gpsimd.memset(f32(valz[0][:]), 0.0).then_inc(sem("valz_zero"), 1)
            pool.wait_ge(sem("a_val"), A_TILES)
            pool.wait_ge(sem("a_cumT"), 1)
            pool.wait_ge(sem("a_pieces"), 6)
            nc.gpsimd.memset(f32(valz[1][:, A_GROUP // 2:]), 0.0).then_inc(sem("valz_zero"), 1)
            with pool.Fori(0, A_TILES - 1) as g:
                a_group_pool(pool, g, False)
            a_group_pool(pool, A_TILES - 1, True)

        def a_group_pool(pool, g, last):
            for u in range(UNITS):
                j, b = u // BATCH, u % BATCH
                split_lo(pool, at(ms_a, slice(None), u % 3), m_a[:, u % 2, :], "a_m_hi", UNITS * g + u + 1, "a_m_split")
                if b == 1 and not (last and j >= A_GROUP - 2):
                    split_lo(pool, at(aw, slice(None), j % 2), aw_raw[:, j % 2], "aw_hi", g * A_GROUP + j + 3, "aw_split")
                if u == OUT_UNIT + 8:
                    split_lo(pool, at(awo, slice(None)), awo_raw[:], "awo_hi", g + 2, "awo_split")

        def a_sp(sp):
            sp.dma_start(apar[:], a_par).then_inc(sem("a_params"), 16)
            for h in range(2):
                sp.dma_start(aw_raw[:, h], a_heads[h * P:(h + 1) * P, :]).then_inc(sem(f"aw_loaded{h}"), 16)
            sp.dma_start(awo_raw[:], a_wo[0:P, :]).then_inc(sem("awo_loaded"), 16)
            sp.dma_start(a_dt_raw[:], a_dt).then_inc(sem("a_pro_loaded"), 16)
            sp.dma_start(a_vg_raw[:], a_vg).then_inc(sem("a_pro_loaded"), 16)
            with sp.Fori(0, A_TILES - 1) as g:
                a_group_sp(sp, g, False)
            a_group_sp(sp, A_TILES - 1, True)

        def a_group_sp(sp, g, last):
            for j in range(A_GROUP):
                if j == 0:
                    sp.wait_ge(sem("awo_split"), g + 1)
                    sp.dma_start(awo_raw[:], a_wo[bass.ds(g * P + P, P), :]).then_inc(sem("awo_loaded"), 16)
                if not (last and j >= A_GROUP - 2):
                    h2 = g * A_GROUP + j + 2
                    sp.wait_ge(sem("aw_split"), h2 - 1)
                    sp.dma_start(aw_raw[:, j % 2], a_heads[bass.ds(h2 * P, P), :]).then_inc(sem(f"aw_loaded{j % 2}"), 16)

        def f_pe(pe, n, f):
            normed(pe, n)
            pe.wait_ge(sem(f"{f}_rw"), 1)
            for i in range(BLOCKS):
                for k in range(KT):
                    ins = mm3(ps[:, 0, i * LOGITS:(i + 1) * LOGITS], at(xn, slice(None), k, slice(i * P, (i + 1) * P)),
                              at(rw, slice(None), k), i == 0 and k == 0, i == BLOCKS - 1 and k == KT - 1)
            ins.then_inc(sem(f"{f}_logits"), 1)
            pe.wait_ge(sem(f"{f}_coef"), 1)
            for i in range(BLOCKS):
                nc.tensor.transpose(ps[:, i // 4, (i % 4) * P:(i % 4 + 1) * P],
                                    cexp[:, i].rearrange("p e r -> p (e r)"), ident)
                ins = nc.tensor.transpose(ps[:, 2 + i // 4, (i % 4) * P:(i % 4 + 1) * P], sexp[:, i], ident)
            ins.then_inc(sem(f"{f}_coefT"), 1)
            pe.wait_ge(sem(f"{f}_coef_ready"), 2)
            for a in range(4):
                ins = nc.tensor.matmul(ps[:, 4 + a, :], zero_w[:], zero_x[:], start=True, stop=False, skip_group_check=True)
            ins.then_inc(sem(f"{f}_down_done"), 1)
            f_up_pe(pe, f, 0, 0)
            with pe.Fori(0, F_TILES // 2 - 1) as i2:
                for p in range(2):
                    f_up_pe(pe, f, 2 * i2 + p + 1, 1 - p)
                    f_down_pe(pe, f, 2 * i2 + p, p)
            f_up_pe(pe, f, F_TILES - 1, 1)
            f_down_pe(pe, f, F_TILES - 2, 0)
            f_down_pe(pe, f, F_TILES - 1, 1)

        def f_up_pe(pe, f, i, p):
            pe.wait_ge(sem(f"{f}_gu_split"), i + 1)
            for c in range(CHUNKS):
                if not (isinstance(i, int) and i == 0):
                    pe.wait_ge(sem(f"{f}_h"), 2 * i + c - 1)
                for s in range(2):
                    for k in range(KT):
                        ins = mm3(ps[:, 2 * s + c, :], at(fgu, slice(None), p, k, s), at(xn, slice(None), k, cols(c)),
                                  k == 0, k == KT - 1)
                ins.then_inc(sem(f"{f}_up_done"), 1)

        def f_down_pe(pe, f, i, p):
            pe.wait_ge(sem(f"{f}_d_split"), i + 1)
            for c in range(CHUNKS):
                pe.wait_ge(sem(f"{f}_h_split"), 2 * i + c + 1)
                for m in range(KT):
                    ins = mm3(ps[:, 4 + 2 * c + m, :], at(fd, slice(None), p, slice(m * P, (m + 1) * P)),
                              at(fh, slice(None), p, cols(c)), False, False)
            ins.then_inc(sem(f"{f}_down_done"), 1)

        def f_act(act, n, f):
            act.wait_ge(sem(f"{f}_rw_loaded"), 16)
            split_hi(at(rw, slice(None)), rw_raw[:], f"{f}_rw_hi")
            for p in range(2):
                act.wait_ge(sem(f"{f}_w_loaded{p}"), 16)
                split_hi(at(fgu, slice(None), p), raw_gu(p), f"{f}_gu_hi")
            split_hi(at(fd, slice(None), 0), raw_d(0), f"{f}_d_hi")
            act.wait_ge(sem(f"{f}_shift"), 1)
            nc.scalar.activation(pr[:], pr[:], ACT.Exp).then_inc(sem(f"{f}_exp"), 1)
            nc.scalar.activation(r_gate[:], lg[:, :, EXPERTS], ACT.Sigmoid).then_inc(sem(f"{f}_gate"), 1)
            act.wait_ge(sem(f"{f}_coefT"), 1)
            nc.scalar.copy(coef_r[:].rearrange("p (a n) -> p a n", a=2), ps[:, 0:2, :]).then_inc(sem(f"{f}_coef_ready"), 1)
            nc.scalar.copy(coef_s[:].rearrange("p (a n) -> p a n", a=2), ps[:, 2:4, :]).then_inc(sem(f"{f}_coef_ready"), 1)
            with act.Fori(0, F_TILES // 2 - 1) as i2:
                for p in range(2):
                    f_hidden_act(act, f, 2 * i2 + p, p, True, True)
            f_hidden_act(act, f, F_TILES - 2, 0, False, True)
            f_hidden_act(act, f, F_TILES - 1, 1, False, False)

        def f_hidden_act(act, f, i, p, more_gu, more_d):
            for c in range(CHUNKS):
                act.wait_ge(sem(f"{f}_up_done"), 2 * i + c + 1)
                nc.scalar.activation(f_s[:, c], ps[:, c, :], ACT.Silu).then_inc(sem(f"{f}_silu"), 1)
            for c in range(CHUNKS):
                act.wait_ge(sem(f"{f}_h"), 2 * i + c + 1)
                split_hi(at(fh, slice(None), p, cols(c)), f_h[:, c], f"{f}_h_hi")
            if more_d:
                act.wait_ge(sem(f"{f}_down_done"), i + 1)
                split_hi(at(fd, slice(None), 1 - p), raw_d(1 - p), f"{f}_d_hi")
            if more_gu:
                act.wait_ge(sem(f"{f}_w_loaded{p}"), 8 * i + 32 - 8 * p)
                split_hi(at(fgu, slice(None), p), raw_gu(p), f"{f}_gu_hi")

        def raw_gu(p):
            return fw_raw[:, p, 0:KT * 2 * P].rearrange("p (k s m) -> p k s m", k=KT, s=2)

        def raw_d(p):
            return fw_raw[:, p, KT * 2 * P:]

        def f_pool(pool, n, f):
            split_lo(pool, at(rw, slice(None)), rw_raw[:], f"{f}_rw_hi", 1, f"{f}_rw")
            for p in range(2):
                f_split_gu_pool(pool, f, p, p)
            f_split_d_pool(pool, f, 0, 0)
            pool.wait_ge(sem(f"{f}_coef_ready"), 2)
            with pool.Fori(0, S_TILES // 2) as i2:
                for p in range(2):
                    f_hidden_pool(pool, f, 2 * i2 + p, p, coef_s, True, True)
            with pool.Fori(S_TILES // 2, F_TILES // 2 - 1) as i2:
                for p in range(2):
                    f_hidden_pool(pool, f, 2 * i2 + p, p, coef_r, True, True)
            f_hidden_pool(pool, f, F_TILES - 2, 0, coef_r, False, True)
            f_hidden_pool(pool, f, F_TILES - 1, 1, coef_r, False, False)

        def f_split_gu_pool(pool, f, i, p):
            split_lo(pool, at(fgu, slice(None), p), raw_gu(p), f"{f}_gu_hi", i + 1, f"{f}_gu_split")

        def f_split_d_pool(pool, f, i, p):
            split_lo(pool, at(fd, slice(None), p), raw_d(p), f"{f}_d_hi", i + 1, f"{f}_d_split")

        def f_hidden_pool(pool, f, i, p, coef, more_gu, more_d):
            for c in range(CHUNKS):
                pool.wait_ge(sem(f"{f}_silu"), 2 * i + c + 1)
                nc.gpsimd.tensor_tensor(f_sc[:, c], f_s[:, c], coef[:, cols(c)], ALU.mult).then_inc(sem(f"{f}_sc"), 1)
            if more_d:
                f_split_d_pool(pool, f, i + 1, 1 - p)
            if more_gu:
                f_split_gu_pool(pool, f, i + 2, p)

        def f_dve(dve, n, f):
            step = counter(dve, f"{f}_dve_step")
            dve.wait_ge(sem(f"{f}_logits"), 1)
            step(nc.vector.tensor_copy(lg[:], ps[:, 0, 0:BLOCKS * LOGITS].rearrange("p (i e) -> p i e", e=LOGITS)))
            step(nc.vector.tensor_reduce(r_mx[:], lg[:, :, 0:EXPERTS], AX_X, ALU.max))
            wide = [P, BLOCKS, EXPERTS]
            nc.vector.tensor_tensor(pr[:], lg[:, :, 0:EXPERTS], r_mx[:, :, None].broadcast_to(wide),
                                    ALU.subtract).then_inc(sem(f"{f}_shift"), 1)
            dve.wait_ge(sem(f"{f}_exp"), 1)
            step(nc.vector.tensor_reduce(r_sum[:], pr[:], AX_X, ALU.add))
            step(nc.vector.reciprocal(r_sum[:], r_sum[:]))
            step(nc.vector.tensor_tensor(pr[:], pr[:], r_sum[:, :, None].broadcast_to(wide), ALU.mult))
            for i in range(BLOCKS):
                pj = pr[:, i, None, :].broadcast_to([P, EXPERTS, EXPERTS])
                pe_ = pr[:, i, :, None].broadcast_to([P, EXPERTS, EXPERTS])
                nc.vector.tensor_tensor(r_gt[:, i], pj, pe_, ALU.is_gt)
                ins = nc.vector.tensor_tensor(r_eq[:, i], pj, pe_, ALU.is_equal)
            step(ins)
            step(nc.vector.tensor_tensor(r_eq[:], r_eq[:], tri[:, None].broadcast_to([P, BLOCKS, EXPERTS, EXPERTS]), ALU.mult))
            step(nc.vector.tensor_tensor(r_gt[:], r_gt[:], r_eq[:], ALU.add))
            step(nc.vector.tensor_reduce(r_rank[:], r_gt[:], AX_X, ALU.add))
            step(nc.vector.scalar_tensor_tensor(pr[:], r_rank[:], TOP_K - 0.5, pr[:], ALU.is_lt, ALU.mult))
            step(nc.vector.tensor_copy(cexp[:], pr[:, :, :, None].broadcast_to([P, BLOCKS, EXPERTS, ROWS_E])))
            dve.wait_ge(sem(f"{f}_gate"), 1)
            nc.vector.tensor_copy(sexp[:], r_gate[:, :, None].broadcast_to([P, BLOCKS, P])).then_inc(sem(f"{f}_coef"), 1)
            with dve.Fori(0, F_TILES // 2) as i2:
                for p in range(2):
                    for c in range(CHUNKS):
                        u = 4 * i2 + 2 * p + c
                        dve.wait_ge(sem(f"{f}_sc"), u + 1)
                        nc.vector.tensor_tensor(f_h[:, c], f_sc[:, c], ps[:, 2 + c, :], ALU.mult).then_inc(sem(f"{f}_h"), 1)
                        dve.wait_ge(sem(f"{f}_h_hi"), u + 1)
                        nc.vector.tensor_tensor(fh[1][:, p, cols(c)], f_h[:, c], f32(fh[0][:, p, cols(c)]),
                                                ALU.subtract).then_inc(sem(f"{f}_h_split"), 1)
            dve.wait_ge(sem(f"{f}_down_done"), F_TILES + 1)
            for c in range(CHUNKS):
                for m in range(KT):
                    nc.vector.tensor_tensor(x[:, m, cols(c)], x[:, m, cols(c)], ps[:, 4 + 2 * c + m, :],
                                            ALU.add).then_inc(sem(f"x_updated{n + 1}"), 1)

        def f_sp(sp, n, f):
            x_final(sp, n, CHUNKS - 1)
            sp.dma_start(rw_raw[:], router_w).then_inc(sem(f"{f}_rw_loaded"), 16)
            for p in range(2):
                sp.dma_start(fw_raw[:, p], ffn_w[p * P:(p + 1) * P, :]).then_inc(sem(f"{f}_w_loaded{p}"), 16)
            with sp.Fori(0, F_TILES // 2 - 1) as i2:
                for p in range(2):
                    sp.wait_ge(sem(f"{f}_d_split"), 2 * i2 + p + 1)
                    sp.dma_start(fw_raw[:, p], ffn_w[bass.ds(i2 * (2 * P) + (2 + p) * P, P), :]).then_inc(sem(f"{f}_w_loaded{p}"), 16)

        def b_pe(pe):
            normed(pe, 2)
            pe.wait_ge(sem("b_bg_w"), 1)
            for s in range(2):
                for c in range(CHUNKS):
                    for k in range(KT):
                        ins = mm3(ps[:, 2 * s + c, :], at(wbg, slice(None), k, s), at(xn, slice(None), k, cols(c)),
                                  k == 0, k == KT - 1)
            ins.then_inc(sem("b_bg_done"), 1)
            pe.wait_ge(sem("b_bg_read"), 2)
            b_make_pe(pe, 0, 0, range(4))
            pe.wait_ge(sem("b_cum"), 1)
            for i in range(BLOCKS):
                ins = nc.tensor.transpose(ps[:, 2, i * 32:(i + 1) * 32], dec_b[2][0:32, i * P:(i + 1) * P], ident[0:32, 0:32])
            ins.then_inc(sem("b_cumT"), 1)
            pe.wait_ge(sem("b_ncum"), 1)
            pe.wait_ge(sem("b_pieces"), 6)
            with pe.Fori(0, B_HEADS // 2 - 1) as h2:
                b_head_pe(pe, 2 * h2, 0, False)
                b_head_pe(pe, 2 * h2 + 1, 1, False)
            b_head_pe(pe, B_HEADS - 2, 0, False)
            b_head_pe(pe, B_HEADS - 1, 1, True)

        def b_bank(pe, h, slot):
            before = slot - 2
            if before < 0:
                if not (isinstance(h, int) and h == 0):
                    pe.wait_ge(sem("b_silu"), 4 * h)
                    pe.wait_ge(sem("x_updated3"), 4 * h - 1 + slot)
            elif before < 4:
                pe.wait_ge(sem("qpad_split"), 4 * h + before + 1)
            elif before < 8:
                pe.wait_ge(sem("v_split"), 4 * h + before - 3)
            else:
                pe.wait_ge(sem("b_silu"), 4 * h + before - 7)
            return ps[:, slot % 2, :]

        def b_make_pe(pe, h, p, parts):
            for part in parts:
                if part == 0:
                    pe.wait_ge(sem("wqk_split"), h + 1)
                    for s in range(2):
                        for c in range(CHUNKS):
                            o = b_bank(pe, h, 2 * s + c)
                            for k in range(KT):
                                ins = mm3(o, at(wqk, slice(None), k, s), at(xn, slice(None), k, cols(c)), k == 0, k == KT - 1)
                            ins.then_inc(sem("b_proj_done"), 1)
                elif part == 1:
                    pe.wait_ge(sem("wv_split"), h + 1)
                    for i in range(BLOCKS // 2):
                        o = b_bank(pe, h, 4 + i)
                        for t in range(2):
                            tok = slice((2 * i + t) * P, (2 * i + t + 1) * P)
                            for k in range(KT):
                                ins = mm3(o[:, t * B_V:(t + 1) * B_V], at(xn, slice(None), k, tok), at(wv, slice(None), k),
                                          t == 0 and k == 0, t == 1 and k == KT - 1)
                        ins.then_inc(sem("b_v_done"), 1)
                else:
                    s = part - 2
                    if s == 0:
                        pe.wait_ge(sem("wconv_split"), h + 1)
                    pe.wait_ge(sem("qpad_split"), 4 * h + 2 * s + 2)
                    for c in range(CHUNKS):
                        o = b_bank(pe, h, 8 + 2 * s + c).rearrange("p (b l) -> p b l", l=SEQ)
                        for j in range(B_TAPS):
                            ins = mm3(o, at(wconv, slice(None), s, j),
                                      at(qpad, slice(None), s, slice(2 * c, 2 * c + 2), slice(j, j + SEQ)),
                                      j == 0, j == B_TAPS - 1)
                        ins.then_inc(sem("b_conv_done"), 1)

        def b_score_pe(pe, h, p, b):
            l0, u = b * SEQ, b % 2
            if b >= 2:
                pe.wait_ge(sem("b_m_done"), BATCH * h + b - 1)
            d, s = ps[:, 2 + u, :], ps[:, 4 + u, :]
            if b % 2 == 0:
                pe.wait_ge(sem("qk_split"), 4 * h + 3 + b // 2)
            lhs = rows_b[:, bass.ds(h, 1)].broadcast_to([P, P])
            nc.tensor.matmul(d[:, 0:TRI], lhs, pieces_b[:, b, :], start=True, stop=False, skip_group_check=True)
            nc.tensor.matmul(d[:, 0:2 * P], ident_b[:], mask_b[:].rearrange("p d n -> p (d n)"), start=False, stop=True, skip_group_check=True)
            mm3(first_m(s), at(qk[p], slice(None), 1, slice(l0, l0 + P)), halves(at(qk[p], slice(None), 0, slice(l0, l0 + SEQ))), True, False)
            mm3(s[:, P:2 * P], at(qk[p], slice(None), 1, slice(l0 + P, l0 + SEQ)),
                at(qk[p], slice(None), 0, slice(l0 + P, l0 + SEQ)), False).then_inc(sem("b_s_done"), 1)

        def b_value_pe(pe, h, p, b):
            u = b % 2
            pe.wait_ge(sem("b_m_split"), BATCH * h + b + 1)
            if b == 0:
                pe.wait_ge(sem("v_split"), 4 * h + 4)
            if b >= 2:
                pe.wait_ge(sem("o_split"), BATCH * h + b - 1)
            o, ms = ps[:, 6 + u, :], at(ms_b, slice(None), u)
            for d in range(B_VT):
                dv = slice(d * P, (d + 1) * P)
                mm3(half_view(o[:, d * SEQ:(d + 1) * SEQ]), at(vtok[p], slice(None), 2 * b, dv), tuple(first_m(v) for v in ms),
                    d == 0, False)
                ins = mm3(o[:, d * SEQ + P:(d + 1) * SEQ], at(vtok[p], slice(None), 2 * b + 1, dv),
                          at(ms, slice(None), slice(P, 2 * P)), False, d == B_VT - 1)
            ins.then_inc(sem("b_o_done"), 1)

        def b_head_pe(pe, h, p, last):
            make = (lambda parts: None) if last else (lambda parts: b_make_pe(pe, h + 1, 1 - p, parts))
            b_score_pe(pe, h, p, 0)
            make([0])
            b_score_pe(pe, h, p, 1)
            make([1])
            b_value_pe(pe, h, p, 0)
            b_score_pe(pe, h, p, 2)
            b_score_pe(pe, h, p, 3)
            b_value_pe(pe, h, p, 1)
            make([2, 3])
            b_value_pe(pe, h, p, 2)
            b_value_pe(pe, h, p, 3)
            pe.wait_ge(sem("wo_split"), h + 1)
            for c in range(CHUNKS):
                pe.wait_ge(sem("o_split"), BATCH * h + 2 * c + 2)
                for m in range(KT):
                    if c == 0 and not last:
                        pe.wait_ge(sem("b_silu"), 4 * h + 7 + m)
                    else:
                        pe.wait_ge(sem("x_updated3"), 4 * h + 2 * c + m + 3)
                    o = ps[:, m, :]
                    for d in range(B_VT):
                        ins = mm3(o, at(wo, slice(None), d, slice(m * P, (m + 1) * P)), at(oT, slice(None), d, cols(c)),
                                  d == 0, d == B_VT - 1)
                    ins.then_inc(sem("b_wo_done"), 1)

        def b_act(act):
            act.wait_ge(sem("b_params"), 16)
            act.wait_ge(sem("wbg_loaded"), 16)
            split_hi(at(wbg, slice(None)), wbg_raw[:], "wbg_hi")
            for name, w, raw in B_WEIGHTS:
                b_weights_act(act, name, w, raw, 0)
            act.wait_ge(sem("b_bg_done"), 1)
            for s in range(2):
                nc.scalar.activation(dec_b[s][:].rearrange("p (a n) -> p a n", a=2), ps[:, 2 * s:2 * s + 2, :], ACT.Identity,
                                     bias=bpar[:, s:s + 1]).then_inc(sem("b_bg_read"), 1)
            for s in range(2):
                act.wait_ge(sem("b_abs"), s + 1)
                nc.scalar.activation(dec_b[2 + s][:], dec_b[2 + s][:], ACT.Exp, scale=-1.0).then_inc(sem("b_exp"), 1)
            for s in range(2):
                act.wait_ge(sem("b_exp"), s + 1)
                nc.scalar.activation(dec_b[2 + s][:], dec_b[2 + s][:], ACT.Ln, bias=1.0).then_inc(sem("b_ln"), 1)
            act.wait_ge(sem("qpad_zero"), 2)
            b_make_act(act, 0, 0, range(3))
            for name, w, raw in B_WEIGHTS[0:2]:
                b_weights_act(act, name, w, raw, 1)
            b_make_act(act, 0, 0, [3])
            b_weights_act(act, *B_WEIGHTS[2], 1)
            act.wait_ge(sem("b_cumT"), 1)
            nc.scalar.mul(ncum_b[:], ps[:, 2, 0:BLOCKS * 32].rearrange("p (i h) -> p i h", h=32), -1.0).then_inc(sem("b_ncum"), 1)
            act.wait_ge(sem("b_ncum"), 1)
            with act.Fori(0, B_HEADS // 2 - 1) as h2:
                b_head_act(act, 2 * h2, 0, False, True)
                b_head_act(act, 2 * h2 + 1, 1, False, True)
            b_head_act(act, B_HEADS - 2, 0, False, False)
            b_head_act(act, B_HEADS - 1, 1, True, False)

        def b_make_act(act, h, p, parts):
            for part in parts:
                if part == 0:
                    for s in range(2):
                        for c in range(CHUNKS):
                            act.wait_ge(sem("b_proj_done"), 4 * h + 2 * s + c + 1)
                            nc.scalar.copy(qpad[0][:, s, 2 * c:2 * c + 2, B_TAPS - 1:PADDED],
                                           ps[:, c, :].rearrange("p (b l) -> p b l", l=SEQ)).then_inc(sem("qpad_hi"), 1)
                elif part == 1:
                    for i in range(BLOCKS // 2):
                        act.wait_ge(sem("b_v_done"), 4 * h + i + 1)
                        nc.scalar.copy(vtok[p][0][:, 2 * i:2 * i + 2], ps[:, i % 2, :].rearrange("p (t v) -> p t v", t=2)
                                       ).then_inc(sem("v_hi"), 1)
                else:
                    s = part - 2
                    for c in range(CHUNKS):
                        act.wait_ge(sem("b_conv_done"), 4 * h + 2 * s + c + 1)
                        if not (isinstance(h, int) and h == 0 and s == 0):
                            act.wait_ge(sem("qk_split"), 4 * h + 2 * s + c - 1)
                        nc.scalar.activation(qf[:, c], ps[:, c, :], ACT.Silu, bias=conv_bias[:, s:s + 1]).then_inc(sem("b_silu"), 1)
                    for c in range(CHUNKS):
                        act.wait_ge(sem("b_silu"), 4 * h + 2 * s + c + 1)
                        split_hi(at(qk[p], slice(None), s, cols(c)), qf[:, c], "qk_hi")

        def b_weights_act(act, name, w, raw, h):
            act.wait_ge(sem(f"{name}_loaded"), 16 * h + 16)
            if name == "wconv":
                nc.scalar.copy(conv_bias[:], wconv_raw_all[:, CONVW:])
            split_hi(at(w, slice(None)), raw[:], f"{name}_hi")

        def b_split_act(act, h, b):
            act.wait_ge(sem("b_m_done"), BATCH * h + b + 1)
            if b >= 2:
                act.wait_ge(sem("b_o_done"), BATCH * h + b - 1)
            split_hi(at(ms_b, slice(None), b % 2), m_b[:, b % 2, :], "b_m_hi")

        def b_score_act(act, h, b):
            act.wait_ge(sem("b_s_done"), BATCH * h + b + 1)
            act.wait_ge(sem("b_ncum"), 1)
            d = ps[:, 2 + b % 2, :]
            nc.scalar.activation(first_m(e_b[:, b % 2]), first_m(d), ACT.Exp, bias=ncum_b[:, 2 * b, bass.ds(h, 1)])
            nc.scalar.activation(e_b[:, b % 2, P:2 * P], d[:, P:2 * P], ACT.Exp,
                                 bias=ncum_b[:, 2 * b + 1, bass.ds(h, 1)]).then_inc(sem("b_e_done"), 1)

        def b_value_act(act, h, b):
            act.wait_ge(sem("b_o_done"), BATCH * h + b + 1)
            nc.scalar.copy(oT[0][:, :, b * SEQ:(b + 1) * SEQ], ps[:, 6 + b % 2, :].rearrange("p (d l) -> p d l", d=B_VT)
                           ).then_inc(sem("o_hi"), 1)

        def b_head_act(act, h, p, last, weights):
            make = (lambda parts: None) if last else (lambda parts: b_make_act(act, h + 1, 1 - p, parts))
            b_score_act(act, h, 0)
            make([0])
            b_split_act(act, h, 0)
            b_score_act(act, h, 1)
            b_split_act(act, h, 1)
            make([1])
            b_weights_act(act, "wo", wo, wo_raw, h)
            b_value_act(act, h, 0)
            b_score_act(act, h, 2)
            b_split_act(act, h, 2)
            b_score_act(act, h, 3)
            b_value_act(act, h, 1)
            b_split_act(act, h, 3)
            if weights:
                b_weights_act(act, *B_WEIGHTS[0], h + 2)
                b_weights_act(act, *B_WEIGHTS[1], h + 2)
            make([2, 3])
            if weights:
                b_weights_act(act, *B_WEIGHTS[2], h + 2)
            b_value_act(act, h, 2)
            b_value_act(act, h, 3)

        def b_dve(dve):
            step = counter(dve, "b_dve_step")
            dve.wait_ge(sem("b_bg_read"), 2)
            for s in range(2):
                nc.vector.scalar_tensor_tensor(dec_b[2 + s][:], dec_b[s][:], -1.0, dec_b[s][:], ALU.mult, ALU.max).then_inc(sem("b_abs"), 1)
            for s in range(2):
                nc.vector.memset(f32(qpad[s][:, :, :, 0:B_TAPS - 1]), 0.0).then_inc(sem("qpad_zero"), 1)
            for s in range(2):
                dve.wait_ge(sem("b_ln"), s + 1)
                step(nc.vector.scalar_tensor_tensor(dec_b[s][:], dec_b[s][:], 0.0, dec_b[2 + s][:], ALU.min, ALU.subtract))
            nc.vector.memset(dec_b[3][:], 1.0).then_inc(sem("x_updated3"), 4)
            dve.wait_ge(sem("x_updated3"), 4)
            step(nc.vector.memset(dec_b[3][:, 0:TOKENS:SEQ], 0.0))
            step(nc.vector.tensor_tensor_scan(dec_b[2][:], dec_b[3][:], dec_b[0][:], 0.0, ALU.mult, ALU.add))
            nc.vector.tensor_tensor(dec_b[1][:], dec_b[1][:], dec_b[2][:], ALU.add).then_inc(sem("b_cum"), 1)
            dve.wait_ge(sem("b_cum"), 1)
            split_pieces(dve, step, pieces_b, dec_b[1], dec_b[4], dec_b[5], "b_pieces")
            b_make_dve(dve, 0, 0, range(4))
            with dve.Fori(0, B_HEADS // 2 - 1) as h2:
                b_head_dve(dve, 2 * h2, 0, False)
                b_head_dve(dve, 2 * h2 + 1, 1, False)
            b_head_dve(dve, B_HEADS - 2, 0, False)
            b_head_dve(dve, B_HEADS - 1, 1, True)

        def b_make_dve(dve, h, p, parts):
            for part in parts:
                if part == 0:
                    for s in range(2):
                        for c in range(CHUNKS):
                            dve.wait_ge(sem("qpad_hi"), 4 * h + 2 * s + c + 1)
                            at_ = (slice(None), s, slice(2 * c, 2 * c + 2), slice(B_TAPS - 1, PADDED))
                            nc.vector.tensor_tensor(qpad[1][at_], ps[:, c, :].rearrange("p (b l) -> p b l", l=SEQ),
                                                    f32(qpad[0][at_]), ALU.subtract
                                                    ).then_inc(sem("qpad_split"), 1)
                elif part == 1:
                    for i in range(BLOCKS // 2):
                        dve.wait_ge(sem("v_hi"), 4 * h + i + 1)
                        at_ = (slice(None), slice(2 * i, 2 * i + 2))
                        nc.vector.tensor_tensor(vtok[p][1][at_], ps[:, i % 2, :].rearrange("p (t v) -> p t v", t=2),
                                                f32(vtok[p][0][at_]), ALU.subtract
                                                ).then_inc(sem("v_split"), 1)

        def b_score_dve(dve, h, b):
            dve.wait_ge(sem("b_e_done"), BATCH * h + b + 1)
            if b >= 2:
                dve.wait_ge(sem("b_m_split"), BATCH * h + b - 1)
            nc.vector.tensor_tensor(m_b[:, b % 2, :], ps[:, 4 + b % 2, 0:TRI], e_b[:, b % 2, :],
                                    ALU.mult).then_inc(sem("b_m_done"), 1)

        def b_value_dve(dve, h, b):
            dve.wait_ge(sem("o_hi"), BATCH * h + b + 1)
            at_ = (slice(None), slice(None), slice(b * SEQ, (b + 1) * SEQ))
            nc.vector.tensor_tensor(oT[1][at_], ps[:, 6 + b % 2, :].rearrange("p (d l) -> p d l", d=B_VT),
                                    f32(oT[0][at_]), ALU.subtract).then_inc(sem("o_split"), 1)

        def b_head_dve(dve, h, p, last):
            make = (lambda parts: None) if last else (lambda parts: b_make_dve(dve, h + 1, 1 - p, parts))
            b_score_dve(dve, h, 0)
            make([0])
            b_score_dve(dve, h, 1)
            make([1])
            b_value_dve(dve, h, 0)
            b_score_dve(dve, h, 2)
            b_score_dve(dve, h, 3)
            b_value_dve(dve, h, 1)
            b_value_dve(dve, h, 2)
            b_value_dve(dve, h, 3)
            for c in range(CHUNKS):
                for m in range(KT):
                    dve.wait_ge(sem("b_wo_done"), 4 * h + 2 * c + m + 1)
                    nc.vector.tensor_tensor(x[:, m, cols(c)], x[:, m, cols(c)], ps[:, m, :],
                                            ALU.add).then_inc(sem("x_updated3"), 1)

        def b_pool(pool):
            split_lo(pool, at(wbg, slice(None)), wbg_raw[:], "wbg_hi", 1, "b_bg_w")
            for name, w, raw in B_WEIGHTS:
                b_weights_pool(pool, name, w, raw, 0)
            b_conv_pool(pool, 0, 0, 0)
            for name, w, raw in B_WEIGHTS[0:2]:
                b_weights_pool(pool, name, w, raw, 1)
            b_conv_pool(pool, 0, 0, 1)
            b_weights_pool(pool, *B_WEIGHTS[2], 1)
            with pool.Fori(0, B_HEADS // 2 - 1) as h2:
                b_head_pool(pool, 2 * h2, 0, True, True)
                b_head_pool(pool, 2 * h2 + 1, 1, True, True)
            b_head_pool(pool, B_HEADS - 2, 0, True, False)
            b_head_pool(pool, B_HEADS - 1, 1, False, False)

        def b_weights_pool(pool, name, w, raw, h):
            split_lo(pool, at(w, slice(None)), raw[:], f"{name}_hi", h + 1, f"{name}_split")

        def b_conv_pool(pool, h, p, s):
            for c in range(CHUNKS):
                split_lo(pool, at(qk[p], slice(None), s, cols(c)), qf[:, c], "qk_hi", 4 * h + 2 * s + c + 1, "qk_split")

        def b_score_pool(pool, h, b):
            split_lo(pool, at(ms_b, slice(None), b % 2), m_b[:, b % 2, :], "b_m_hi", BATCH * h + b + 1, "b_m_split")

        def b_head_pool(pool, h, p, make, weights):
            b_score_pool(pool, h, 0)
            b_score_pool(pool, h, 1)
            b_weights_pool(pool, "wo", wo, wo_raw, h)
            b_score_pool(pool, h, 2)
            b_score_pool(pool, h, 3)
            if weights:
                b_weights_pool(pool, *B_WEIGHTS[0], h + 2)
                b_weights_pool(pool, *B_WEIGHTS[1], h + 2)
            if make:
                b_conv_pool(pool, h + 1, 1 - p, 0)
                b_conv_pool(pool, h + 1, 1 - p, 1)
            if weights:
                b_weights_pool(pool, *B_WEIGHTS[2], h + 2)

        B_WEIGHTS = (("wqk", wqk, wqk_raw), ("wv", wv, wv_raw), ("wconv", wconv, wconv_raw))
        B_PARTS = (("wqk", wqk_raw, b_qk), ("wv", wv_raw, b_v), ("wconv", wconv_raw_all, b_conv))

        def b_sp(sp):
            x_final(sp, 2, CHUNKS - 1)
            sp.dma_start(bpar[:], b_par).then_inc(sem("b_params"), 16)
            sp.dma_start(wbg_raw[:], b_bg).then_inc(sem("wbg_loaded"), 16)
            for name, raw, src in B_PARTS:
                sp.dma_start(raw[:], src[0:P, :]).then_inc(sem(f"{name}_loaded"), 16)
            sp.dma_start(wo_raw[:], b_wo[0:P, :]).then_inc(sem("wo_loaded"), 16)
            for name, raw, src in B_PARTS:
                sp.wait_ge(sem(f"{name}_split"), 1)
                sp.dma_start(raw[:], src[P:2 * P, :]).then_inc(sem(f"{name}_loaded"), 16)
            with sp.Fori(0, B_HEADS - 2) as h:
                sp.wait_ge(sem("wo_split"), h + 1)
                sp.dma_start(wo_raw[:], b_wo[bass.ds(h * P + P, P), :]).then_inc(sem("wo_loaded"), 16)
                for name, raw, src in B_PARTS:
                    sp.wait_ge(sem(f"{name}_split"), h + 2)
                    sp.dma_start(raw[:], src[bass.ds(h * P + 2 * P, P), :]).then_inc(sem(f"{name}_loaded"), 16)
            sp.wait_ge(sem("wo_split"), B_HEADS - 1)
            sp.dma_start(wo_raw[:], b_wo[(B_HEADS - 1) * P:B_HEADS * P, :]).then_inc(sem("wo_loaded"), 16)

        block = ctx.enter_context(nc.Block())

        @block.sync
        def _(sp):
            sp.dma_start(x[:], xT).then_inc(sem("x_updated0"), 16)
            sp.dma_start(const[:], consts).then_inc(sem("consts_loaded"), 16)
            a_sp(sp)
            f_sp(sp, 1, "f1")
            b_sp(sp)
            f_sp(sp, 3, "f2")
            x_final(sp, 4, CHUNKS - 1)
            sp.dma_start(out, x[:]).then_inc(sem("out_stored"), 16)
            sp.wait_ge(sem("out_stored"), 16)

        @block.gpsimd
        def _(pool):
            a_pool(pool)
            f_pool(pool, 1, "f1")
            b_pool(pool)
            f_pool(pool, 3, "f2")

        @block.scalar
        def _(act):
            norm_act(act, 0)
            a_act(act)
            norm_act(act, 1)
            f_act(act, 1, "f1")
            norm_act(act, 2)
            b_act(act)
            norm_act(act, 3)
            f_act(act, 3, "f2")

        @block.vector
        def _(dve):
            dve.wait_ge(sem("consts_loaded"), 16)
            nc.vector.memset(zero_w[:], 0.0)
            nc.vector.memset(zero_x[:], 0.0)
            nc.vector.tensor_copy(ident_b[:], const[:, 0:P])
            for d in range(2):
                nc.vector.tensor_copy(mask_b[:, d], const[:, P:2 * P])
            nc.vector.tensor_copy(rows_b[:], const[:, 2 * P:2 * P + 32])
            nc.vector.memset(mean_w[:], 1.0 / DM).then_inc(sem("consts_made"), 1)
            norm_dve(dve, 0)
            a_dve(dve)
            norm_dve(dve, 1)
            f_dve(dve, 1, "f1")
            norm_dve(dve, 2)
            b_dve(dve)
            norm_dve(dve, 3)
            f_dve(dve, 3, "f2")

        @block.tensor
        def _(pe):
            norm_pe(pe, 0)
            a_pe(pe)
            norm_pe(pe, 1)
            f_pe(pe, 1, "f1")
            norm_pe(pe, 2)
            b_pe(pe)
            norm_pe(pe, 3)
            f_pe(pe, 3, "f2")


def _constants():
    i = np.arange(P)
    c = np.zeros((P, N_CONST), np.float32)
    c[:, 0:P] = np.eye(P)
    c[:, P:2 * P] = np.where(i[None, :] >= i[:, None], 0.0, MASKED)
    c[:, 2 * P:2 * P + 32] = (i[:, None] % 32 == np.arange(32)[None, :]) & (i[:, None] < 96)
    e = np.arange(EXPERTS)
    c[:, 2 * P + 32:] = (e[None, :] < e[:, None]).reshape(1, -1)
    return c


def _feature_major(w):
    return w.T.reshape(KT, P, w.shape[0]).transpose(1, 0, 2)


def _layout(i):
    c = np.ascontiguousarray
    i = {k: np.asarray(v) for k, v in i.items()}
    w = i["L0_attn_a_W_in"]
    hn = A_HEADS * A_STATE
    bc = w[2 * A_INNER:2 * A_INNER + 2 * hn].reshape(2, A_HEADS, A_STATE, KT, P)
    vg = w[:2 * A_INNER].reshape(2, A_TILES, P, KT, P)
    par = [i["L0_attn_a_conv_w"].reshape(A_TILES, P, A_TAPS).transpose(1, 0, 2).reshape(P, -1),
           i["L0_attn_a_conv_b"].reshape(A_TILES, P).T, i["L0_attn_a_D_param"].reshape(A_TILES, P).T,
           np.tile(i["L0_attn_a_A_log"], 4)[:, None], np.tile(i["L0_attn_a_dt_bias"], 4)[:, None]]
    a_wo = np.zeros((A_TILES + 1, P, DM), np.float32)
    a_wo[1:] = i["L0_attn_a_W_out"].T.reshape(A_TILES, P, DM)

    gu = np.zeros((F_TILES, 2, P, DM), np.float32)
    dn = np.zeros((F_TILES, P, DM), np.float32)
    sg = i["L0_ffn_shared_gate_up_w"].reshape(2, S_HIDDEN, DM)
    sd = i["L0_ffn_shared_down_w"].T
    for t in range(S_TILES):
        n = min(P, S_HIDDEN - t * P)
        gu[t, :, :n] = sg[:, t * P:t * P + n]
        dn[t, :n] = sd[t * P:t * P + n]
    gu[S_TILES:] = i["L0_ffn_w13"].reshape(EXPERTS, 2, R_TILES, ROWS_E, DM).transpose(2, 1, 0, 3, 4).reshape(R_TILES, 2, P, DM)
    dn[S_TILES:] = i["L0_ffn_w2"].reshape(EXPERTS, DM, R_TILES, ROWS_E).transpose(2, 0, 3, 1).reshape(R_TILES, P, DM)
    gu = gu.reshape(F_TILES, 2, P, KT, P).transpose(0, 4, 3, 1, 2).reshape(F_TILES, P, KT * 2 * P)
    rw = np.zeros((LOGITS, DM), np.float32)
    rw[:EXPERTS] = i["L0_ffn_gate_w"]
    rw[EXPERTS] = i["L0_ffn_sgate_w"][0]

    qk = np.stack([i["L0_attn_b_Wq"], i["L0_attn_b_Wk"]]).reshape(2, B_HEADS, B_KD, KT, P)
    v = i["L0_attn_b_Wv"].reshape(B_HEADS, B_V, KT, P)
    cv = np.stack([i["L0_attn_b_Wq_conv"], i["L0_attn_b_Wk_conv"]]).reshape(2, B_HEADS, B_KD, P, B_TAPS)
    cb = np.stack([i["L0_attn_b_bq_conv"], i["L0_attn_b_bk_conv"]], axis=1)
    wo = i["L0_attn_b_Wo"].reshape(DM, B_HEADS, B_VT, P)
    reps = P // B_HEADS
    bg = np.stack([np.tile(i["L0_attn_b_Wb"], (reps, 1)), np.tile(i["L0_attn_b_Wg"], (reps, 1))])
    bpar = [np.tile(i["L0_attn_b_bb"], reps)[:, None], np.tile(i["L0_attn_b_bg"], reps)[:, None]]
    return dict(
        xT=c(i["L0_attn_a_x"].reshape(TOKENS, KT, P).transpose(2, 1, 0)),
        consts=_constants(),
        a_vg=c(vg.transpose(4, 1, 3, 0, 2)),
        a_dt=c(_feature_major(np.tile(w[2 * A_INNER + 2 * hn:], (4, 1)))),
        a_heads=c(bc.transpose(1, 4, 3, 0, 2)).reshape(A_HEADS * P, KT * 2 * P),
        a_wo=a_wo.reshape(-1, DM),
        a_par=c(np.concatenate(par, axis=1)),
        ffn_w=c(np.concatenate([gu, dn], axis=2)).reshape(F_TILES * P, KT * 2 * P + DM),
        router_w=c(_feature_major(rw)),
        b_qk=c(qk.transpose(1, 4, 3, 0, 2)).reshape(B_HEADS * P, QKW),
        b_v=c(v.transpose(0, 3, 2, 1)).reshape(B_HEADS * P, VW),
        b_conv=c(np.concatenate([cv.transpose(1, 3, 0, 4, 2).reshape(B_HEADS * P, CONVW), cb], axis=1)),
        b_wo=c(wo.transpose(1, 3, 2, 0)).reshape(B_HEADS * P, WOW),
        b_bg=c(bg.reshape(2, P, KT, P).transpose(3, 2, 0, 1)),
        b_par=c(np.concatenate(bpar, axis=1)),
    )


def kernel(**inputs):
    import concourse.bacc as bacc
    from concourse.bass_utils import run_bass_kernel_spmd

    arrays = _layout(inputs)
    nc = bacc.Bacc("TRN2", target_bir_lowering=False, num_devices=1)
    args = [nc.dram_tensor(k, a.shape, F32, kind="ExternalInput").ap() for k, a in arrays.items()]
    out = nc.dram_tensor("out", (P, KT, TOKENS), F32, kind="ExternalOutput").ap()
    build_layer(nc, *args, out)
    result = run_bass_kernel_spmd(nc, [arrays], core_ids=[0]).results[0]["out"]
    return np.ascontiguousarray(result.transpose(2, 1, 0)).reshape(BATCH, SEQ, DM)
```

```python
from contextlib import ExitStack

import numpy as np

import concourse.bass as bass
from concourse import mybir

F32 = mybir.dt.float32
FR = mybir.dt.float32r
BF16 = mybir.dt.bfloat16
ALU = mybir.AluOpType
ACT = mybir.ActivationFunctionType
AX_X = mybir.AxisListType.X

P = 128
BATCH, SEQ, DM = 4, 256, 256
TOKENS = BATCH * SEQ
KT = DM // P
CHUNK = 512
CHUNKS = TOKENS // CHUNK
BLOCKS = TOKENS // P
EPS = 1e-5
MASKED = -1e30

A_HEADS, A_STATE, A_HD, A_TAPS = 32, 128, 16, 4
A_INNER = A_HEADS * A_HD
A_TILES = A_INNER // P
A_GROUP = P // A_HD
UNITS = A_GROUP * BATCH
OUT_UNIT = 8
PADDED = SEQ + A_TAPS - 1

B_HEADS, B_KD, B_V, B_TAPS = 16, 128, 256, 4
B_VT = B_V // P

EXPERTS, TOP_K, E_HIDDEN, S_HIDDEN = 16, 4, 176, 704
ROWS_E = P // EXPERTS
R_TILES = E_HIDDEN // ROWS_E
S_TILES = -(-S_HIDDEN // P)
F_TILES = S_TILES + R_TILES
LOGITS = 32

QKW, VW, CONVW, WOW = KT * 2 * P, KT * B_V, 2 * B_TAPS * P, B_VT * DM
TRI = 3 * P

N_CONST = 2 * P + 32
N_APAR = A_TILES * (A_TAPS + 2) + 2
N_BPAR = 2
CHUNK_BLOCKS = CHUNK // P
N_NORM = (2 * KT + 1) * TOKENS + 4 * BLOCKS


def build_layer(nc, xT, consts, a_vg, a_dt, a_heads, a_wo, a_par, ffn_w, router_w, b_qk, b_v, b_conv, b_wo,
                b_bg, b_par, out):
    ctx = ExitStack()
    with ctx:
        sems = {}

        def sem(name):
            if name not in sems:
                sems[name] = ctx.enter_context(nc.semaphore(name))
            return sems[name]

        def sb(stack, name, shape, dt=F32):
            return stack.enter_context(nc.sbuf_tensor(name, shape, dt))

        def pair(stack, name, shape):
            return sb(stack, name + "_hi", shape, FR), sb(stack, name + "_lo", shape, FR)

        x = sb(ctx, "x", [P, KT, TOKENS])
        xn = pair(ctx, "xn", [P, KT, TOKENS])
        const = sb(ctx, "const", [P, N_CONST])
        ident = const[:, 0:P]
        ident_b = sb(ctx, "ident_b", [P, P], BF16)
        mask_b = sb(ctx, "mask_b", [P, 2, P], BF16)
        rows_b = sb(ctx, "rows_b", [P, 32], BF16)
        mean_w = sb(ctx, "mean_w", [P, P])
        zero_w = sb(ctx, "zero_w", [P, P], BF16)
        zero_x = sb(ctx, "zero_x", [P, CHUNK], BF16)
        ps = ctx.enter_context(nc.psum_tensor("ps", [P, 8, CHUNK], F32))

        pro = ExitStack()
        ln_xc = sb(pro, "ln_xc", [P, KT, TOKENS])
        ln_sq = sb(pro, "ln_sq", [P, KT, TOKENS])
        ln_diag = sb(pro, "ln_diag", [P, CHUNKS, CHUNK])
        ln_v = sb(pro, "ln_v", [P, BLOCKS])
        ln_s = sb(pro, "ln_s", [P, BLOCKS])
        ln_r = sb(pro, "ln_r", [P, BLOCKS])
        ln_t = sb(pro, "ln_t", [P, BLOCKS])
        pro.close()

        ma = ExitStack()
        valz = pair(ma, "valz", [P, A_GROUP, BLOCKS, P])
        bc_at = ExitStack()
        bmat = [pair(bc_at, f"bmat{p}", [P, TOKENS]) for p in range(2)]
        cmat = [pair(bc_at, f"cmat{p}", [P, TOKENS]) for p in range(2)]
        bc_at.close()
        pro = ExitStack()
        a_vg_raw = sb(pro, "a_vg_raw", [P, A_TILES, KT, 2, P])
        a_vg_w = pair(pro, "a_vg_w", [P, A_TILES, KT, 2, P])
        a_dt_raw = sb(pro, "a_dt_raw", [P, KT, P])
        a_dt_w = pair(pro, "a_dt_w", [P, KT, P])
        pro.close()
        ma2 = ExitStack()
        bc_hold = sb(ma2, "bc_hold", [P, 8 * TOKENS])
        valT = sb(ma2, "valT", [P, A_TILES, TOKENS])
        gateT = sb(ma2, "gateT", [P, A_TILES, TOKENS])
        e_a = sb(ma2, "e_a", [P, 2, TRI])
        m_a = sb(ma2, "m_a", [P, 2, TRI])
        ms_a = pair(ma2, "ms_a", [P, 3, TRI])
        aw_raw = sb(ma2, "aw_raw", [P, 2, KT, 2, P])
        aw = pair(ma2, "aw", [P, 2, KT, 2, P])
        awo_raw = sb(ma2, "awo_raw", [P, DM])
        awo = pair(ma2, "awo", [P, DM])
        yT = sb(ma2, "yT", [P, TOKENS])
        ys = pair(ma2, "ys", [P, TOKENS])
        stage = sb(ma2, "stage", [P, TOKENS])
        pieces_a = sb(ma2, "pieces_a", [P, BATCH, TRI], BF16)
        ncum_a = sb(ma2, "ncum_a", [P, BLOCKS, 32])
        apar = sb(ma2, "apar", [P, N_APAR])
        neg_a = sb(ma2, "neg_a", [P, 1])
        ma2.close()
        ma.close()
        tmp = ExitStack()
        VALZ, VPAD = A_GROUP * BLOCKS * P, A_TILES * BATCH * PADDED
        sb(tmp, "valz_hold", [P, 2 * VALZ - VPAD])
        vpad = sb(tmp, "vpad", [P, A_TILES, BATCH, PADDED])
        sb(tmp, "bc_vg_hold", [P, 8 * TOKENS + 2 * A_TILES * TOKENS])
        dec_z = sb(tmp, "dec_z", [P, TOKENS])
        dec_e = sb(tmp, "dec_e", [P, TOKENS])
        tmp.close()
        a_conv_w = apar[:, 0:A_TILES * A_TAPS].rearrange("p (t j) -> p t j", j=A_TAPS)
        a_conv_b = apar[:, A_TILES * A_TAPS:A_TILES * (A_TAPS + 1)]
        a_d = apar[:, A_TILES * (A_TAPS + 1):A_TILES * (A_TAPS + 2)]
        a_log = apar[:, N_APAR - 2:N_APAR - 1]
        a_dt_b = apar[:, N_APAR - 1:N_APAR]

        mb = ExitStack()
        sb(mb, "ln_hold_b", [P, max(N_NORM, 6 * TOKENS)])
        qpad = pair(mb, "qpad", [P, 2, BATCH, PADDED])
        qk = [pair(mb, f"qk{p}", [P, 2, TOKENS]) for p in range(2)]
        qf = sb(mb, "qf", [P, 2, CHUNK])
        vtok = [pair(mb, f"vtok{p}", [P, BLOCKS, B_V]) for p in range(2)]
        pro = ExitStack()
        wbg_raw = sb(pro, "wbg_raw", [P, KT, 2, P])
        wbg = pair(pro, "wbg", [P, KT, 2, P])
        pro.close()
        oT = pair(mb, "oT", [P, B_VT, TOKENS])
        e_b = sb(mb, "e_b", [P, 2, TRI])
        m_b = sb(mb, "m_b", [P, 2, TRI])
        ms_b = pair(mb, "ms_b", [P, 2, TRI])
        wqk_raw = sb(mb, "wqk_raw", [P, KT, 2, P])
        wqk = pair(mb, "wqk", [P, KT, 2, P])
        wv_raw = sb(mb, "wv_raw", [P, KT, B_V])
        wv = pair(mb, "wv", [P, KT, B_V])
        wconv_raw_all = sb(mb, "wconv_raw", [P, CONVW + 2])
        wconv_raw = wconv_raw_all[:, 0:CONVW].rearrange("p (s j m) -> p s j m", s=2, j=B_TAPS)
        conv_bias = sb(mb, "conv_bias", [P, 2])
        wconv = pair(mb, "wconv", [P, 2, B_TAPS, P])
        wo_raw = sb(mb, "wo_raw", [P, B_VT, DM])
        wo = pair(mb, "wo", [P, B_VT, DM])
        pieces_b = sb(mb, "pieces_b", [P, BATCH, TRI], BF16)
        ncum_b = sb(mb, "ncum_b", [P, BLOCKS, 32])
        bpar = sb(mb, "bpar", [P, N_BPAR])
        mb.close()
        tmp = ExitStack()
        dec_b = [sb(tmp, f"dec_b{i}", [P, TOKENS]) for i in range(6)]
        tmp.close()

        mf = ExitStack()
        sb(mf, "ln_hold_f", [P, N_NORM])
        fw_raw = sb(mf, "fw_raw", [P, 2, KT * 2 * P + DM])
        fgu = pair(mf, "fgu", [P, 2, KT, 2, P])
        fd = pair(mf, "fd", [P, 2, DM])
        f_s = sb(mf, "f_s", [P, CHUNKS, CHUNK])
        f_sc = sb(mf, "f_sc", [P, CHUNKS, CHUNK])
        f_h = sb(mf, "f_h", [P, CHUNKS, CHUNK])
        fh = pair(mf, "fh", [P, 2, TOKENS])
        coef_r = sb(mf, "coef_r", [P, TOKENS])
        coef_s = sb(mf, "coef_s", [P, TOKENS])
        lgT = coef_r
        rw_raw = sb(mf, "rw_raw", [P, KT, 2, P])
        rw = pair(mf, "rw", [P, KT, 2, P])
        lg = sb(mf, "lg", [P, BLOCKS, LOGITS])
        pr = sb(mf, "pr", [P, BLOCKS, EXPERTS])
        r_mx = sb(mf, "r_mx", [P, BLOCKS])
        r_sum = sb(mf, "r_sum", [P, BLOCKS])
        r_keep = sb(mf, "r_keep", [P, BLOCKS, EXPERTS])
        r_top = sb(mf, "r_top", [P, BLOCKS, 8])
        r_gt = sb(mf, "r_gt", [P, BLOCKS, EXPERTS])
        r_eq = sb(mf, "r_eq", [P, BLOCKS, EXPERTS])
        r_before = sb(mf, "r_before", [P, BLOCKS, EXPERTS])
        r_cnt = sb(mf, "r_cnt", [P, BLOCKS])
        cexp = sb(mf, "cexp", [P, BLOCKS, EXPERTS, ROWS_E])
        mf.close()

        def f32(ap):
            return ap.bitcast(F32)

        def mm3(o, w, v, first, last=True):
            nc.tensor.matmul(o, w[0], v[0], start=first, stop=False, skip_group_check=True)
            nc.tensor.matmul(o, w[0], v[1], start=False, stop=False, skip_group_check=True)
            return nc.tensor.matmul(o, w[1], v[0], start=False, stop=last, skip_group_check=True)

        def at(t, *idx):
            return tuple(v[idx] for v in t)

        def half_view(ap):
            return ap.rearrange("p (h n) -> p h n", n=P)

        def halves(t):
            return tuple(half_view(v) for v in t)

        def first_m(ap):
            return half_view(ap[:, 0:TRI])[:, 0:3:2, :]

        def cols(c):
            return slice(c * CHUNK, (c + 1) * CHUNK)

        def counter(eng, name, start=0):
            n = [start]

            def step(ins):
                n[0] += 1
                ins.then_inc(sem(name), 1)
                eng.wait_ge(sem(name), n[0])
            return step

        X_FINAL = {1: lambda c: 4 * A_TILES + 2 * c + 2, 2: lambda c: 2 * c + 2,
                   3: lambda c: 4 * B_HEADS + 2 * c + 2, 4: lambda c: 2 * c + 2}

        def x_final(eng, n, c):
            if n == 0:
                eng.wait_ge(sem(f"x_loaded{c}"), 16)
            else:
                eng.wait_ge(sem(f"x_updated{n}"), X_FINAL[n](c))

        def mean_bank(n):
            return 6 if n % 2 else 0

        def norm_pe(pe, n):
            pe.wait_ge(sem("mean_made"), 1)
            for c in range(CHUNKS):
                x_final(pe, n, c)
                for k in range(KT):
                    ins = nc.tensor.matmul(ps[:, mean_bank(n) + c, :], mean_w[:], x[:, k, cols(c)], start=k == 0, stop=k == KT - 1)
                ins.then_inc(sem("ln_mean"), 1)
            for c in range(CHUNKS):
                pe.wait_ge(sem("ln_sq"), CHUNKS * n + c + 1)
                for i in range(CHUNK_BLOCKS):
                    for k in range(KT):
                        ins = nc.tensor.matmul(ps[:, 2 + c, i:i + 1], ln_sq[:, k, block_of(c, i)], mean_w[:, 0:1],
                                               start=i == 0 and k == 0, stop=i == CHUNK_BLOCKS - 1 and k == KT - 1,
                                               skip_group_check=True)
                ins.then_inc(sem("ln_var"), 1)
            pe.wait_ge(sem("consts_loaded"), 16)
            for c in range(CHUNKS):
                pe.wait_ge(sem("ln_diag"), CHUNKS * n + c + 1)
                nc.tensor.matmul(ps[:, 2 + c, :], mean_w[:], ln_diag[:, c, :], start=True, stop=True).then_inc(sem("ln_rstd"), 1)

        def block_of(c, i):
            return slice(c * CHUNK + i * P, c * CHUNK + (i + 1) * P)

        def norm_act(act, n, prepare_first, prepare_rest):
            for c in range(CHUNKS):
                act.wait_ge(sem("ln_xc"), CHUNKS * n + c + 1)
                nc.scalar.activation(ln_sq[:, :, cols(c)], ln_xc[:, :, cols(c)], ACT.Square).then_inc(sem("ln_sq"), 1)
            for c in range(CHUNKS):
                act.wait_ge(sem("ln_v"), CHUNKS * n + c + 1)
                nc.scalar.activation(norm_cols(ln_s, c), norm_cols(ln_v, c), ACT.Sqrt).then_inc(sem("ln_std"), 1)
            prepare_first(act)
            for c in range(CHUNKS):
                act.wait_ge(sem("ln_xn"), CHUNKS * n + c + 1)
                nc.scalar.copy(xn[0][:, :, cols(c)], ln_xc[:, :, cols(c)]).then_inc(sem("ln_hi"), 1)
            prepare_rest(act)

        def norm_cols(t, c):
            return t[:, c * CHUNK_BLOCKS:(c + 1) * CHUNK_BLOCKS]

        def norm_dve(dve, n):
            step = counter(dve, "ln_step", 4 * CHUNKS * n)

            def rstd(c):
                v, s, r, t = (norm_cols(a, c) for a in (ln_v, ln_s, ln_r, ln_t))
                dve.wait_ge(sem("ln_var"), CHUNKS * n + c + 1)
                nc.vector.tensor_scalar(v, ps[:, 2 + c, 0:CHUNK_BLOCKS], EPS, None, ALU.add).then_inc(sem("ln_v"), 1)
                dve.wait_ge(sem("ln_std"), CHUNKS * n + c + 1)
                step(nc.vector.reciprocal(r, s))
                step(nc.vector.tensor_tensor(t, r, r, ALU.mult))
                step(nc.vector.scalar_tensor_tensor(t, t, -0.5, v, ALU.mult, ALU.mult))
                step(nc.vector.scalar_tensor_tensor(r, t, 1.5, r, ALU.add, ALU.mult))
                for i in range(CHUNK_BLOCKS):
                    ins = nc.vector.tensor_scalar(ln_diag[:, c, i * P:(i + 1) * P], ident, r[:, i:i + 1], float(DM), ALU.mult, ALU.mult)
                ins.then_inc(sem("ln_diag"), 1)

            def scale(c):
                dve.wait_ge(sem("ln_rstd"), CHUNKS * n + c + 1)
                nc.vector.tensor_tensor(ln_xc[:, :, cols(c)], ln_xc[:, :, cols(c)],
                                        ps[:, 2 + c, None, :].broadcast_to([P, KT, CHUNK]), ALU.mult).then_inc(sem("ln_xn"), 1)

            def lo(c):
                dve.wait_ge(sem("ln_hi"), CHUNKS * n + c + 1)
                nc.vector.tensor_tensor(xn[1][:, :, cols(c)], ln_xc[:, :, cols(c)], f32(xn[0][:, :, cols(c)]),
                                        ALU.subtract).then_inc(sem("ln_done"), 1)

            for c in range(CHUNKS):
                dve.wait_ge(sem("ln_mean"), CHUNKS * n + c + 1)
                mean = ps[:, mean_bank(n) + c, None, :].broadcast_to([P, KT, CHUNK])
                nc.vector.tensor_tensor(ln_xc[:, :, cols(c)], x[:, :, cols(c)], mean,
                                        ALU.subtract).then_inc(sem("ln_xc"), 1)
            rstd(0)
            rstd(1)
            scale(0)
            scale(1)
            lo(0)
            lo(1)

        def normed(eng, n, c=CHUNKS - 1):
            eng.wait_ge(sem("ln_done"), CHUNKS * n + c + 1)

        def split_hi(dst, src, hi_sem):
            return nc.scalar.copy(dst[0], src).then_inc(sem(hi_sem), 1)

        def split_lo(pool, dst, src, hi_sem, count, done_sem):
            pool.wait_ge(sem(hi_sem), count)
            return nc.gpsimd.tensor_tensor(dst[1], src, f32(dst[0]), ALU.subtract).then_inc(sem(done_sem), 1)

        def a_pe(pe):
            pe.wait_ge(sem("a_pro_w"), 1)
            products = A_PRODUCTS
            for n, (t, s, c) in enumerate(products):
                normed(pe, 0, c)
                if n >= 8:
                    pe.wait_ge(sem("a_pro_read"), n - 7)
                if c == 0 and t >= 0 and s == 0:
                    pe.wait_ge(sem("a_pro_w"), 2 + t)
                for k in range(KT):
                    w = at(a_dt_w, slice(None), k) if t < 0 else at(a_vg_w, slice(None), t, k, s)
                    ins = mm3(ps[:, n % 8, :], w, at(xn, slice(None), k, cols(c)), k == 0, k == KT - 1)
                ins.then_inc(sem("a_pro_done"), 1)
            pe.wait_ge(sem("a_pro_read"), len(products))
            a_project_pe(pe, 0, 0, 0)
            a_project_pe(pe, 0, 0, 1)
            a_project_pe(pe, 0, 0, 2)
            a_project_pe(pe, 0, 0, 3)
            pe.wait_ge(sem("a_cum"), 1)
            for i in range(BLOCKS):
                ins = nc.tensor.transpose(ps[:, 2, i * 32:(i + 1) * 32], dec_e[0:32, i * P:(i + 1) * P], ident[0:32, 0:32])
            ins.then_inc(sem("a_cumT"), 1)
            pe.wait_ge(sem("a_ncum"), 1)
            pe.wait_ge(sem("a_pieces"), 6)
            with pe.Fori(0, A_TILES - 1) as g:
                a_group_pe(pe, g, False)
            a_group_pe(pe, A_TILES - 1, True)
            for n in range(4):
                if n >= 2:
                    pe.wait_ge(sem("x_updated1"), 4 * A_TILES + n - 1)
                a_out_pe(pe, A_TILES, n, n % 2)

        A_PRODUCTS = ([(-1, 0, 0), (0, 0, 0), (-1, 0, 1), (0, 0, 1)]
                      + [(t, 0, c) for t in range(1, A_TILES) for c in range(CHUNKS)]
                      + [(t, 1, c) for t in range(A_TILES) for c in range(CHUNKS)])

        def a_project_pe(pe, h, parity, q):
            s, c = q // 2, q % 2
            if q == 0:
                pe.wait_ge(sem("aw_split"), h + 1)
            if not (isinstance(h, int) and h == 0 and q < 2):
                pe.wait_ge(sem("bc_split"), 4 * h + q - 1)
            for k in range(KT):
                ins = mm3(ps[:, c, :], at(aw, slice(None), parity, k, s), at(xn, slice(None), k, cols(c)),
                          k == 0, k == KT - 1)
            ins.then_inc(sem("a_p_done"), 1)

        def a_out_pe(pe, g, n, bank):
            c, m = n // KT, n % KT
            if n == 0:
                pe.wait_ge(sem("ys_split"), 2 * g + 2)
                pe.wait_ge(sem("awo_split"), g + 1)
            mm3(ps[:, bank, :], at(awo, slice(None), slice(m * P, (m + 1) * P)), at(ys, slice(None), cols(c)),
                True).then_inc(sem("a_wo_done"), 1)

        def a_state_pe(pe, g, u):
            j, b = u // BATCH, u % BATCH
            p, l0 = j % 2, b * SEQ
            if u >= 2:
                pe.wait_ge(sem("a_m_done"), UNITS * g + u - 1)
            if b % 2 == 0:
                pe.wait_ge(sem("bc_split"), UNITS * g + 4 * j + 3 + b // 2)
            d, s = ps[:, 2 + u % 2, :], ps[:, 4 + u % 2, :]
            lhs = rows_b[:, bass.ds(g * A_GROUP + j, 1)].broadcast_to([P, P])
            nc.tensor.matmul(d[:, 0:TRI], lhs, pieces_a[:, b, :], start=True, stop=False, skip_group_check=True)
            nc.tensor.matmul(d[:, 0:2 * P], ident_b[:], mask_b[:].rearrange("p d n -> p (d n)"), start=False, stop=True, skip_group_check=True)
            mm3(first_m(s), at(bmat[p], slice(None), slice(l0, l0 + P)), halves(at(cmat[p], slice(None), slice(l0, l0 + SEQ))), True, False)
            mm3(s[:, P:2 * P], at(bmat[p], slice(None), slice(l0 + P, l0 + SEQ)),
                at(cmat[p], slice(None), slice(l0 + P, l0 + SEQ)), False).then_inc(sem("a_s_done"), 1)

        def a_value_pe(pe, g, u):
            j, b = u // BATCH, u % BATCH
            pe.wait_ge(sem("a_m_split"), UNITS * g + u + 1)
            if u == 0:
                pe.wait_ge(sem("valz_split"), 2 * g + 2)
                pe.wait_ge(sem("y_read"), 2 * g + 2)
            o, l0, t = ps[:, 6 + b // 2, :], (b % 2) * SEQ, 2 * b
            ms = at(ms_a, slice(None), u % 3)
            mm3(half_view(o[:, l0:l0 + SEQ]), at(valz, slice(None), j, t), tuple(first_m(v) for v in ms),
                j == 0 and b % 2 == 0, False)
            mm3(o[:, l0 + P:l0 + SEQ], at(valz, slice(None), j, t + 1), at(ms, slice(None), slice(P, 2 * P)),
                False, j == A_GROUP - 1).then_inc(sem("a_y_done"), 1)

        def a_group_pe(pe, g, last):
            pe.wait_ge(sem("stage_ready"), g + 1)
            pe.wait_ge(sem("bc_split"), UNITS * g + BATCH)
            for i in range(BLOCKS):
                ins = nc.tensor.transpose(ps[:, i // 4, (i % 4) * P:(i % 4 + 1) * P], stage[:, i * P:(i + 1) * P], ident)
                if i % 4 == 3:
                    ins.then_inc(sem("val_T"), 1)
            for u in range(UNITS):
                a_state_pe(pe, g, u)
                if u < 2:
                    pe.wait_ge(sem("valz_split"), 2 * g + u + 1)
                n = u - OUT_UNIT
                if 0 < n <= 4:
                    pe.wait_ge(sem("x_updated1"), 4 * g + n)
                if not (last and u >= UNITS - BATCH):
                    a_project_pe(pe, g * A_GROUP + u // BATCH + 1, (u // BATCH + 1) % 2, u % BATCH)
                if 0 <= n < 4:
                    pe.wait_ge(sem("bc_split"), UNITS * g + BATCH + u)
                    a_out_pe(pe, g, n, (u + 1) % 2)
                if u >= 2:
                    a_value_pe(pe, g, u - 2)
            a_value_pe(pe, g, UNITS - 2)
            a_value_pe(pe, g, UNITS - 1)

        def a_prepare_act(act):
            act.wait_ge(sem("a_pro_loaded"), 32)
            split_hi(at(a_dt_w, slice(None)), a_dt_raw[:], "a_pro_hi")
            for t in range(A_TILES):
                split_hi(at(a_vg_w, slice(None), t), a_vg_raw[:, t], "a_pro_hi")

        def a_prepare_rest_act(act):
            for h in range(2):
                act.wait_ge(sem(f"aw_loaded{h}"), 16)
                split_hi(at(aw, slice(None), h), aw_raw[:, h], "aw_hi")
            act.wait_ge(sem("awo_loaded"), 16)
            split_hi(at(awo, slice(None)), awo_raw[:], "awo_hi")

        def a_act(act):
            act.wait_ge(sem("a_params"), 16)
            act.wait_ge(sem("vpad_zero"), 1)
            for n, (t, s, c) in enumerate(A_PRODUCTS):
                act.wait_ge(sem("a_pro_done"), n + 1)
                if t < 0:
                    ins = nc.scalar.activation(dec_z[:, cols(c)], ps[:, n, :], ACT.Identity, bias=a_dt_b)
                elif s == 0:
                    ins = nc.scalar.copy(vpad[:, t, 2 * c:2 * c + 2, A_TAPS - 1:PADDED],
                                         ps[:, n % 8, :].rearrange("p (b l) -> p b l", l=SEQ))
                else:
                    ins = nc.scalar.activation(gateT[:, t, cols(c)], ps[:, n % 8, :], ACT.Silu)
                ins.then_inc(sem("a_pro_read"), 1)
                if (t, s, c) == (1, 0, 1):
                    act.wait_ge(sem("a_abs"), 1)
                    nc.scalar.activation(dec_e[:], dec_e[:], ACT.Exp, scale=-1.0).then_inc(sem("a_exp"), 1)
                    nc.scalar.activation(neg_a[:], a_log, ACT.Exp)
                    act.wait_ge(sem("a_exp"), 1)
                    nc.scalar.activation(dec_e[:], dec_e[:], ACT.Ln, bias=1.0).then_inc(sem("a_ln"), 1)
            for t in range(A_TILES):
                act.wait_ge(sem("a_conv"), t + 1)
                nc.scalar.activation(valT[:, t, :], valT[:, t, :], ACT.Silu, bias=a_conv_b[:, t:t + 1]).then_inc(sem("a_val"), 1)
                if t % 2 == 0:
                    for q in range(t, t + 2):
                        a_project_act(act, 0, 0, q)
            act.wait_ge(sem("a_cumT"), 1)
            nc.scalar.mul(ncum_a[:], ps[:, 2, 0:BLOCKS * 32].rearrange("p (i h) -> p i h", h=32), -1.0).then_inc(sem("a_ncum"), 1)
            act.wait_ge(sem("a_ncum"), 1)
            act.wait_ge(sem("valz_zero"), 3 + A_TILES)
            with act.Fori(0, A_TILES - 1) as g:
                a_group_act(act, g, False)
            a_group_act(act, A_TILES - 1, True)

        def a_project_act(act, h, parity, q):
            s, c = q // 2, q % 2
            act.wait_ge(sem("a_p_done"), 4 * h + q + 1)
            nc.scalar.copy((bmat, cmat)[s][parity][0][:, cols(c)], ps[:, c, :]).then_inc(sem("bc_hi"), 1)

        def a_group_act(act, g, last):
            for c in range(2):
                act.wait_ge(sem("val_T"), 2 * g + c + 1)
                nc.scalar.copy(valz_diagonal(valz[0], c), val_blocks(c)).then_inc(sem("valz_hi"), 1)
            for u in range(UNITS):
                j, b = u // BATCH, u % BATCH
                h = g * A_GROUP + j
                d = ps[:, 2 + u % 2, :]
                act.wait_ge(sem("a_s_done"), UNITS * g + u + 1)
                act.wait_ge(sem("a_ncum"), 1)
                nc.scalar.activation(first_m(e_a[:, u % 2]), first_m(d), ACT.Exp, bias=ncum_a[:, 2 * b, bass.ds(h, 1)])
                nc.scalar.activation(e_a[:, u % 2, P:2 * P], d[:, P:2 * P], ACT.Exp,
                                     bias=ncum_a[:, 2 * b + 1, bass.ds(h, 1)]).then_inc(sem("a_e_done"), 1)
                if not (last and u >= UNITS - BATCH):
                    a_project_act(act, h + 1, (j + 1) % 2, b)
                act.wait_ge(sem("a_m_done"), UNITS * g + u + 1)
                split_hi(at(ms_a, slice(None), u % 3), m_a[:, u % 2, :], "a_m_hi")
                if b == 1 and not (last and j >= A_GROUP - 2):
                    act.wait_ge(sem(f"aw_loaded{j % 2}"), 8 * h + 32 - 8 * (j % 2))
                    split_hi(at(aw, slice(None), j % 2), aw_raw[:, j % 2], "aw_hi")
                if u == OUT_UNIT + 8:
                    act.wait_ge(sem("awo_loaded"), 16 * g + 32)
                    split_hi(at(awo, slice(None)), awo_raw[:], "awo_hi")
            for c in range(CHUNKS):
                act.wait_ge(sem("y_gated"), 2 * g + c + 1)
                split_hi(at(ys, slice(None), cols(c)), yT[:, cols(c)], "ys_hi")

        def val_blocks(c):
            return ps[:, c, :].rearrange("p (i j d) -> p i j d", j=A_GROUP, d=A_HD)

        def valz_diagonal(z, c):
            flat = z[:].rearrange("p j i m -> p (j i m)")
            step = BLOCKS * P + A_HD
            ap = flat[:, 4 * c * P:4 * c * P + A_HD]
            return bass.AP(ap.tensor, ap.offset, [list(ap.ap[0]), [P, 4], [step, A_GROUP], [1, A_HD]])

        def a_dve(dve):
            step = counter(dve, "a_dve_step")
            dve.wait_ge(sem("a_params"), 16)
            dve.wait_ge(sem("a_pro_read"), 3)
            nc.vector.scalar_tensor_tensor(dec_e[:], dec_z[:], -1.0, dec_z[:], ALU.mult, ALU.max).then_inc(sem("a_abs"), 1)
            a_conv_dve(dve, step, 0)
            dve.wait_ge(sem("a_ln"), 1)
            step(nc.vector.scalar_tensor_tensor(dec_e[:], dec_z[:], 0.0, dec_e[:], ALU.max, ALU.add))
            step(nc.vector.tensor_scalar(dec_z[:], dec_e[:], neg_a[:], -1.0, ALU.mult, ALU.mult))
            nc.vector.tensor_tensor_scan(dec_e[:], yT[:], dec_z[:], 0.0, ALU.mult, ALU.add).then_inc(sem("a_cum"), 1)
            dve.wait_ge(sem("a_cum"), 1)
            split_pieces(dve, step, pieces_a, dec_e, dec_z, stage, "a_pieces")
            a_conv_dve(dve, step, 1)
            for q in range(2):
                a_project_dve(dve, 0, 0, q)
            a_conv_dve(dve, step, 2)
            for q in range(2, 4):
                a_project_dve(dve, 0, 0, q)
            a_conv_dve(dve, step, 3)
            dve.wait_ge(sem("a_val"), 1)
            nc.vector.tensor_copy(stage[:], valT[:, 0, :]).then_inc(sem("stage_ready"), 1)
            dve.wait_ge(sem("a_val"), A_TILES)
            dve.wait_ge(sem("valz_zero"), 3 + A_TILES)
            with dve.Fori(0, A_TILES - 1) as g:
                a_group_dve(dve, g, False)
            a_group_dve(dve, A_TILES - 1, True)
            for n in range(4):
                a_out_dve(dve, A_TILES, n, n % 2)

        def a_early_dve(dve):
            nc.vector.memset(vpad[:, :, :, 0:A_TAPS - 1], 0.0).then_inc(sem("vpad_zero"), 1)
            nc.vector.memset(yT[:], 1.0).then_inc(sem("a_early"), 1)
            dve.wait_ge(sem("a_early"), 1)
            nc.vector.memset(yT[:, 0:TOKENS:SEQ], 0.0).then_inc(sem("a_early"), 1)
            nc.vector.memset(pieces_a[:], 0.0).then_inc(sem("a_early"), 1)
            nc.vector.memset(f32(ys[0][:]), 0.0).then_inc(sem("ys_split"), 1)
            nc.vector.memset(f32(ys[1][:]), 0.0).then_inc(sem("ys_split"), 1)
            nc.vector.memset(neg_a[:], 0.0).then_inc(sem("y_read"), 2)
            dve.wait_ge(sem("a_early"), 3)

        def a_conv_dve(dve, step, t):
            dve.wait_ge(sem("a_pro_read"), 1 + max(A_PRODUCTS.index((t, 0, c)) for c in range(CHUNKS)))
            v = valT[:, t, :].rearrange("p (b l) -> p b l", l=SEQ)
            step(nc.vector.tensor_scalar(v, vpad[:, t, :, 0:SEQ], a_conv_w[:, t, 0:1], None, ALU.mult))
            for j in range(1, A_TAPS):
                ins = nc.vector.scalar_tensor_tensor(v, vpad[:, t, :, j:j + SEQ], a_conv_w[:, t, j:j + 1], v, ALU.mult, ALU.add)
                if j < A_TAPS - 1:
                    step(ins)
            ins.then_inc(sem("a_conv"), 1)

        def split_pieces(dve, step, dst, v, t, hold, done):
            hb = hold[:].bitcast(BF16)
            p1, p2 = hb[:, 0:TOKENS], hb[:, TOKENS:2 * TOKENS]

            def place(rows, src):
                src = src[rows].rearrange("p (b l) -> p b l", l=SEQ)
                nc.vector.tensor_copy(dst[rows, :, 0:SEQ], src).then_inc(sem(done), 1)
                nc.vector.tensor_copy(dst[rows, :, SEQ:TRI], src[:, :, P:SEQ]).then_inc(sem(done), 1)
            step(nc.vector.tensor_copy(p1, v[:]))
            place(slice(0, 32), p1)
            step(nc.vector.tensor_tensor(t[:], v[:], p1, ALU.subtract))
            step(nc.vector.tensor_copy(p2, t[:]))
            place(slice(32, 64), p2)
            step(nc.vector.tensor_tensor(t[:], t[:], p2, ALU.subtract))
            place(slice(64, 96), t[:])

        def a_project_dve(dve, h, parity, q):
            s, c = q // 2, q % 2
            m = (bmat, cmat)[s][parity]
            dve.wait_ge(sem("bc_hi"), 4 * h + q + 1)
            nc.vector.tensor_tensor(m[1][:, cols(c)], ps[:, c, :], f32(m[0][:, cols(c)]),
                                    ALU.subtract).then_inc(sem("bc_split"), 1)

        def a_out_dve(dve, g, n, bank):
            c, m = n // KT, n % KT
            dve.wait_ge(sem("a_wo_done"), 4 * g + n + 1)
            nc.vector.tensor_tensor(x[:, m, cols(c)], x[:, m, cols(c)], ps[:, bank, :], ALU.add).then_inc(sem("x_updated1"), 1)

        def a_group_dve(dve, g, last):
            for c in range(2):
                dve.wait_ge(sem("valz_hi"), 2 * g + c + 1)
                nc.vector.tensor_tensor(valz_diagonal(valz[1], c), val_blocks(c), f32(valz_diagonal(valz[0], c)),
                                        ALU.subtract).then_inc(sem("valz_split"), 1)
            for u in range(UNITS):
                j, b = u // BATCH, u % BATCH
                dve.wait_ge(sem("a_e_done"), UNITS * g + u + 1)
                if u >= 2:
                    dve.wait_ge(sem("a_m_split"), UNITS * g + u - 1)
                nc.vector.tensor_tensor(m_a[:, u % 2, :], ps[:, 4 + u % 2, 0:TRI], e_a[:, u % 2, :],
                                        ALU.mult).then_inc(sem("a_m_done"), 1)
                if not (last and u >= UNITS - BATCH):
                    a_project_dve(dve, g * A_GROUP + j + 1, (j + 1) % 2, b)
                if 0 <= u - OUT_UNIT < 4:
                    a_out_dve(dve, g, u - OUT_UNIT, (u + 1) % 2)
                if u == OUT_UNIT - 2 and not last:
                    nc.vector.tensor_copy(stage[:], group_tile(valT, g + 1, 0, TOKENS)).then_inc(sem("stage_ready"), 1)
            for c in range(CHUNKS):
                dve.wait_ge(sem("a_y_done"), UNITS * g + UNITS)
                nc.vector.scalar_tensor_tensor(yT[:, cols(c)], group_tile(valT, g, c * CHUNK, CHUNK), a_d[:, bass.ds(g, 1)],
                                               ps[:, 6 + c, :], ALU.mult, ALU.add).then_inc(sem("y_read"), 1)
            for c in range(CHUNKS):
                dve.wait_ge(sem("y_read"), 2 * g + 2 + c + 1)
                nc.vector.tensor_tensor(yT[:, cols(c)], yT[:, cols(c)], group_tile(gateT, g, c * CHUNK, CHUNK),
                                        ALU.mult).then_inc(sem("y_gated"), 1)
            for c in range(CHUNKS):
                dve.wait_ge(sem("ys_hi"), 2 * g + c + 1)
                nc.vector.tensor_tensor(ys[1][:, cols(c)], yT[:, cols(c)], f32(ys[0][:, cols(c)]),
                                        ALU.subtract).then_inc(sem("ys_split"), 1)

        def group_tile(t, g, first, n):
            return t[:].rearrange("p t n -> p (t n)")[:, bass.ds(g * TOKENS + first, n)]

        def a_pool(pool):
            hi, lo = (f32(v[:].rearrange("p j i m -> p (j i m)")) for v in valz)
            nc.gpsimd.memset(hi[:, N_NORM:], 0.0).then_inc(sem("valz_zero"), 1)
            nc.gpsimd.memset(lo[:, 0:VALZ - VPAD], 0.0).then_inc(sem("valz_zero"), 1)
            split_lo(pool, at(a_dt_w, slice(None)), a_dt_raw[:], "a_pro_hi", 1, "a_pro_w")
            for t in range(A_TILES):
                split_lo(pool, at(a_vg_w, slice(None), t), a_vg_raw[:, t], "a_pro_hi", 2 + t, "a_pro_w")
            for h in range(2):
                split_lo(pool, at(aw, slice(None), h), aw_raw[:, h], "aw_hi", h + 1, "aw_split")
            split_lo(pool, at(awo, slice(None)), awo_raw[:], "awo_hi", 1, "awo_split")
            normed(pool, 0)
            nc.gpsimd.memset(hi[:, 0:N_NORM], 0.0).then_inc(sem("valz_zero"), 1)
            part = VPAD // A_TILES
            for t in range(A_TILES):
                pool.wait_ge(sem("a_conv"), t + 1)
                nc.gpsimd.memset(lo[:, VALZ - VPAD + t * part:VALZ - VPAD + (t + 1) * part], 0.0).then_inc(sem("valz_zero"), 1)
            with pool.Fori(0, A_TILES - 1) as g:
                a_group_pool(pool, g, False)
            a_group_pool(pool, A_TILES - 1, True)

        def a_group_pool(pool, g, last):
            for u in range(UNITS):
                j, b = u // BATCH, u % BATCH
                split_lo(pool, at(ms_a, slice(None), u % 3), m_a[:, u % 2, :], "a_m_hi", UNITS * g + u + 1, "a_m_split")
                if b == 1 and not (last and j >= A_GROUP - 2):
                    split_lo(pool, at(aw, slice(None), j % 2), aw_raw[:, j % 2], "aw_hi", g * A_GROUP + j + 3, "aw_split")
                if u == OUT_UNIT + 8:
                    split_lo(pool, at(awo, slice(None)), awo_raw[:], "awo_hi", g + 2, "awo_split")

        def a_sp(sp):
            sp.dma_start(a_dt_raw[:], a_dt).then_inc(sem("a_pro_loaded"), 16)
            sp.dma_start(a_vg_raw[:], a_vg).then_inc(sem("a_pro_loaded"), 16)
            sp.dma_start(apar[:], a_par).then_inc(sem("a_params"), 16)
            for h in range(2):
                sp.dma_start(aw_raw[:, h], a_heads[h * P:(h + 1) * P, :]).then_inc(sem(f"aw_loaded{h}"), 16)
            sp.dma_start(awo_raw[:], a_wo[0:P, :]).then_inc(sem("awo_loaded"), 16)
            with sp.Fori(0, A_TILES - 1) as g:
                a_group_sp(sp, g, False)
            a_group_sp(sp, A_TILES - 1, True)

        def a_group_sp(sp, g, last):
            for j in range(A_GROUP):
                if j == 0:
                    sp.wait_ge(sem("awo_split"), g + 1)
                    sp.dma_start(awo_raw[:], a_wo[bass.ds(g * P + P, P), :]).then_inc(sem("awo_loaded"), 16)
                if not (last and j >= A_GROUP - 2):
                    h2 = g * A_GROUP + j + 2
                    sp.wait_ge(sem("aw_split"), h2 - 1)
                    sp.dma_start(aw_raw[:, j % 2], a_heads[bass.ds(h2 * P, P), :]).then_inc(sem(f"aw_loaded{j % 2}"), 16)

        EACH_CHUNK, EACH_LOAD = CHUNKS * F_TILES, 16 * (F_TILES // 2)
        F_TOTAL = dict(rw=1, rw_hi=1, rw_loaded=16, w_loaded0=EACH_LOAD, w_loaded1=EACH_LOAD, gu_hi=F_TILES, gu_split=F_TILES,
                       d_hi=F_TILES, d_split=F_TILES, gate_logits=CHUNKS, gate=CHUNKS, logits=CHUNKS, lgT=CHUNKS, lg_T=1, lg=1,
                       shift=1, exp=1, keep=2, dve_step=11, coef=1, coefT=1, coef_ready=1, up_done=EACH_CHUNK,
                       silu=EACH_CHUNK, sc=EACH_CHUNK, h=EACH_CHUNK, h_hi=EACH_CHUNK, h_split=EACH_CHUNK,
                       down_done=F_TILES + CHUNKS)

        def f_count(f, name, count):
            return count + f * F_TOTAL[name]

        def f_pe(pe, n, f):
            pe.wait_ge(sem("f_rw"), f_count(f, "rw", 1))
            for c in range(CHUNKS):
                normed(pe, n, c)
                f_logits_pe(pe, 0, c).then_inc(sem("f_gate_logits"), 1)
                f_up_pe(pe, f, 0, 0, [c])
            for c in range(CHUNKS):
                f_logits_pe(pe, 1, c).then_inc(sem("f_logits"), 1)
            f_up_pe(pe, f, 1, 1)
            for c in range(CHUNKS):
                pe.wait_ge(sem("f_lgT"), f_count(f, "lgT", c + 1))
                for i in range(CHUNK_BLOCKS):
                    b = c * CHUNK_BLOCKS + i
                    if b == 0:
                        pe.wait_ge(sem("f_lgT"), f_count(f, "lgT", CHUNKS))
                    ins = nc.tensor.transpose(ps[:, 6, b * LOGITS:(b + 1) * LOGITS], lgT[0:LOGITS, b * P:(b + 1) * P],
                                              ident[0:LOGITS, 0:LOGITS])
            ins.then_inc(sem("f_lg_T"), 1)
            pe.wait_ge(sem("f_gate"), f_count(f, "gate", CHUNKS))
            pe.wait_ge(sem("f_lg"), f_count(f, "lg", 1))
            for a in range(4):
                ins = nc.tensor.matmul(ps[:, 4 + a, :], zero_w[:], zero_x[:], start=True, stop=False, skip_group_check=True)
            ins.then_inc(sem("f_down_done"), 1)
            for i in range(S_TILES - 2):
                f_down_pe(pe, f, i, i % 2)
                f_up_pe(pe, f, i + 2, i % 2)
            f_down_pe(pe, f, S_TILES - 2, 0)
            pe.wait_ge(sem("f_coef"), f_count(f, "coef", 1))
            pe.wait_ge(sem("f_silu"), f_count(f, "silu", CHUNKS * S_TILES))
            for i in range(BLOCKS):
                ins = nc.tensor.transpose(ps[:, i // 4, (i % 4) * P:(i % 4 + 1) * P],
                                          cexp[:, i].rearrange("p e r -> p (e r)"), ident)
            ins.then_inc(sem("f_coefT"), 1)
            f_down_pe(pe, f, S_TILES - 1, 1)
            pe.wait_ge(sem("f_coef_ready"), f_count(f, "coef_ready", 1))
            f_up_pe(pe, f, S_TILES, 0)
            with pe.Fori(S_TILES // 2, F_TILES // 2 - 1) as i2:
                for p in range(2):
                    f_up_pe(pe, f, 2 * i2 + p + 1, 1 - p)
                    f_down_pe(pe, f, 2 * i2 + p, p)
            f_up_pe(pe, f, F_TILES - 1, 1)
            f_down_pe(pe, f, F_TILES - 2, 0)
            f_down_pe(pe, f, F_TILES - 1, 1, True)

        def f_logits_pe(pe, s, c):
            for k in range(KT):
                ins = mm3(ps[:, 4 + 2 * s + c, :], at(rw, slice(None), k, s), at(xn, slice(None), k, cols(c)), k == 0, k == KT - 1)
            return ins

        def f_up_pe(pe, f, i, p, chunks=range(CHUNKS)):
            pe.wait_ge(sem("f_gu_split"), f_count(f, "gu_split", i + 1))
            for c in chunks:
                if not (isinstance(i, int) and i == 0):
                    pe.wait_ge(sem("f_h"), f_count(f, "h", 2 * i + c - 1))
                for s in range(2):
                    for k in range(KT):
                        ins = mm3(ps[:, 2 * s + c, :], at(fgu, slice(None), p, k, s), at(xn, slice(None), k, cols(c)),
                                  k == 0, k == KT - 1)
                ins.then_inc(sem("f_up_done"), 1)

        def f_down_pe(pe, f, i, p, last=False):
            pe.wait_ge(sem("f_d_split"), f_count(f, "d_split", i + 1))
            for c in range(CHUNKS):
                pe.wait_ge(sem("f_h_split"), f_count(f, "h_split", 2 * i + c + 1))
                for m in range(KT):
                    ins = mm3(ps[:, 4 + 2 * c + m, :], at(fd, slice(None), p, slice(m * P, (m + 1) * P)),
                              at(fh, slice(None), p, cols(c)), False, False)
                if last or c == CHUNKS - 1:
                    ins.then_inc(sem("f_down_done"), 1)

        def f_act(act, n, f):
            for c in range(CHUNKS):
                act.wait_ge(sem("f_gate_logits"), f_count(f, "gate_logits", c + 1))
                nc.scalar.activation(coef_s[:, cols(c)], ps[:, 4 + c, :], ACT.Sigmoid).then_inc(sem("f_gate"), 1)
            for i in range(S_TILES):
                f_hidden_act(act, f, i, i % 2, True, True)
                if i == 1:
                    act.wait_ge(sem("f_shift"), f_count(f, "shift", 1))
                    nc.scalar.activation(pr[:], pr[:], ACT.Exp).then_inc(sem("f_exp"), 1)
            act.wait_ge(sem("f_coefT"), f_count(f, "coefT", 1))
            nc.scalar.copy(coef_r[:].rearrange("p (a n) -> p a n", a=2), ps[:, 0:2, :]).then_inc(sem("f_coef_ready"), 1)
            with act.Fori(S_TILES // 2, F_TILES // 2 - 1) as i2:
                for p in range(2):
                    f_hidden_act(act, f, 2 * i2 + p, p, True, True)
            f_hidden_act(act, f, F_TILES - 2, 0, False, True)
            f_hidden_act(act, f, F_TILES - 1, 1, False, False)

        def f_prepare_act(act, f):
            act.wait_ge(sem("f_rw_loaded"), f_count(f, "rw_loaded", 16))
            split_hi(at(rw, slice(None)), rw_raw[:], "f_rw_hi")
            f_prepare_gu_act(act, f, 0)

        def f_prepare_rest_act(act, f):
            f_prepare_gu_act(act, f, 1)
            split_hi(at(fd, slice(None), 0), raw_d(0), "f_d_hi")

        def f_prepare_gu_act(act, f, p):
            act.wait_ge(sem(f"f_w_loaded{p}"), f_count(f, f"w_loaded{p}", 16))
            split_hi(at(fgu, slice(None), p), raw_gu(p), "f_gu_hi")

        def f_hidden_act(act, f, i, p, more_gu, more_d):
            for c in range(CHUNKS):
                act.wait_ge(sem("f_up_done"), f_count(f, "up_done", 2 * i + c + 1))
                nc.scalar.activation(f_s[:, c], ps[:, c, :], ACT.Silu).then_inc(sem("f_silu"), 1)
            for c in range(CHUNKS):
                act.wait_ge(sem("f_h"), f_count(f, "h", 2 * i + c + 1))
                split_hi(at(fh, slice(None), p, cols(c)), f_h[:, c], "f_h_hi")
            if more_d:
                act.wait_ge(sem("f_down_done"), f_count(f, "down_done", i + 1))
                split_hi(at(fd, slice(None), 1 - p), raw_d(1 - p), "f_d_hi")
            if more_gu:
                act.wait_ge(sem(f"f_w_loaded{p}"), f_count(f, f"w_loaded{p}", 8 * i + 32 - 8 * p))
                split_hi(at(fgu, slice(None), p), raw_gu(p), "f_gu_hi")

        def raw_gu(p):
            return fw_raw[:, p, 0:KT * 2 * P].rearrange("p (k s m) -> p k s m", k=KT, s=2)

        def raw_d(p):
            return fw_raw[:, p, KT * 2 * P:]

        def f_pool(pool, n, f):
            split_lo(pool, at(rw, slice(None)), rw_raw[:], "f_rw_hi", f_count(f, "rw_hi", 1), "f_rw")
            for p in range(2):
                f_split_gu_pool(pool, f, p, p)
            f_split_d_pool(pool, f, 0, 0)
            pool.wait_ge(sem("f_gate"), f_count(f, "gate", CHUNKS))
            for i in range(S_TILES):
                f_hidden_pool(pool, f, i, i % 2, coef_s, True, True)
            pool.wait_ge(sem("f_coef_ready"), f_count(f, "coef_ready", 1))
            with pool.Fori(S_TILES // 2, F_TILES // 2 - 1) as i2:
                for p in range(2):
                    f_hidden_pool(pool, f, 2 * i2 + p, p, coef_r, True, True)
            f_hidden_pool(pool, f, F_TILES - 2, 0, coef_r, False, True)
            f_hidden_pool(pool, f, F_TILES - 1, 1, coef_r, False, False)

        def f_split_gu_pool(pool, f, i, p):
            split_lo(pool, at(fgu, slice(None), p), raw_gu(p), "f_gu_hi", f_count(f, "gu_hi", i + 1), "f_gu_split")

        def f_split_d_pool(pool, f, i, p):
            split_lo(pool, at(fd, slice(None), p), raw_d(p), "f_d_hi", f_count(f, "d_hi", i + 1), "f_d_split")

        def f_hidden_pool(pool, f, i, p, coef, more_gu, more_d):
            for c in range(CHUNKS):
                pool.wait_ge(sem("f_silu"), f_count(f, "silu", 2 * i + c + 1))
                nc.gpsimd.tensor_tensor(f_sc[:, c], f_s[:, c], coef[:, cols(c)], ALU.mult).then_inc(sem("f_sc"), 1)
            if more_d:
                f_split_d_pool(pool, f, i + 1, 1 - p)
            if more_gu:
                f_split_gu_pool(pool, f, i + 2, p)

        def f_dve(dve, n, f):
            step = counter(dve, "f_dve_step", f_count(f, "dve_step", 0))
            nc.vector.memset(r_keep[:], 1.0).then_inc(sem("f_keep"), 1)
            dve.wait_ge(sem("f_keep"), f_count(f, "keep", 1))
            nc.vector.memset(r_keep[:, :, 0], 0.0).then_inc(sem("f_keep"), 1)
            for i in range(S_TILES):
                f_hidden_dve(dve, f, i, i % 2)
                if i == 0:
                    for c in range(CHUNKS):
                        dve.wait_ge(sem("f_logits"), f_count(f, "logits", c + 1))
                        nc.vector.tensor_copy(lgT[0:LOGITS, cols(c)], ps[0:LOGITS, 6 + c, :]).then_inc(sem("f_lgT"), 1)
                    dve.wait_ge(sem("f_lg_T"), f_count(f, "lg_T", 1))
                    nc.vector.tensor_copy(lg[:], ps[:, 6, 0:BLOCKS * LOGITS].rearrange("p (i e) -> p i e", e=LOGITS)
                                          ).then_inc(sem("f_lg"), 1)
                    dve.wait_ge(sem("f_lg"), f_count(f, "lg", 1))
                    step(nc.vector.tensor_reduce(r_mx[:], lg[:, :, 0:EXPERTS], AX_X, ALU.max))
                    nc.vector.tensor_tensor(pr[:], lg[:, :, 0:EXPERTS], r_mx[:, :, None].broadcast_to(R_WIDE),
                                            ALU.subtract).then_inc(sem("f_shift"), 1)
                if i == 2:
                    f_route_dve(dve, f, step)
            with dve.Fori(S_TILES // 2, F_TILES // 2) as i2:
                for p in range(2):
                    f_hidden_dve(dve, f, 2 * i2 + p, p)
            for c in range(CHUNKS):
                dve.wait_ge(sem("f_down_done"), f_count(f, "down_done", F_TILES + 1 + c))
                for m in range(KT):
                    nc.vector.tensor_tensor(x[:, m, cols(c)], x[:, m, cols(c)], ps[:, 4 + 2 * c + m, :],
                                            ALU.add).then_inc(sem(f"x_updated{n + 1}"), 1)

        R_WIDE = [P, BLOCKS, EXPERTS]

        def f_route_dve(dve, f, step):
            dve.wait_ge(sem("f_exp"), f_count(f, "exp", 1))
            dve.wait_ge(sem("f_keep"), f_count(f, "keep", 2))
            step(nc.vector.tensor_reduce(r_sum[:], pr[:], AX_X, ALU.add))
            step(nc.vector.reciprocal(r_sum[:], r_sum[:]))
            step(nc.vector.tensor_tensor(pr[:], pr[:], r_sum[:, :, None].broadcast_to(R_WIDE), ALU.mult))
            for b in range(BLOCKS):
                ins = nc.vector.max(out=r_top[:, b], in_=pr[:, b])
            step(ins)
            least = r_top[:, :, TOP_K - 1:TOP_K].broadcast_to(R_WIDE)
            nc.vector.tensor_tensor(r_gt[:], pr[:], least, ALU.is_gt)
            step(nc.vector.tensor_tensor(r_eq[:], pr[:], least, ALU.is_equal))
            nc.vector.tensor_reduce(r_cnt[:], r_gt[:], AX_X, ALU.add)
            step(nc.vector.tensor_tensor_scan(flat(r_before), flat(r_keep), flat(r_eq), 0.0, ALU.mult, ALU.add))
            step(nc.vector.tensor_tensor(r_before[:], r_before[:], r_cnt[:, :, None].broadcast_to(R_WIDE), ALU.add))
            step(nc.vector.scalar_tensor_tensor(r_eq[:], r_before[:], TOP_K + 0.5, r_eq[:], ALU.is_lt, ALU.mult))
            step(nc.vector.tensor_tensor(r_gt[:], r_gt[:], r_eq[:], ALU.add))
            step(nc.vector.tensor_tensor(pr[:], pr[:], r_gt[:], ALU.mult))
            nc.vector.tensor_copy(cexp[:], pr[:, :, :, None].broadcast_to([P, BLOCKS, EXPERTS, ROWS_E])).then_inc(sem("f_coef"), 1)

        def flat(t):
            return t[:].rearrange("p i e -> p (i e)")

        def f_hidden_dve(dve, f, i, p):
            for c in range(CHUNKS):
                dve.wait_ge(sem("f_sc"), f_count(f, "sc", 2 * i + c + 1))
                nc.vector.tensor_tensor(f_h[:, c], f_sc[:, c], ps[:, 2 + c, :], ALU.mult).then_inc(sem("f_h"), 1)
                dve.wait_ge(sem("f_h_hi"), f_count(f, "h_hi", 2 * i + c + 1))
                nc.vector.tensor_tensor(fh[1][:, p, cols(c)], f_h[:, c], f32(fh[0][:, p, cols(c)]),
                                        ALU.subtract).then_inc(sem("f_h_split"), 1)

        def f_sp(sp, n, f):
            x_final(sp, n, CHUNKS - 1)
            sp.dma_start(rw_raw[:], router_w).then_inc(sem("f_rw_loaded"), 16)
            for p in range(2):
                sp.dma_start(fw_raw[:, p], ffn_w[p * P:(p + 1) * P, :]).then_inc(sem(f"f_w_loaded{p}"), 16)
            with sp.Fori(0, F_TILES // 2 - 1) as i2:
                for p in range(2):
                    sp.wait_ge(sem("f_d_split"), f_count(f, "d_split", 2 * i2 + p + 1))
                    sp.dma_start(fw_raw[:, p], ffn_w[bass.ds(i2 * (2 * P) + (2 + p) * P, P), :]).then_inc(sem(f"f_w_loaded{p}"), 16)

        def b_pe(pe):
            pe.wait_ge(sem("b_bg_w"), 1)
            for c in range(CHUNKS):
                normed(pe, 2, c)
                for s in range(2):
                    for k in range(KT):
                        ins = mm3(ps[:, 2 * s + c, :], at(wbg, slice(None), k, s), at(xn, slice(None), k, cols(c)),
                                  k == 0, k == KT - 1)
                ins.then_inc(sem("b_bg_done"), 1)
            pe.wait_ge(sem("b_bg_read"), 2)
            b_make_pe(pe, 0, 0, range(4))
            pe.wait_ge(sem("b_cum"), 1)
            for i in range(BLOCKS):
                ins = nc.tensor.transpose(ps[:, 2, i * 32:(i + 1) * 32], dec_b[2][0:32, i * P:(i + 1) * P], ident[0:32, 0:32])
            ins.then_inc(sem("b_cumT"), 1)
            pe.wait_ge(sem("b_ncum"), 1)
            pe.wait_ge(sem("b_pieces"), 6)
            with pe.Fori(0, B_HEADS // 2 - 1) as h2:
                b_head_pe(pe, 2 * h2, 0, False)
                b_head_pe(pe, 2 * h2 + 1, 1, False)
            b_head_pe(pe, B_HEADS - 2, 0, False)
            b_head_pe(pe, B_HEADS - 1, 1, True)

        def b_bank(pe, h, slot):
            before = slot - 2
            if before < 0:
                if not (isinstance(h, int) and h == 0):
                    pe.wait_ge(sem("b_silu"), 4 * h)
                    pe.wait_ge(sem("x_updated3"), 4 * h - 1 + slot)
            elif before < 4:
                pe.wait_ge(sem("qpad_split"), 4 * h + before + 1)
            elif before < 8:
                pe.wait_ge(sem("v_split"), 4 * h + before - 3)
            else:
                pe.wait_ge(sem("b_silu"), 4 * h + before - 7)
            return ps[:, slot % 2, :]

        def b_make_pe(pe, h, p, parts):
            for part in parts:
                if part == 0:
                    pe.wait_ge(sem("wqk_split"), h + 1)
                    for s in range(2):
                        for c in range(CHUNKS):
                            o = b_bank(pe, h, 2 * s + c)
                            for k in range(KT):
                                ins = mm3(o, at(wqk, slice(None), k, s), at(xn, slice(None), k, cols(c)), k == 0, k == KT - 1)
                            ins.then_inc(sem("b_proj_done"), 1)
                elif part == 1:
                    pe.wait_ge(sem("wv_split"), h + 1)
                    for i in range(BLOCKS // 2):
                        o = b_bank(pe, h, 4 + i)
                        for t in range(2):
                            tok = slice((2 * i + t) * P, (2 * i + t + 1) * P)
                            for k in range(KT):
                                ins = mm3(o[:, t * B_V:(t + 1) * B_V], at(xn, slice(None), k, tok), at(wv, slice(None), k),
                                          t == 0 and k == 0, t == 1 and k == KT - 1)
                        ins.then_inc(sem("b_v_done"), 1)
                else:
                    s = part - 2
                    if s == 0:
                        pe.wait_ge(sem("wconv_split"), h + 1)
                    pe.wait_ge(sem("qpad_split"), 4 * h + 2 * s + 2)
                    for c in range(CHUNKS):
                        o = b_bank(pe, h, 8 + 2 * s + c).rearrange("p (b l) -> p b l", l=SEQ)
                        for j in range(B_TAPS):
                            ins = mm3(o, at(wconv, slice(None), s, j),
                                      at(qpad, slice(None), s, slice(2 * c, 2 * c + 2), slice(j, j + SEQ)),
                                      j == 0, j == B_TAPS - 1)
                        ins.then_inc(sem("b_conv_done"), 1)

        def b_score_pe(pe, h, p, b):
            l0, u = b * SEQ, b % 2
            if b >= 2:
                pe.wait_ge(sem("b_m_done"), BATCH * h + b - 1)
            d, s = ps[:, 2 + u, :], ps[:, 4 + u, :]
            if b % 2 == 0:
                pe.wait_ge(sem("qk_split"), 4 * h + 3 + b // 2)
            lhs = rows_b[:, bass.ds(h, 1)].broadcast_to([P, P])
            nc.tensor.matmul(d[:, 0:TRI], lhs, pieces_b[:, b, :], start=True, stop=False, skip_group_check=True)
            nc.tensor.matmul(d[:, 0:2 * P], ident_b[:], mask_b[:].rearrange("p d n -> p (d n)"), start=False, stop=True, skip_group_check=True)
            mm3(first_m(s), at(qk[p], slice(None), 1, slice(l0, l0 + P)), halves(at(qk[p], slice(None), 0, slice(l0, l0 + SEQ))), True, False)
            mm3(s[:, P:2 * P], at(qk[p], slice(None), 1, slice(l0 + P, l0 + SEQ)),
                at(qk[p], slice(None), 0, slice(l0 + P, l0 + SEQ)), False).then_inc(sem("b_s_done"), 1)

        def b_value_pe(pe, h, p, b):
            u = b % 2
            pe.wait_ge(sem("b_m_split"), BATCH * h + b + 1)
            if b == 0:
                pe.wait_ge(sem("v_split"), 4 * h + 4)
            if b >= 2:
                pe.wait_ge(sem("o_split"), BATCH * h + b - 1)
            o, ms = ps[:, 6 + u, :], at(ms_b, slice(None), u)
            for d in range(B_VT):
                dv = slice(d * P, (d + 1) * P)
                mm3(half_view(o[:, d * SEQ:(d + 1) * SEQ]), at(vtok[p], slice(None), 2 * b, dv), tuple(first_m(v) for v in ms),
                    d == 0, False)
                ins = mm3(o[:, d * SEQ + P:(d + 1) * SEQ], at(vtok[p], slice(None), 2 * b + 1, dv),
                          at(ms, slice(None), slice(P, 2 * P)), False, d == B_VT - 1)
            ins.then_inc(sem("b_o_done"), 1)

        def b_head_pe(pe, h, p, last):
            make = (lambda parts: None) if last else (lambda parts: b_make_pe(pe, h + 1, 1 - p, parts))
            b_score_pe(pe, h, p, 0)
            make([0])
            b_score_pe(pe, h, p, 1)
            make([1])
            b_value_pe(pe, h, p, 0)
            b_score_pe(pe, h, p, 2)
            b_score_pe(pe, h, p, 3)
            b_value_pe(pe, h, p, 1)
            make([2, 3])
            b_value_pe(pe, h, p, 2)
            b_value_pe(pe, h, p, 3)
            pe.wait_ge(sem("wo_split"), h + 1)
            for c in range(CHUNKS):
                pe.wait_ge(sem("o_split"), BATCH * h + 2 * c + 2)
                for m in range(KT):
                    if c == 0 and not last:
                        pe.wait_ge(sem("b_silu"), 4 * h + 7 + m)
                    else:
                        pe.wait_ge(sem("x_updated3"), 4 * h + 2 * c + m + 3)
                    o = ps[:, m, :]
                    for d in range(B_VT):
                        ins = mm3(o, at(wo, slice(None), d, slice(m * P, (m + 1) * P)), at(oT, slice(None), d, cols(c)),
                                  d == 0, d == B_VT - 1)
                    ins.then_inc(sem("b_wo_done"), 1)

        def b_prepare_act(act):
            act.wait_ge(sem("wbg_loaded"), 16)
            split_hi(at(wbg, slice(None)), wbg_raw[:], "wbg_hi")
            b_weights_act(act, *B_WEIGHTS[0], 0)

        def b_prepare_rest_act(act):
            for name, w, raw in B_WEIGHTS[1:]:
                b_weights_act(act, name, w, raw, 0)

        def b_act(act):
            act.wait_ge(sem("b_params"), 16)
            act.wait_ge(sem("b_bg_done"), CHUNKS)
            for s in range(2):
                nc.scalar.activation(dec_b[s][:].rearrange("p (a n) -> p a n", a=2), ps[:, 2 * s:2 * s + 2, :], ACT.Identity,
                                     bias=bpar[:, s:s + 1]).then_inc(sem("b_bg_read"), 1)
            act.wait_ge(sem("qpad_zero"), 2)
            b_make_act(act, 0, 0, [0])
            for s in range(2):
                act.wait_ge(sem("b_abs"), s + 1)
                nc.scalar.activation(dec_b[2 + s][:], dec_b[2 + s][:], ACT.Exp, scale=-1.0).then_inc(sem("b_exp"), 1)
            for s in range(2):
                act.wait_ge(sem("b_exp"), s + 1)
                nc.scalar.activation(dec_b[2 + s][:], dec_b[2 + s][:], ACT.Ln, bias=1.0).then_inc(sem("b_ln"), 1)
            b_make_act(act, 0, 0, [1, 2])
            for name, w, raw in B_WEIGHTS[0:2]:
                b_weights_act(act, name, w, raw, 1)
            b_make_act(act, 0, 0, [3])
            b_weights_act(act, *B_WEIGHTS[2], 1)
            act.wait_ge(sem("b_cumT"), 1)
            nc.scalar.mul(ncum_b[:], ps[:, 2, 0:BLOCKS * 32].rearrange("p (i h) -> p i h", h=32), -1.0).then_inc(sem("b_ncum"), 1)
            act.wait_ge(sem("b_ncum"), 1)
            with act.Fori(0, B_HEADS // 2 - 1) as h2:
                b_head_act(act, 2 * h2, 0, False, True)
                b_head_act(act, 2 * h2 + 1, 1, False, True)
            b_head_act(act, B_HEADS - 2, 0, False, False)
            b_head_act(act, B_HEADS - 1, 1, True, False)

        def b_make_act(act, h, p, parts):
            for part in parts:
                if part == 0:
                    for s in range(2):
                        for c in range(CHUNKS):
                            act.wait_ge(sem("b_proj_done"), 4 * h + 2 * s + c + 1)
                            nc.scalar.copy(qpad[0][:, s, 2 * c:2 * c + 2, B_TAPS - 1:PADDED],
                                           ps[:, c, :].rearrange("p (b l) -> p b l", l=SEQ)).then_inc(sem("qpad_hi"), 1)
                elif part == 1:
                    for i in range(BLOCKS // 2):
                        act.wait_ge(sem("b_v_done"), 4 * h + i + 1)
                        nc.scalar.copy(vtok[p][0][:, 2 * i:2 * i + 2], ps[:, i % 2, :].rearrange("p (t v) -> p t v", t=2)
                                       ).then_inc(sem("v_hi"), 1)
                else:
                    s = part - 2
                    for c in range(CHUNKS):
                        act.wait_ge(sem("b_conv_done"), 4 * h + 2 * s + c + 1)
                        if not (isinstance(h, int) and h == 0 and s == 0):
                            act.wait_ge(sem("qk_split"), 4 * h + 2 * s + c - 1)
                        nc.scalar.activation(qf[:, c], ps[:, c, :], ACT.Silu, bias=conv_bias[:, s:s + 1]).then_inc(sem("b_silu"), 1)
                    for c in range(CHUNKS):
                        act.wait_ge(sem("b_silu"), 4 * h + 2 * s + c + 1)
                        split_hi(at(qk[p], slice(None), s, cols(c)), qf[:, c], "qk_hi")

        def b_weights_act(act, name, w, raw, h):
            act.wait_ge(sem(f"{name}_loaded"), 16 * h + 16)
            if name == "wconv":
                nc.scalar.copy(conv_bias[:], wconv_raw_all[:, CONVW:])
            split_hi(at(w, slice(None)), raw[:], f"{name}_hi")

        def b_split_act(act, h, b):
            act.wait_ge(sem("b_m_done"), BATCH * h + b + 1)
            if b >= 2:
                act.wait_ge(sem("b_o_done"), BATCH * h + b - 1)
            split_hi(at(ms_b, slice(None), b % 2), m_b[:, b % 2, :], "b_m_hi")

        def b_score_act(act, h, b):
            act.wait_ge(sem("b_s_done"), BATCH * h + b + 1)
            act.wait_ge(sem("b_ncum"), 1)
            d = ps[:, 2 + b % 2, :]
            nc.scalar.activation(first_m(e_b[:, b % 2]), first_m(d), ACT.Exp, bias=ncum_b[:, 2 * b, bass.ds(h, 1)])
            nc.scalar.activation(e_b[:, b % 2, P:2 * P], d[:, P:2 * P], ACT.Exp,
                                 bias=ncum_b[:, 2 * b + 1, bass.ds(h, 1)]).then_inc(sem("b_e_done"), 1)

        def b_value_act(act, h, b):
            act.wait_ge(sem("b_o_done"), BATCH * h + b + 1)
            nc.scalar.copy(oT[0][:, :, b * SEQ:(b + 1) * SEQ], ps[:, 6 + b % 2, :].rearrange("p (d l) -> p d l", d=B_VT)
                           ).then_inc(sem("o_hi"), 1)

        def b_head_act(act, h, p, last, weights):
            make = (lambda parts: None) if last else (lambda parts: b_make_act(act, h + 1, 1 - p, parts))
            b_score_act(act, h, 0)
            make([0])
            b_split_act(act, h, 0)
            b_score_act(act, h, 1)
            b_split_act(act, h, 1)
            make([1])
            b_weights_act(act, "wo", wo, wo_raw, h)
            b_value_act(act, h, 0)
            b_score_act(act, h, 2)
            b_split_act(act, h, 2)
            b_score_act(act, h, 3)
            b_value_act(act, h, 1)
            b_split_act(act, h, 3)
            if weights:
                b_weights_act(act, *B_WEIGHTS[0], h + 2)
                b_weights_act(act, *B_WEIGHTS[1], h + 2)
            make([2, 3])
            if weights:
                b_weights_act(act, *B_WEIGHTS[2], h + 2)
            b_value_act(act, h, 2)
            b_value_act(act, h, 3)

        def b_dve(dve):
            step = counter(dve, "b_dve_step")
            for s in range(2):
                nc.vector.memset(f32(qpad[s][:, :, :, 0:B_TAPS - 1]), 0.0).then_inc(sem("qpad_zero"), 1)
            nc.vector.memset(dec_b[4][:], 1.0).then_inc(sem("x_updated3"), 4)
            dve.wait_ge(sem("x_updated3"), 4)
            step(nc.vector.memset(dec_b[4][:, 0:TOKENS:SEQ], 0.0))
            step(nc.vector.memset(pieces_b[:], 0.0))
            dve.wait_ge(sem("b_bg_read"), 2)
            for s in range(2):
                nc.vector.scalar_tensor_tensor(dec_b[2 + s][:], dec_b[s][:], -1.0, dec_b[s][:], ALU.mult, ALU.max).then_inc(sem("b_abs"), 1)
            b_make_dve(dve, 0, 0, [0])
            for s in range(2):
                dve.wait_ge(sem("b_ln"), s + 1)
                step(nc.vector.scalar_tensor_tensor(dec_b[s][:], dec_b[s][:], 0.0, dec_b[2 + s][:], ALU.min, ALU.subtract))
            step(nc.vector.tensor_tensor_scan(dec_b[2][:], dec_b[4][:], dec_b[0][:], 0.0, ALU.mult, ALU.add))
            nc.vector.tensor_tensor(dec_b[1][:], dec_b[1][:], dec_b[2][:], ALU.add).then_inc(sem("b_cum"), 1)
            b_make_dve(dve, 0, 0, [1])
            dve.wait_ge(sem("b_cum"), 1)
            split_pieces(dve, step, pieces_b, dec_b[1], dec_b[4], dec_b[5], "b_pieces")
            b_make_dve(dve, 0, 0, range(2, 4))
            with dve.Fori(0, B_HEADS // 2 - 1) as h2:
                b_head_dve(dve, 2 * h2, 0, False)
                b_head_dve(dve, 2 * h2 + 1, 1, False)
            b_head_dve(dve, B_HEADS - 2, 0, False)
            b_head_dve(dve, B_HEADS - 1, 1, True)

        def b_make_dve(dve, h, p, parts):
            for part in parts:
                if part == 0:
                    for s in range(2):
                        for c in range(CHUNKS):
                            dve.wait_ge(sem("qpad_hi"), 4 * h + 2 * s + c + 1)
                            at_ = (slice(None), s, slice(2 * c, 2 * c + 2), slice(B_TAPS - 1, PADDED))
                            nc.vector.tensor_tensor(qpad[1][at_], ps[:, c, :].rearrange("p (b l) -> p b l", l=SEQ),
                                                    f32(qpad[0][at_]), ALU.subtract
                                                    ).then_inc(sem("qpad_split"), 1)
                elif part == 1:
                    for i in range(BLOCKS // 2):
                        dve.wait_ge(sem("v_hi"), 4 * h + i + 1)
                        at_ = (slice(None), slice(2 * i, 2 * i + 2))
                        nc.vector.tensor_tensor(vtok[p][1][at_], ps[:, i % 2, :].rearrange("p (t v) -> p t v", t=2),
                                                f32(vtok[p][0][at_]), ALU.subtract
                                                ).then_inc(sem("v_split"), 1)

        def b_score_dve(dve, h, b):
            dve.wait_ge(sem("b_e_done"), BATCH * h + b + 1)
            if b >= 2:
                dve.wait_ge(sem("b_m_split"), BATCH * h + b - 1)
            nc.vector.tensor_tensor(m_b[:, b % 2, :], ps[:, 4 + b % 2, 0:TRI], e_b[:, b % 2, :],
                                    ALU.mult).then_inc(sem("b_m_done"), 1)

        def b_value_dve(dve, h, b):
            dve.wait_ge(sem("o_hi"), BATCH * h + b + 1)
            at_ = (slice(None), slice(None), slice(b * SEQ, (b + 1) * SEQ))
            nc.vector.tensor_tensor(oT[1][at_], ps[:, 6 + b % 2, :].rearrange("p (d l) -> p d l", d=B_VT),
                                    f32(oT[0][at_]), ALU.subtract).then_inc(sem("o_split"), 1)

        def b_head_dve(dve, h, p, last):
            make = (lambda parts: None) if last else (lambda parts: b_make_dve(dve, h + 1, 1 - p, parts))
            b_score_dve(dve, h, 0)
            make([0])
            b_score_dve(dve, h, 1)
            make([1])
            b_value_dve(dve, h, 0)
            b_score_dve(dve, h, 2)
            b_score_dve(dve, h, 3)
            b_value_dve(dve, h, 1)
            b_value_dve(dve, h, 2)
            b_value_dve(dve, h, 3)
            for c in range(CHUNKS):
                for m in range(KT):
                    dve.wait_ge(sem("b_wo_done"), 4 * h + 2 * c + m + 1)
                    nc.vector.tensor_tensor(x[:, m, cols(c)], x[:, m, cols(c)], ps[:, m, :],
                                            ALU.add).then_inc(sem("x_updated3"), 1)

        def b_pool(pool):
            split_lo(pool, at(wbg, slice(None)), wbg_raw[:], "wbg_hi", 1, "b_bg_w")
            for name, w, raw in B_WEIGHTS:
                b_weights_pool(pool, name, w, raw, 0)
            b_conv_pool(pool, 0, 0, 0)
            for name, w, raw in B_WEIGHTS[0:2]:
                b_weights_pool(pool, name, w, raw, 1)
            b_conv_pool(pool, 0, 0, 1)
            b_weights_pool(pool, *B_WEIGHTS[2], 1)
            with pool.Fori(0, B_HEADS // 2 - 1) as h2:
                b_head_pool(pool, 2 * h2, 0, True, True)
                b_head_pool(pool, 2 * h2 + 1, 1, True, True)
            b_head_pool(pool, B_HEADS - 2, 0, True, False)
            b_head_pool(pool, B_HEADS - 1, 1, False, False)

        def b_weights_pool(pool, name, w, raw, h):
            split_lo(pool, at(w, slice(None)), raw[:], f"{name}_hi", h + 1, f"{name}_split")

        def b_conv_pool(pool, h, p, s):
            for c in range(CHUNKS):
                split_lo(pool, at(qk[p], slice(None), s, cols(c)), qf[:, c], "qk_hi", 4 * h + 2 * s + c + 1, "qk_split")

        def b_score_pool(pool, h, b):
            split_lo(pool, at(ms_b, slice(None), b % 2), m_b[:, b % 2, :], "b_m_hi", BATCH * h + b + 1, "b_m_split")

        def b_head_pool(pool, h, p, make, weights):
            b_score_pool(pool, h, 0)
            b_score_pool(pool, h, 1)
            b_weights_pool(pool, "wo", wo, wo_raw, h)
            b_score_pool(pool, h, 2)
            b_score_pool(pool, h, 3)
            if weights:
                b_weights_pool(pool, *B_WEIGHTS[0], h + 2)
                b_weights_pool(pool, *B_WEIGHTS[1], h + 2)
            if make:
                b_conv_pool(pool, h + 1, 1 - p, 0)
                b_conv_pool(pool, h + 1, 1 - p, 1)
            if weights:
                b_weights_pool(pool, *B_WEIGHTS[2], h + 2)

        B_WEIGHTS = (("wqk", wqk, wqk_raw), ("wv", wv, wv_raw), ("wconv", wconv, wconv_raw))
        B_PARTS = (("wqk", wqk_raw, b_qk), ("wv", wv_raw, b_v), ("wconv", wconv_raw_all, b_conv))

        def b_sp(sp):
            x_final(sp, 2, CHUNKS - 1)
            sp.dma_start(bpar[:], b_par).then_inc(sem("b_params"), 16)
            sp.dma_start(wbg_raw[:], b_bg).then_inc(sem("wbg_loaded"), 16)
            for name, raw, src in B_PARTS:
                sp.dma_start(raw[:], src[0:P, :]).then_inc(sem(f"{name}_loaded"), 16)
            sp.dma_start(wo_raw[:], b_wo[0:P, :]).then_inc(sem("wo_loaded"), 16)
            for name, raw, src in B_PARTS:
                sp.wait_ge(sem(f"{name}_split"), 1)
                sp.dma_start(raw[:], src[P:2 * P, :]).then_inc(sem(f"{name}_loaded"), 16)
            with sp.Fori(0, B_HEADS - 2) as h:
                sp.wait_ge(sem("wo_split"), h + 1)
                sp.dma_start(wo_raw[:], b_wo[bass.ds(h * P + P, P), :]).then_inc(sem("wo_loaded"), 16)
                for name, raw, src in B_PARTS:
                    sp.wait_ge(sem(f"{name}_split"), h + 2)
                    sp.dma_start(raw[:], src[bass.ds(h * P + 2 * P, P), :]).then_inc(sem(f"{name}_loaded"), 16)
            sp.wait_ge(sem("wo_split"), B_HEADS - 1)
            sp.dma_start(wo_raw[:], b_wo[(B_HEADS - 1) * P:B_HEADS * P, :]).then_inc(sem("wo_loaded"), 16)

        block = ctx.enter_context(nc.Block())

        @block.sync
        def _(sp):
            for c in range(CHUNKS):
                sp.dma_start(x[:, :, cols(c)], xT[:, :, cols(c)]).then_inc(sem(f"x_loaded{c}"), 16)
            sp.dma_start(const[:], consts).then_inc(sem("consts_loaded"), 16)
            a_sp(sp)
            f_sp(sp, 1, 0)
            b_sp(sp)
            f_sp(sp, 3, 1)
            x_final(sp, 4, CHUNKS - 1)
            sp.dma_start(out, x[:]).then_inc(sem("out_stored"), 16)
            sp.wait_ge(sem("out_stored"), 16)

        @block.gpsimd
        def _(pool):
            a_pool(pool)
            f_pool(pool, 1, 0)
            b_pool(pool)
            f_pool(pool, 3, 1)

        @block.scalar
        def _(act):
            norm_act(act, 0, a_prepare_act, a_prepare_rest_act)
            a_act(act)
            norm_act(act, 1, lambda act: f_prepare_act(act, 0), lambda act: f_prepare_rest_act(act, 0))
            f_act(act, 1, 0)
            norm_act(act, 2, b_prepare_act, b_prepare_rest_act)
            b_act(act)
            norm_act(act, 3, lambda act: f_prepare_act(act, 1), lambda act: f_prepare_rest_act(act, 1))
            f_act(act, 3, 1)

        @block.vector
        def _(dve):
            nc.vector.memset(mean_w[:], 1.0 / DM).then_inc(sem("mean_made"), 1)
            a_early_dve(dve)
            dve.wait_ge(sem("consts_loaded"), 16)
            nc.vector.memset(zero_w[:], 0.0)
            nc.vector.memset(zero_x[:], 0.0)
            nc.vector.tensor_copy(ident_b[:], const[:, 0:P])
            for d in range(2):
                nc.vector.tensor_copy(mask_b[:, d], const[:, P:2 * P])
            nc.vector.tensor_copy(rows_b[:], const[:, 2 * P:2 * P + 32])
            norm_dve(dve, 0)
            a_dve(dve)
            norm_dve(dve, 1)
            f_dve(dve, 1, 0)
            norm_dve(dve, 2)
            b_dve(dve)
            norm_dve(dve, 3)
            f_dve(dve, 3, 1)

        @block.tensor
        def _(pe):
            norm_pe(pe, 0)
            a_pe(pe)
            norm_pe(pe, 1)
            f_pe(pe, 1, 0)
            norm_pe(pe, 2)
            b_pe(pe)
            norm_pe(pe, 3)
            f_pe(pe, 3, 1)


def _constants():
    i = np.arange(P)
    c = np.zeros((P, N_CONST), np.float32)
    c[:, 0:P] = np.eye(P)
    c[:, P:2 * P] = np.where(i[None, :] >= i[:, None], 0.0, MASKED)
    c[:, 2 * P:2 * P + 32] = (i[:, None] % 32 == np.arange(32)[None, :]) & (i[:, None] < 96)
    return c


def _feature_major(w):
    return w.T.reshape(KT, P, w.shape[0]).transpose(1, 0, 2)


def _layout(i):
    c = np.ascontiguousarray
    i = {k: np.asarray(v) for k, v in i.items()}
    w = i["L0_attn_a_W_in"]
    hn = A_HEADS * A_STATE
    bc = w[2 * A_INNER:2 * A_INNER + 2 * hn].reshape(2, A_HEADS, A_STATE, KT, P)
    vg = w[:2 * A_INNER].reshape(2, A_TILES, P, KT, P)
    par = [i["L0_attn_a_conv_w"].reshape(A_TILES, P, A_TAPS).transpose(1, 0, 2).reshape(P, -1),
           i["L0_attn_a_conv_b"].reshape(A_TILES, P).T, i["L0_attn_a_D_param"].reshape(A_TILES, P).T,
           np.tile(i["L0_attn_a_A_log"], 4)[:, None], np.tile(i["L0_attn_a_dt_bias"], 4)[:, None]]
    a_wo = np.zeros((A_TILES + 1, P, DM), np.float32)
    a_wo[1:] = i["L0_attn_a_W_out"].T.reshape(A_TILES, P, DM)

    gu = np.zeros((F_TILES, 2, P, DM), np.float32)
    dn = np.zeros((F_TILES, P, DM), np.float32)
    sg = i["L0_ffn_shared_gate_up_w"].reshape(2, S_HIDDEN, DM)
    sd = i["L0_ffn_shared_down_w"].T
    for t in range(S_TILES):
        n = min(P, S_HIDDEN - t * P)
        gu[t, :, :n] = sg[:, t * P:t * P + n]
        dn[t, :n] = sd[t * P:t * P + n]
    gu[S_TILES:] = i["L0_ffn_w13"].reshape(EXPERTS, 2, R_TILES, ROWS_E, DM).transpose(2, 1, 0, 3, 4).reshape(R_TILES, 2, P, DM)
    dn[S_TILES:] = i["L0_ffn_w2"].reshape(EXPERTS, DM, R_TILES, ROWS_E).transpose(2, 0, 3, 1).reshape(R_TILES, P, DM)
    gu = gu.reshape(F_TILES, 2, P, KT, P).transpose(0, 4, 3, 1, 2).reshape(F_TILES, P, KT * 2 * P)
    rw = np.zeros((2, P, DM), np.float32)
    rw[0] = i["L0_ffn_sgate_w"]
    rw[1, :EXPERTS] = i["L0_ffn_gate_w"]

    qk = np.stack([i["L0_attn_b_Wq"], i["L0_attn_b_Wk"]]).reshape(2, B_HEADS, B_KD, KT, P)
    v = i["L0_attn_b_Wv"].reshape(B_HEADS, B_V, KT, P)
    cv = np.stack([i["L0_attn_b_Wq_conv"], i["L0_attn_b_Wk_conv"]]).reshape(2, B_HEADS, B_KD, P, B_TAPS)
    cb = np.stack([i["L0_attn_b_bq_conv"], i["L0_attn_b_bk_conv"]], axis=1)
    wo = i["L0_attn_b_Wo"].reshape(DM, B_HEADS, B_VT, P)
    reps = P // B_HEADS
    bg = np.stack([np.tile(i["L0_attn_b_Wb"], (reps, 1)), np.tile(i["L0_attn_b_Wg"], (reps, 1))])
    bpar = [np.tile(i["L0_attn_b_bb"], reps)[:, None], np.tile(i["L0_attn_b_bg"], reps)[:, None]]
    return dict(
        xT=c(i["L0_attn_a_x"].reshape(TOKENS, KT, P).transpose(2, 1, 0)),
        consts=_constants(),
        a_vg=c(vg.transpose(4, 1, 3, 0, 2)),
        a_dt=c(_feature_major(np.tile(w[2 * A_INNER + 2 * hn:], (4, 1)))),
        a_heads=c(bc.transpose(1, 4, 3, 0, 2)).reshape(A_HEADS * P, KT * 2 * P),
        a_wo=a_wo.reshape(-1, DM),
        a_par=c(np.concatenate(par, axis=1)),
        ffn_w=c(np.concatenate([gu, dn], axis=2)).reshape(F_TILES * P, KT * 2 * P + DM),
        router_w=c(rw.reshape(2, P, KT, P).transpose(3, 2, 0, 1)),
        b_qk=c(qk.transpose(1, 4, 3, 0, 2)).reshape(B_HEADS * P, QKW),
        b_v=c(v.transpose(0, 3, 2, 1)).reshape(B_HEADS * P, VW),
        b_conv=c(np.concatenate([cv.transpose(1, 3, 0, 4, 2).reshape(B_HEADS * P, CONVW), cb], axis=1)),
        b_wo=c(wo.transpose(1, 3, 2, 0)).reshape(B_HEADS * P, WOW),
        b_bg=c(bg.reshape(2, P, KT, P).transpose(3, 2, 0, 1)),
        b_par=c(np.concatenate(bpar, axis=1)),
    )


def kernel(**inputs):
    import concourse.bacc as bacc
    from concourse.bass_utils import run_bass_kernel_spmd

    arrays = _layout(inputs)
    nc = bacc.Bacc("TRN2", target_bir_lowering=False, num_devices=1)
    args = [nc.dram_tensor(k, a.shape, F32, kind="ExternalInput").ap() for k, a in arrays.items()]
    out = nc.dram_tensor("out", (P, KT, TOKENS), F32, kind="ExternalOutput").ap()
    build_layer(nc, *args, out)
    result = run_bass_kernel_spmd(nc, [arrays], core_ids=[0]).results[0]["out"]
    return np.ascontiguousarray(result.transpose(2, 1, 0)).reshape(BATCH, SEQ, DM)
```

```python
from contextlib import ExitStack

import numpy as np

import concourse.bass as bass
from concourse import mybir

F32 = mybir.dt.float32
FR = mybir.dt.float32r
BF16 = mybir.dt.bfloat16
ALU = mybir.AluOpType
ACT = mybir.ActivationFunctionType
AX_X = mybir.AxisListType.X

P = 128
BATCH, SEQ, DM = 4, 256, 256
TOKENS = BATCH * SEQ
KT = DM // P
CHUNK = 512
CHUNKS = TOKENS // CHUNK
BLOCKS = TOKENS // P
EPS = 1e-5
MASKED = -1e30
BOUND = 80.0

A_HEADS, A_STATE, A_HD, A_TAPS = 32, 128, 16, 4
A_INNER = A_HEADS * A_HD
A_TILES = A_INNER // P
A_GROUP = P // A_HD
UNITS = A_GROUP * BATCH
OUT_UNITS = (8, 10, 12, 14)
PADDED = SEQ + A_TAPS - 1

B_HEADS, B_KD, B_V, B_TAPS = 16, 128, 256, 4
B_VT = B_V // P
PAIRS = SEQ // 2
PLANE = PAIRS + 4

EXPERTS, TOP_K, E_HIDDEN, S_HIDDEN = 16, 4, 176, 704
ROWS_E = P // EXPERTS
R_TILES = E_HIDDEN // ROWS_E
S_TILES = -(-S_HIDDEN // P)
F_TILES = S_TILES + R_TILES
LOGITS = 32

QKW, VOW, CONVW = KT * 2 * P, 2 * B_VT * DM, 2 * B_TAPS * P
TRI = 3 * P

N_CONST = 3 * P + 32
N_APAR = A_TILES * (A_TAPS + 2) + 2
N_BPAR = 2
CHUNK_BLOCKS = CHUNK // P
N_NORM = (2 * KT + 1) * TOKENS + 4 * BLOCKS


def build_layer(nc, xT, consts, a_vg, a_dt, a_heads, a_wo, a_par, ffn_w, router_w, b_qk, b_vo, b_conv,
                b_bg, b_par, out):
    ctx = ExitStack()
    with ctx:
        sems = {}

        def sem(name):
            if name not in sems:
                sems[name] = ctx.enter_context(nc.semaphore(name))
            return sems[name]

        def sb(stack, name, shape, dt=F32):
            return stack.enter_context(nc.sbuf_tensor(name, shape, dt))

        def pair(stack, name, shape):
            return sb(stack, name + "_hi", shape, FR), sb(stack, name + "_lo", shape, FR)

        x = sb(ctx, "x", [P, KT, TOKENS])
        xn = pair(ctx, "xn", [P, KT, TOKENS])
        const = sb(ctx, "const", [P, N_CONST])
        ident = const[:, 0:P]
        bounds = const[:, P:3 * P].rearrange("p (d l) -> p d l", d=2)
        rows_b = sb(ctx, "rows_b", [P, 32], BF16)
        mean_w = sb(ctx, "mean_w", [P, P])
        ones_w = sb(ctx, "ones_w", [P, P])
        warm = sb(ctx, "warm", [P, 1])
        zero_w = sb(ctx, "zero_w", [P, P], BF16)
        zero_x = sb(ctx, "zero_x", [P, CHUNK], BF16)
        ps = ctx.enter_context(nc.psum_tensor("ps", [P, 8, CHUNK], F32))

        pro = ExitStack()
        ln_xc = sb(pro, "ln_xc", [P, KT, TOKENS])
        ln_sq = sb(pro, "ln_sq", [P, KT, TOKENS])
        ln_diag = sb(pro, "ln_diag", [P, CHUNKS, CHUNK])
        ln_v = sb(pro, "ln_v", [P, BLOCKS])
        ln_s = sb(pro, "ln_s", [P, BLOCKS])
        ln_r = sb(pro, "ln_r", [P, BLOCKS])
        ln_t = sb(pro, "ln_t", [P, BLOCKS])
        pro.close()

        ma = ExitStack()
        valz = pair(ma, "valz", [P, A_GROUP, BLOCKS, P])
        bc_at = ExitStack()
        bmat = [pair(bc_at, f"bmat{p}", [P, TOKENS]) for p in range(2)]
        cmat = [pair(bc_at, f"cmat{p}", [P, TOKENS]) for p in range(2)]
        bc_at.close()
        pro = ExitStack()
        a_vg_raw = sb(pro, "a_vg_raw", [P, A_TILES, KT, 2, P])
        a_vg_w = pair(pro, "a_vg_w", [P, A_TILES, KT, 2, P])
        a_dt_raw = sb(pro, "a_dt_raw", [P, KT, P])
        a_dt_w = pair(pro, "a_dt_w", [P, KT, P])
        pro.close()
        ma2 = ExitStack()
        bc_hold = sb(ma2, "bc_hold", [P, 8 * TOKENS])
        valT = sb(ma2, "valT", [P, A_TILES, TOKENS])
        gateT = sb(ma2, "gateT", [P, A_TILES, TOKENS])
        e_a = sb(ma2, "e_a", [P, 2, TRI])
        m_a = sb(ma2, "m_a", [P, 2, TRI])
        ms_a = pair(ma2, "ms_a", [P, 3, TRI])
        aw_raw = sb(ma2, "aw_raw", [P, 2, KT, 2, P])
        aw = pair(ma2, "aw", [P, 2, KT, 2, P])
        awo_raw = sb(ma2, "awo_raw", [P, DM])
        awo = pair(ma2, "awo", [P, DM])
        yT = sb(ma2, "yT", [P, TOKENS])
        ys = pair(ma2, "ys", [P, TOKENS])
        stage = sb(ma2, "stage", [P, TOKENS])
        pieces_a = sb(ma2, "pieces_a", [P, BATCH, TRI], BF16)
        ncum_a = sb(ma2, "ncum_a", [P, BLOCKS, 32])
        apar = sb(ma2, "apar", [P, N_APAR])
        neg_a = sb(ma2, "neg_a", [P, 1])
        ma2.close()
        ma.close()
        tmp = ExitStack()
        VALZ, VPAD = A_GROUP * BLOCKS * P, A_TILES * BATCH * PADDED
        sb(tmp, "valz_hold", [P, 2 * VALZ - VPAD])
        vpad = sb(tmp, "vpad", [P, A_TILES, BATCH, PADDED])
        sb(tmp, "bc_vg_hold", [P, 8 * TOKENS + 2 * A_TILES * TOKENS])
        dec_z = sb(tmp, "dec_z", [P, SEQ])
        dec_e = sb(tmp, "dec_e", [P, SEQ])
        dec_p = sb(tmp, "dec_p", [P, 2, SEQ], BF16)
        conv_t = sb(tmp, "conv_t", [P, BATCH, SEQ])
        tmp.close()
        a_conv_w = apar[:, 0:A_TILES * A_TAPS].rearrange("p (t j) -> p t j", j=A_TAPS)
        a_conv_b = apar[:, A_TILES * A_TAPS:A_TILES * (A_TAPS + 1)]
        a_d = apar[:, A_TILES * (A_TAPS + 1):A_TILES * (A_TAPS + 2)]
        a_log = apar[:, N_APAR - 2:N_APAR - 1]
        a_dt_b = apar[:, N_APAR - 1:N_APAR]

        mb = ExitStack()
        e_b = sb(mb, "e_b", [P, 2, TRI])
        m_b = sb(mb, "m_b", [P, 2, TRI])
        ms_b = pair(mb, "ms_b", [P, 2, TRI])
        CONV_HELD = 2 * 2 * (B_TAPS + B_TAPS // 2) * P
        wconv1 = pair(mb, "wconv1", [P, 2, B_TAPS, P])
        wsum1 = pair(mb, "wsum1", [P, 2, B_TAPS // 2, P])
        sb(mb, "ln_hold_b", [P, max(1, N_NORM - 4 * 2 * TRI - CONV_HELD)])
        planes = pair(mb, "planes", [P, 2, BATCH, 3, PLANE])
        q32 = sb(mb, "q32", [P, CHUNKS, 2, 2, PAIRS])
        qsum = sb(mb, "qsum", [P, CHUNKS, 2, PAIRS])
        conv_y = sb(mb, "conv_y", [P, CHUNKS, 2, PAIRS, 2])
        qk = [pair(mb, f"qk{p}", [P, 2, TOKENS]) for p in range(2)]
        qf = sb(mb, "qf", [P, 2, CHUNK])
        vtok = [pair(mb, f"vtok{p}", [P, BLOCKS, DM]) for p in range(2)]
        wbg_raw = sb(mb, "wbg_raw", [P, KT, 2, P])
        wbg = pair(mb, "wbg", [P, KT, 2, P])
        wqk_raw = sb(mb, "wqk_raw", [P, KT, 2, P])
        wqk = pair(mb, "wqk", [P, KT, 2, P])
        wvo_raw = sb(mb, "wvo_raw", [P, 2, B_VT, DM])
        wvo = pair(mb, "wvo", [P, 2, B_VT, DM])
        fold = pair(mb, "fold", [P, KT, DM])
        wconv_raw_all = sb(mb, "wconv_raw", [P, CONVW + 2])
        wconv_raw = wconv_raw_all[:, 0:CONVW].rearrange("p (s j m) -> p s j m", s=2, j=B_TAPS)
        conv_bias = sb(mb, "conv_bias", [P, 2, 2])
        wsum_raw = sb(mb, "wsum_raw", [P, 2, B_TAPS // 2, P])
        wsum = pair(mb, "wsum0", [P, 2, B_TAPS // 2, P]), wsum1
        wconv = pair(mb, "wconv0", [P, 2, B_TAPS, P]), wconv1
        pieces_b = sb(mb, "pieces_b", [P, BATCH, TRI], BF16)
        ncum_b = sb(mb, "ncum_b", [P, BLOCKS, 32])
        bpar = sb(mb, "bpar", [P, N_BPAR])
        mb.close()
        tmp = ExitStack()
        bg_z = sb(tmp, "bg_z", [P, 2, SEQ])
        bg_e = sb(tmp, "bg_e", [P, 2, SEQ])
        bg_cum = sb(tmp, "bg_cum", [P, SEQ])
        bg_ones = sb(tmp, "bg_ones", [P, SEQ])
        bg_p = sb(tmp, "bg_p", [P, 2, SEQ], BF16)
        tmp.close()

        mf = ExitStack()
        sb(mf, "ln_hold_f", [P, N_NORM])
        fw_raw = sb(mf, "fw_raw", [P, 2, KT * 2 * P + DM])
        fgu = pair(mf, "fgu", [P, 2, KT, 2, P])
        fd = pair(mf, "fd", [P, 2, DM])
        f_s = sb(mf, "f_s", [P, CHUNKS, CHUNK])
        f_sc = sb(mf, "f_sc", [P, CHUNKS, CHUNK])
        f_h = sb(mf, "f_h", [P, CHUNKS, CHUNK])
        fh = pair(mf, "fh", [P, 2, TOKENS])
        coef_r = sb(mf, "coef_r", [P, TOKENS])
        coef_s = sb(mf, "coef_s", [P, TOKENS])
        lgT = coef_r
        rw_raw = sb(mf, "rw_raw", [P, KT, 2, P])
        rw = pair(mf, "rw", [P, KT, 2, P])
        lg = sb(mf, "lg", [P, BLOCKS, LOGITS])
        pr = sb(mf, "pr", [P, BLOCKS, EXPERTS])
        r_mx = sb(mf, "r_mx", [P, BLOCKS])
        r_sum = sb(mf, "r_sum", [P, BLOCKS])
        r_keep = sb(mf, "r_keep", [P, BLOCKS, EXPERTS])
        r_top = sb(mf, "r_top", [P, BLOCKS, 8])
        r_gt = sb(mf, "r_gt", [P, BLOCKS, EXPERTS])
        r_eq = sb(mf, "r_eq", [P, BLOCKS, EXPERTS])
        r_before = sb(mf, "r_before", [P, BLOCKS, EXPERTS])
        r_cnt = sb(mf, "r_cnt", [P, BLOCKS])
        cexp = sb(mf, "cexp", [P, BLOCKS, EXPERTS, ROWS_E])
        mf.close()

        def f32(ap):
            return ap.bitcast(F32)

        def mm3(o, w, v, first, last=True):
            nc.tensor.matmul(o, w[0], v[0], start=first, stop=False, skip_group_check=True)
            nc.tensor.matmul(o, w[0], v[1], start=False, stop=False, skip_group_check=True)
            return nc.tensor.matmul(o, w[1], v[0], start=False, stop=last, skip_group_check=True)

        def at(t, *idx):
            return tuple(v[idx] for v in t)

        def half_view(ap):
            return ap.rearrange("p (h n) -> p h n", n=P)

        def halves(t):
            return tuple(half_view(v) for v in t)

        def first_m(ap):
            return half_view(ap[:, 0:TRI])[:, 0:3:2, :]

        def cols(c):
            return slice(c * CHUNK, (c + 1) * CHUNK)

        def counter(eng, name, start=0):
            n = [start]

            def step(ins):
                n[0] += 1
                ins.then_inc(sem(name), 1)
                eng.wait_ge(sem(name), n[0])
            return step

        X_FINAL = {1: lambda c: 4 * A_TILES + 2 * c + 2, 2: lambda c: 2 * c + 2,
                   3: lambda c: BATCH * (B_HEADS - 1) + 2 * c + 2, 4: lambda c: 2 * c + 2}

        def x_final(eng, n, c):
            if n == 0:
                eng.wait_ge(sem(f"x_loaded{c}"), 16)
            else:
                eng.wait_ge(sem(f"x_updated{n}"), X_FINAL[n](c))

        def mean_bank(n):
            return 6 if n == 1 else 0

        def norm_pe(pe, n):
            pe.wait_ge(sem("mean_made"), 1)
            for c in range(CHUNKS):
                x_final(pe, n, c)
                for k in range(KT):
                    ins = nc.tensor.matmul(ps[:, mean_bank(n) + c, :], mean_w[:], x[:, k, cols(c)], start=k == 0, stop=k == KT - 1)
                ins.then_inc(sem("ln_mean"), 1)
            for c in range(CHUNKS):
                for k in range(KT):
                    pe.wait_ge(sem("ln_sq"), KT * (CHUNKS * n + c) + k + 1)
                    for i in range(CHUNK_BLOCKS):
                        ins = nc.tensor.matmul(ps[:, 2 + c, i:i + 1], ln_sq[:, k, block_of(c, i)], mean_w[:, 0:1],
                                               start=k == 0 and i == 0, stop=k == KT - 1 and i == CHUNK_BLOCKS - 1,
                                               skip_group_check=True)
                ins.then_inc(sem("ln_var"), 1)
                keep_busy(pe, (6, 3)[c])
            pe.wait_ge(sem("ones_made"), 1)
            for c in range(CHUNKS):
                pe.wait_ge(sem("ln_diag"), CHUNKS * n + c + 1)
                nc.tensor.matmul(ps[:, 2 + c, :], ones_w[:], ln_diag[:, c, :], start=True, stop=True).then_inc(sem("ln_rstd"), 1)
                keep_busy(pe, 3)

        def keep_busy(pe, n):
            for _ in range(n):
                nc.tensor.matmul(ps[:, 4, :], zero_w[:], zero_x[:], start=True, stop=True)

        def block_of(c, i):
            return slice(c * CHUNK + i * P, c * CHUNK + (i + 1) * P)

        def norm_act(act, n, prepare_first, prepare_rest):
            act.wait_ge(sem("mean_made"), 1)
            nc.scalar.activation(warm[:], mean_w[:, 0:1], ACT.Sqrt)
            for c in range(CHUNKS):
                for k in range(KT):
                    act.wait_ge(sem("ln_xc"), KT * (CHUNKS * n + c) + k + 1)
                    nc.scalar.activation(ln_sq[:, k, cols(c)], ln_xc[:, k, cols(c)], ACT.Square).then_inc(sem("ln_sq"), 1)
            for c in range(CHUNKS):
                act.wait_ge(sem("ln_v"), CHUNKS * n + c + 1)
                nc.scalar.activation(norm_cols(ln_s, c), norm_cols(ln_v, c), ACT.Sqrt).then_inc(sem("ln_std"), 1)
            prepare_first(act)
            for c in range(CHUNKS):
                for k in range(KT):
                    act.wait_ge(sem("ln_xn"), KT * (CHUNKS * n + c) + k + 1)
                    nc.scalar.copy(xn[0][:, k, cols(c)], ln_xc[:, k, cols(c)]).then_inc(sem("ln_hi"), 1)
            prepare_rest(act)

        def norm_cols(t, c):
            return t[:, c * CHUNK_BLOCKS:(c + 1) * CHUNK_BLOCKS]

        def norm_dve(dve, n):
            step = counter(dve, "ln_step", 4 * CHUNKS * n)

            def rstd(c):
                v, s, r, t = (norm_cols(a, c) for a in (ln_v, ln_s, ln_r, ln_t))
                dve.wait_ge(sem("ln_var"), CHUNKS * n + c + 1)
                nc.vector.tensor_scalar(v, ps[:, 2 + c, 0:CHUNK_BLOCKS], EPS, None, ALU.add).then_inc(sem("ln_v"), 1)
                dve.wait_ge(sem("ln_std"), CHUNKS * n + c + 1)
                step(nc.vector.reciprocal(r, s))
                step(nc.vector.tensor_tensor(t, r, r, ALU.mult))
                step(nc.vector.scalar_tensor_tensor(t, t, -0.5, v, ALU.mult, ALU.mult))
                step(nc.vector.scalar_tensor_tensor(r, t, 1.5, r, ALU.add, ALU.mult))
                nc.vector.tensor_tensor(ln_diag[:, c].rearrange("p (i m) -> p i m", m=P),
                                        ident[:, None, :].broadcast_to([P, CHUNK_BLOCKS, P]),
                                        r[:, :, None].broadcast_to([P, CHUNK_BLOCKS, P]), ALU.mult).then_inc(sem("ln_diag"), 1)

            def scale(c):
                dve.wait_ge(sem("ln_rstd"), CHUNKS * n + c + 1)
                for k in range(KT):
                    nc.vector.tensor_tensor(ln_xc[:, k, cols(c)], ln_xc[:, k, cols(c)], ps[:, 2 + c, :],
                                            ALU.mult).then_inc(sem("ln_xn"), 1)

            def lo(c):
                for k in range(KT):
                    dve.wait_ge(sem("ln_hi"), KT * (CHUNKS * n + c) + k + 1)
                    ins = nc.vector.tensor_tensor(xn[1][:, k, cols(c)], ln_xc[:, k, cols(c)], f32(xn[0][:, k, cols(c)]), ALU.subtract)
                ins.then_inc(sem("ln_done"), 1)

            for c in range(CHUNKS):
                dve.wait_ge(sem("ln_mean"), CHUNKS * n + c + 1)
                for k in range(KT):
                    nc.vector.tensor_tensor(ln_xc[:, k, cols(c)], x[:, k, cols(c)], ps[:, mean_bank(n) + c, :],
                                            ALU.subtract).then_inc(sem("ln_xc"), 1)
            rstd(0)
            rstd(1)
            for c in range(CHUNKS):
                scale(c)
                lo(c)

        def normed(eng, n, c=CHUNKS - 1):
            eng.wait_ge(sem("ln_done"), CHUNKS * n + c + 1)

        def split_hi(dst, src, hi_sem):
            return nc.scalar.copy(dst[0], src).then_inc(sem(hi_sem), 1)

        def split_lo(pool, dst, src, hi_sem, count, done_sem):
            pool.wait_ge(sem(hi_sem), count)
            return nc.gpsimd.tensor_tensor(dst[1], src, f32(dst[0]), ALU.subtract).then_inc(sem(done_sem), 1)

        def a_pe(pe):
            pe.wait_ge(sem("a_pro_w"), 1)
            products = A_PRODUCTS
            for n, (t, s, c) in enumerate(products):
                normed(pe, 0, c)
                if n >= 8:
                    pe.wait_ge(sem("a_pro_read"), n - 7)
                if c == 0 and t >= 0 and s == 0:
                    pe.wait_ge(sem("a_pro_w"), 2 + t)
                for k in range(KT):
                    w = at(a_dt_w, slice(None), k) if t < 0 else at(a_vg_w, slice(None), t, k, s)
                    ins = mm3(ps[:, n % 8, :], w, at(xn, slice(None), k, cols(c)), k == 0, k == KT - 1)
                ins.then_inc(sem("a_pro_done"), 1)
            pe.wait_ge(sem("a_pro_read"), len(products))
            pe.wait_ge(sem("a_cum"), 1)
            cum_transpose_pe(dec_e, 2).then_inc(sem("a_cumT"), 1)
            a_project_pe(pe, 0, 0, 0)
            a_project_pe(pe, 0, 0, 1)
            a_project_pe(pe, 0, 0, 2)
            a_project_pe(pe, 0, 0, 3)
            pe.wait_ge(sem("a_pieces"), PIECES)
            pe.wait_ge(sem("a_ncum"), 1)
            a_state_pe(pe, 0, 0)
            with pe.Fori(0, A_TILES - 1) as g:
                a_group_pe(pe, g, False)
            a_group_pe(pe, A_TILES - 1, True)
            for n in range(4):
                if n >= 2:
                    pe.wait_ge(sem("x_updated1"), 4 * A_TILES + n - 1)
                a_out_pe(pe, A_TILES, n, n % 2)

        A_PRODUCTS = ([(-1, 0, 0), (0, 0, 0), (-1, 0, 1), (0, 0, 1)]
                      + [(t, 0, c) for t in range(1, A_TILES) for c in range(CHUNKS)]
                      + [(t, 1, c) for t in range(A_TILES) for c in range(CHUNKS)])

        def a_project_pe(pe, h, parity, q):
            s, c = q // 2, q % 2
            if q == 0:
                pe.wait_ge(sem("aw_split"), h + 1)
            if not (isinstance(h, int) and h == 0 and q < 2):
                pe.wait_ge(sem("bc_split"), 4 * h + q - 1)
            for k in range(KT):
                ins = mm3(ps[:, c, :], at(aw, slice(None), parity, k, s), at(xn, slice(None), k, cols(c)),
                          k == 0, k == KT - 1)
            ins.then_inc(sem("a_p_done"), 1)

        def a_out_pe(pe, g, n, bank):
            c, m = n // KT, n % KT
            if m == 0:
                pe.wait_ge(sem("ys_split"), 2 * g + c + 1)
                pe.wait_ge(sem("awo_split"), g + 1)
            mm3(ps[:, bank, :], at(awo, slice(None), slice(m * P, (m + 1) * P)), at(ys, slice(None), cols(c)),
                True).then_inc(sem("a_wo_done"), 1)

        def a_state_pe(pe, g, u):
            j, b = u // BATCH, u % BATCH
            p, l0 = j % 2, b * SEQ
            if u >= 2:
                pe.wait_ge(sem("a_m_done"), UNITS * g + u - 1)
            if b % 2 == 0:
                pe.wait_ge(sem("bc_split"), UNITS * g + 4 * j + 3 + b // 2)
            d, s = ps[:, 2 + u % 2, :], ps[:, 4 + u % 2, :]
            lhs = rows_b[:, bass.ds(g * A_GROUP + j, 1)].broadcast_to([P, P])
            nc.tensor.matmul(d[:, 0:TRI], lhs, pieces_a[:, b, :], start=True, stop=True, skip_group_check=True).then_inc(sem("a_d_done"), 1)
            mm3(first_m(s), at(bmat[p], slice(None), slice(l0, l0 + P)), halves(at(cmat[p], slice(None), slice(l0, l0 + SEQ))), True, False)
            mm3(s[:, P:2 * P], at(bmat[p], slice(None), slice(l0 + P, l0 + SEQ)),
                at(cmat[p], slice(None), slice(l0 + P, l0 + SEQ)), False).then_inc(sem("a_s_done"), 1)

        def a_value_pe(pe, g, u):
            j, b = u // BATCH, u % BATCH
            pe.wait_ge(sem("a_m_split"), UNITS * g + u + 1)
            if u == 0:
                pe.wait_ge(sem("valz_split"), 2 * g + 2)
            o, l0, t = ps[:, 6 + b // 2, :], (b % 2) * SEQ, 2 * b
            ms = at(ms_a, slice(None), u % 3)
            mm3(half_view(o[:, l0:l0 + SEQ]), at(valz, slice(None), j, t), tuple(first_m(v) for v in ms),
                j == 0 and b % 2 == 0, False)
            mm3(o[:, l0 + P:l0 + SEQ], at(valz, slice(None), j, t + 1), at(ms, slice(None), slice(P, 2 * P)),
                False, j == A_GROUP - 1).then_inc(sem("a_y_done"), 1)

        def a_group_pe(pe, g, last):
            for u in range(UNITS):
                if u > 0:
                    a_state_pe(pe, g, u)
                if u == 1:
                    pe.wait_ge(sem("stage_ready"), g + 1)
                    pe.wait_ge(sem("y_read"), 2 * g + 2)
                    for i in range(BLOCKS):
                        ins = nc.tensor.transpose(ps[:, 6 + i // 4, (i % 4) * P:(i % 4 + 1) * P], stage[:, i * P:(i + 1) * P], ident)
                        if i % 4 == 3:
                            ins.then_inc(sem("val_T"), 1)
                if u - 1 in OUT_UNITS:
                    pe.wait_ge(sem("x_updated1"), 4 * g + OUT_UNITS.index(u - 1) + 1)
                if not (last and u >= UNITS - BATCH):
                    a_project_pe(pe, g * A_GROUP + u // BATCH + 1, (u // BATCH + 1) % 2, u % BATCH)
                if u in OUT_UNITS:
                    pe.wait_ge(sem("bc_split"), UNITS * g + BATCH + u)
                    a_out_pe(pe, g, OUT_UNITS.index(u), (u + 1) % 2)
                if u >= 2:
                    a_value_pe(pe, g, u - 2)
            a_value_pe(pe, g, UNITS - 2)
            if not last:
                a_state_pe(pe, g + 1, 0)
            a_value_pe(pe, g, UNITS - 1)

        def a_prepare_act(act):
            act.wait_ge(sem("a_pro_loaded"), 32)
            split_hi(at(a_dt_w, slice(None)), a_dt_raw[:], "a_pro_hi")
            for t in range(A_TILES):
                split_hi(at(a_vg_w, slice(None), t), a_vg_raw[:, t], "a_pro_hi")

        def a_prepare_rest_act(act):
            for h in range(2):
                act.wait_ge(sem(f"aw_loaded{h}"), 16)
                split_hi(at(aw, slice(None), h), aw_raw[:, h], "aw_hi")
            act.wait_ge(sem("awo_loaded"), 16)
            split_hi(at(awo, slice(None)), awo_raw[:], "awo_hi")

        def a_act(act):
            act.wait_ge(sem("a_params"), 16)
            act.wait_ge(sem("vpad_zero"), 1)
            for n, (t, s, c) in enumerate(A_PRODUCTS):
                act.wait_ge(sem("a_pro_done"), n + 1)
                if t < 0:
                    for b in range(2 * c, 2 * c + 2):
                        ins = nc.scalar.activation(dec_z[of_batch(b), :], ps[of_batch(b), n, (b % 2) * SEQ:(b % 2 + 1) * SEQ],
                                                   ACT.Identity, bias=a_dt_b[of_batch(b)])
                elif s == 0:
                    ins = nc.scalar.copy(vpad[:, t, 2 * c:2 * c + 2, A_TAPS - 1:PADDED],
                                         ps[:, n % 8, :].rearrange("p (b l) -> p b l", l=SEQ))
                else:
                    ins = nc.scalar.activation(gateT[:, t, cols(c)], ps[:, n % 8, :], ACT.Silu)
                ins.then_inc(sem("a_pro_read"), 1)
                if (t, s, c) == (1, 0, 1):
                    act.wait_ge(sem("a_abs"), 1)
                    nc.scalar.activation(dec_e[:], dec_e[:], ACT.Exp, scale=-1.0).then_inc(sem("a_exp"), 1)
                    nc.scalar.activation(neg_a[:], a_log, ACT.Exp)
                    act.wait_ge(sem("a_exp"), 1)
                    nc.scalar.activation(dec_e[:], dec_e[:], ACT.Ln, bias=1.0).then_inc(sem("a_ln"), 1)
            for t in range(A_TILES):
                if t < A_TILES - 1:
                    act.wait_ge(sem("a_conv"), t + 1)
                else:
                    act.wait_ge(sem("a_pool_step"), 2 * A_TAPS - 1)
                nc.scalar.activation(valT[:, t, :], valT[:, t, :], ACT.Silu, bias=a_conv_b[:, t:t + 1]).then_inc(sem("a_val"), 1)
                if t < 2:
                    for q in range(2 * t, 2 * t + 2):
                        a_project_act(act, 0, 0, q)
                if t == 0:
                    act.wait_ge(sem("a_cumT"), 1)
                    ncum_act(ncum_a, 2).then_inc(sem("a_ncum"), 1)
            nc.scalar.activation(warm[:], mean_w[:, 0:1], ACT.Exp)
            act.wait_ge(sem("a_ncum"), 1)
            with act.Fori(0, A_TILES - 1) as g:
                a_group_act(act, g, False)
            a_group_act(act, A_TILES - 1, True)
            for c in range(CHUNKS):
                a_y_act(act, A_TILES, c)

        def a_project_act(act, h, parity, q):
            s, c = q // 2, q % 2
            act.wait_ge(sem("a_p_done"), 4 * h + q + 1)
            nc.scalar.copy((bmat, cmat)[s][parity][0][:, cols(c)], ps[:, c, :]).then_inc(sem("bc_hi"), 1)

        def a_group_act(act, g, last):
            for u in range(UNITS):
                j, b = u // BATCH, u % BATCH
                h = g * A_GROUP + j
                act.wait_ge(sem("a_bounded"), UNITS * g + u + 1)
                nc.scalar.activation(e_a[:, u % 2], e_a[:, u % 2], ACT.Exp).then_inc(sem("a_e_done"), 1)
                if not (last and u >= UNITS - BATCH):
                    a_project_act(act, h + 1, (j + 1) % 2, b)
                act.wait_ge(sem("a_m_done"), UNITS * g + u + 1)
                split_hi(at(ms_a, slice(None), u % 3), m_a[:, u % 2, :], "a_m_hi")
                if u == 0:
                    act.wait_ge(sem("valz_zero"), 5)
                    for c in range(2):
                        act.wait_ge(sem("val_T"), 2 * g + c + 1)
                        nc.scalar.copy(valz_diagonal(valz[0], c), val_blocks(c)).then_inc(sem("valz_hi"), 1)
                if b == 1 and not (last and j >= A_GROUP - 2):
                    act.wait_ge(sem(f"aw_loaded{j % 2}"), 8 * h + 32 - 8 * (j % 2))
                    split_hi(at(aw, slice(None), j % 2), aw_raw[:, j % 2], "aw_hi")
                if 2 <= u < 2 + CHUNKS:
                    a_y_act(act, g, u - 2)
                if u == OUT_UNITS[0] + 8:
                    act.wait_ge(sem("awo_loaded"), 16 * g + 32)
                    split_hi(at(awo, slice(None)), awo_raw[:], "awo_hi")

        def a_y_act(act, g, c):
            act.wait_ge(sem("y_gated"), 2 * g + c + 1)
            split_hi(at(ys, slice(None), cols(c)), yT[:, cols(c)], "ys_hi")

        def a_y_dve(dve, g, c):
            dve.wait_ge(sem("ys_hi"), 2 * g + c + 1)
            nc.vector.tensor_tensor(ys[1][:, cols(c)], yT[:, cols(c)], f32(ys[0][:, cols(c)]), ALU.subtract).then_inc(sem("ys_split"), 1)

        def val_blocks(c):
            return ps[:, 6 + c, :].rearrange("p (i j d) -> p i j d", j=A_GROUP, d=A_HD)

        def valz_diagonal(z, c):
            flat = z[:].rearrange("p j i m -> p (j i m)")
            step = BLOCKS * P + A_HD
            ap = flat[:, 4 * c * P:4 * c * P + A_HD]
            return bass.AP(ap.tensor, ap.offset, [list(ap.ap[0]), [P, 4], [step, A_GROUP], [1, A_HD]])

        def a_dve(dve):
            step = counter(dve, "a_dve_step")
            dve.wait_ge(sem("a_params"), 16)
            dve.wait_ge(sem("a_pro_read"), 3)
            nc.vector.scalar_tensor_tensor(dec_e[:], dec_z[:], -1.0, dec_z[:], ALU.mult, ALU.max).then_inc(sem("a_abs"), 1)
            a_conv_dve(dve, step, 0)
            dve.wait_ge(sem("a_ln"), 1)
            step(nc.vector.scalar_tensor_tensor(dec_e[:], dec_z[:], 0.0, dec_e[:], ALU.max, ALU.add))
            step(nc.vector.tensor_scalar(dec_z[:], dec_e[:], neg_a[:], -1.0, ALU.mult, ALU.mult))
            nc.vector.tensor_tensor_scan(dec_e[:], yT[:, 0:SEQ], dec_z[:], 0.0, ALU.mult, ALU.add).then_inc(sem("a_cum"), 1)
            a_conv_dve(dve, step, 1)
            dve.wait_ge(sem("a_cum"), 1)
            step(nc.vector.tensor_copy(dec_z[:], dec_e[:]))
            split_pieces(dve, step, pieces_a, dec_z[:], dec_p, "a_pieces")
            a_conv_dve(dve, step, 2)
            for q in range(4):
                a_project_dve(dve, 0, 0, q)
            dve.wait_ge(sem("a_val"), 1)
            nc.vector.tensor_copy(stage[:], valT[:, 0, :]).then_inc(sem("stage_ready"), 1)
            dve.wait_ge(sem("a_val"), A_TILES)
            with dve.Fori(0, A_TILES - 1) as g:
                a_group_dve(dve, g, False)
            a_group_dve(dve, A_TILES - 1, True)
            for n in range(4):
                a_out_dve(dve, A_TILES, n, n % 2)

        def a_early_dve(dve):
            nc.vector.memset(vpad[:, :, :, 0:A_TAPS - 1], 0.0).then_inc(sem("vpad_zero"), 1)
            nc.vector.memset(yT[:, 0:CHUNK], 1.0).then_inc(sem("a_early"), 1)
            nc.vector.memset(yT[:, CHUNK:], 1.0).then_inc(sem("y_gated"), 2)
            nc.vector.memset(pieces_a[:], 0.0).then_inc(sem("a_early"), 1)
            nc.vector.memset(neg_a[:], 0.0).then_inc(sem("y_read"), 2)
            dve.wait_ge(sem("a_early"), 2)

        def a_conv_dve(dve, step, t):
            dve.wait_ge(sem("a_pro_read"), 1 + max(A_PRODUCTS.index((t, 0, c)) for c in range(CHUNKS)))
            v = valT[:, t, :].rearrange("p (b l) -> p b l", l=SEQ)
            step(nc.vector.tensor_scalar(v, vpad[:, t, :, 0:SEQ], a_conv_w[:, t, 0:1], None, ALU.mult))
            for j in range(1, A_TAPS):
                ins = nc.vector.scalar_tensor_tensor(v, vpad[:, t, :, j:j + SEQ], a_conv_w[:, t, j:j + 1], v, ALU.mult, ALU.add)
                if j < A_TAPS - 1:
                    step(ins)
            ins.then_inc(sem("a_conv"), 1)

        def a_conv_pool(pool, t):
            pool.wait_ge(sem("a_pro_read"), 1 + max(A_PRODUCTS.index((t, 0, c)) for c in range(CHUNKS)))
            step = counter(pool, "a_pool_step")
            v = valT[:, t, :].rearrange("p (b l) -> p b l", l=SEQ)
            for j in range(A_TAPS):
                w = a_conv_w[:, t, j:j + 1, None].broadcast_to([P, BATCH, SEQ])
                step(nc.gpsimd.tensor_tensor(v if j == 0 else conv_t[:], vpad[:, t, :, j:j + SEQ], w, ALU.mult))
                if j:
                    step(nc.gpsimd.tensor_tensor(v, v, conv_t[:], ALU.add))

        def of_batch(b):
            return slice(32 * b, 32 * b + 32)

        def split_pieces(dve, step, dst, v, pieces, done, which=range(3)):
            for j in which:
                p = pieces[:, j % 2]
                step(nc.vector.tensor_copy(p, v))
                if j < 2:
                    step(nc.vector.tensor_tensor(v, v, p, ALU.subtract))
                for b in range(BATCH):
                    nc.vector.tensor_copy(dst[of_batch(j), b, 0:SEQ], p[of_batch(b)]).then_inc(sem(done), 1)
            if j < 2:
                return
            dve.wait_ge(sem(done), 3 * BATCH)
            nc.vector.tensor_copy(dst[0:96, :, SEQ:TRI], dst[0:96, :, P:SEQ]).then_inc(sem(done), 1)

        PIECES = 3 * BATCH + 1

        def cum_transpose_pe(cum, bank):
            for i in range(2):
                ins = nc.tensor.transpose(ps[:, bank, i * P:(i + 1) * P], cum[:, i * P:(i + 1) * P], ident)
            return ins

        def ncum_act(dst, bank):
            return nc.scalar.mul(dst[:].rearrange("p (b i) h -> p i b h", i=2),
                                 ps[:, bank, 0:2 * P].rearrange("p (i b h) -> p i b h", i=2, h=32), -1.0)

        def a_project_dve(dve, h, parity, q):
            s, c = q // 2, q % 2
            m = (bmat, cmat)[s][parity]
            dve.wait_ge(sem("bc_hi"), 4 * h + q + 1)
            nc.vector.tensor_tensor(m[1][:, cols(c)], ps[:, c, :], f32(m[0][:, cols(c)]),
                                    ALU.subtract).then_inc(sem("bc_split"), 1)

        def a_out_dve(dve, g, n, bank):
            c, m = n // KT, n % KT
            dve.wait_ge(sem("a_wo_done"), 4 * g + n + 1)
            nc.vector.tensor_tensor(x[:, m, cols(c)], x[:, m, cols(c)], ps[:, bank, :], ALU.add).then_inc(sem("x_updated1"), 1)

        def exponents_dve(e, d, ncum, b, h):
            nc.vector.scalar_tensor_tensor(first_m(e), first_m(d), ncum[:, 2 * b, bass.ds(h, 1)], bounds, ALU.add, ALU.min)
            return nc.vector.scalar_tensor_tensor(e[:, P:2 * P], d[:, P:2 * P], ncum[:, 2 * b + 1, bass.ds(h, 1)],
                                                  bounds[:, 0], ALU.add, ALU.min)

        def a_values_dve(dve, g, c):
            dve.wait_ge(sem("valz_zero"), 5)
            dve.wait_ge(sem("valz_hi"), 2 * g + c + 1)
            nc.vector.tensor_tensor(valz_diagonal(valz[1], c), val_blocks(c), f32(valz_diagonal(valz[0], c)),
                                    ALU.subtract).then_inc(sem("valz_split"), 1)

        def a_group_dve(dve, g, last):
            def project_before(u):
                j, b = (u - 1) // BATCH, (u - 1) % BATCH
                a_project_dve(dve, g * A_GROUP + j + 1, (j + 1) % 2, b)

            for u in range(UNITS):
                j, b = u // BATCH, u % BATCH
                dve.wait_ge(sem("a_d_done"), UNITS * g + u + 1)
                dve.wait_ge(sem("a_ncum"), 1)
                exponents_dve(e_a[:, u % 2], ps[:, 2 + u % 2, :], ncum_a, b, g * A_GROUP + j).then_inc(sem("a_bounded"), 1)
                if u > 0 and not (last and u > UNITS - BATCH):
                    project_before(u)
                if u == 1:
                    a_values_dve(dve, g, 0)
                dve.wait_ge(sem("a_s_done"), UNITS * g + u + 1)
                dve.wait_ge(sem("a_e_done"), UNITS * g + u + 1)
                if u >= 2:
                    dve.wait_ge(sem("a_m_split"), UNITS * g + u - 1)
                nc.vector.tensor_tensor(m_a[:, u % 2, :], ps[:, 4 + u % 2, 0:TRI], e_a[:, u % 2, :],
                                        ALU.mult).then_inc(sem("a_m_done"), 1)
                if u == 1:
                    a_values_dve(dve, g, 1)
                if 3 <= u < 3 + CHUNKS:
                    a_y_dve(dve, g, u - 3)
                if u in OUT_UNITS:
                    a_out_dve(dve, g, OUT_UNITS.index(u), (u + 1) % 2)
                if u == OUT_UNITS[0] - 2 and not last:
                    nc.vector.tensor_copy(stage[:], group_tile(valT, g + 1, 0, TOKENS)).then_inc(sem("stage_ready"), 1)
            if not last:
                project_before(UNITS)
            for c in range(CHUNKS):
                dve.wait_ge(sem("a_y_done"), UNITS * g + UNITS - BATCH + 2 * c + 2)
                nc.vector.scalar_tensor_tensor(yT[:, cols(c)], group_tile(valT, g, c * CHUNK, CHUNK), a_d[:, bass.ds(g, 1)],
                                               ps[:, 6 + c, :], ALU.mult, ALU.add).then_inc(sem("y_read"), 1)
                dve.wait_ge(sem("y_read"), 2 * g + 2 + c + 1)
                nc.vector.tensor_tensor(yT[:, cols(c)], yT[:, cols(c)], group_tile(gateT, g, c * CHUNK, CHUNK),
                                        ALU.mult).then_inc(sem("y_gated"), 1)
                if last:
                    a_y_dve(dve, g + 1, c)

        def group_tile(t, g, first, n):
            return t[:].rearrange("p t n -> p (t n)")[:, bass.ds(g * TOKENS + first, n)]

        def a_pool(pool):
            hi, lo = (f32(v[:].rearrange("p j i m -> p (j i m)")) for v in valz)
            nc.gpsimd.memset(hi[:, N_NORM:], 0.0).then_inc(sem("valz_zero"), 1)
            nc.gpsimd.memset(lo[:, 0:VALZ - VPAD], 0.0).then_inc(sem("valz_zero"), 1)
            split_lo(pool, at(a_dt_w, slice(None)), a_dt_raw[:], "a_pro_hi", 1, "a_pro_w")
            for t in range(A_TILES):
                split_lo(pool, at(a_vg_w, slice(None), t), a_vg_raw[:, t], "a_pro_hi", 2 + t, "a_pro_w")
            for h in range(2):
                split_lo(pool, at(aw, slice(None), h), aw_raw[:, h], "aw_hi", h + 1, "aw_split")
            split_lo(pool, at(awo, slice(None)), awo_raw[:], "awo_hi", 1, "awo_split")
            pool.wait_ge(sem("a_params"), 16)
            a_conv_pool(pool, A_TILES - 1)
            normed(pool, 0)
            nc.gpsimd.memset(hi[:, 0:N_NORM], 0.0).then_inc(sem("valz_zero"), 1)
            part = VALZ - VPAD // A_TILES
            nc.gpsimd.memset(lo[:, part:], 0.0).then_inc(sem("valz_zero"), 1)
            pool.wait_ge(sem("a_conv"), A_TILES - 1)
            nc.gpsimd.memset(lo[:, VALZ - VPAD:part], 0.0).then_inc(sem("valz_zero"), 1)
            with pool.Fori(0, A_TILES - 1) as g:
                a_group_pool(pool, g, False)
            a_group_pool(pool, A_TILES - 1, True)

        def a_group_pool(pool, g, last):
            for u in range(UNITS):
                j, b = u // BATCH, u % BATCH
                split_lo(pool, at(ms_a, slice(None), u % 3), m_a[:, u % 2, :], "a_m_hi", UNITS * g + u + 1, "a_m_split")
                if b == 1 and not (last and j >= A_GROUP - 2):
                    split_lo(pool, at(aw, slice(None), j % 2), aw_raw[:, j % 2], "aw_hi", g * A_GROUP + j + 3, "aw_split")
                if u == OUT_UNITS[0] + 8:
                    split_lo(pool, at(awo, slice(None)), awo_raw[:], "awo_hi", g + 2, "awo_split")

        def a_sp(sp):
            sp.dma_start(a_dt_raw[:], a_dt).then_inc(sem("a_pro_loaded"), 16)
            sp.dma_start(a_vg_raw[:], a_vg).then_inc(sem("a_pro_loaded"), 16)
            sp.dma_start(apar[:], a_par).then_inc(sem("a_params"), 16)
            for h in range(2):
                sp.dma_start(aw_raw[:, h], a_heads[h * P:(h + 1) * P, :]).then_inc(sem(f"aw_loaded{h}"), 16)
            sp.dma_start(awo_raw[:], a_wo[0:P, :]).then_inc(sem("awo_loaded"), 16)
            with sp.Fori(0, A_TILES - 1) as g:
                a_group_sp(sp, g, False)
            a_group_sp(sp, A_TILES - 1, True)

        def a_group_sp(sp, g, last):
            for j in range(A_GROUP):
                if j == 0:
                    sp.wait_ge(sem("awo_split"), g + 1)
                    sp.dma_start(awo_raw[:], a_wo[bass.ds(g * P + P, P), :]).then_inc(sem("awo_loaded"), 16)
                if not (last and j >= A_GROUP - 2):
                    h2 = g * A_GROUP + j + 2
                    sp.wait_ge(sem("aw_split"), h2 - 1)
                    sp.dma_start(aw_raw[:, j % 2], a_heads[bass.ds(h2 * P, P), :]).then_inc(sem(f"aw_loaded{j % 2}"), 16)

        EACH_CHUNK, EACH_LOAD = CHUNKS * F_TILES, 16 * (F_TILES // 2)
        F_TOTAL = dict(rw=1, rw_hi=1, rw_loaded=16, w_loaded0=EACH_LOAD, w_loaded1=EACH_LOAD, gu_hi=F_TILES, gu_split=F_TILES,
                       d_hi=F_TILES, d_split=F_TILES, gate_logits=CHUNKS, gate=CHUNKS, logits=CHUNKS, lgT=CHUNKS, lg_T=1, lg=1,
                       shift=1, exp=1, keep=2, dve_step=11, coef=1, coefT=1, coef_ready=1, up_done=EACH_CHUNK,
                       silu=EACH_CHUNK, sc=EACH_CHUNK, h=EACH_CHUNK, h_hi=EACH_CHUNK, h_split=EACH_CHUNK,
                       down_done=F_TILES + CHUNKS)

        F_LATE_D = 1

        def f_count(f, name, count):
            return count + f * F_TOTAL[name]

        def f_pe(pe, n, f):
            pe.wait_ge(sem("f_rw"), f_count(f, "rw", 1))
            for c in range(CHUNKS):
                normed(pe, n, c)
                f_logits_pe(pe, 0, c).then_inc(sem("f_gate_logits"), 1)
                f_up_pe(pe, f, 0, 0, [c])
            for c in range(CHUNKS):
                f_logits_pe(pe, 1, c).then_inc(sem("f_logits"), 1)
            f_up_pe(pe, f, 1, 1)
            for c in range(CHUNKS):
                pe.wait_ge(sem("f_lgT"), f_count(f, "lgT", c + 1))
                for i in range(CHUNK_BLOCKS):
                    b = c * CHUNK_BLOCKS + i
                    if b == 0:
                        pe.wait_ge(sem("f_lgT"), f_count(f, "lgT", CHUNKS))
                    ins = nc.tensor.transpose(ps[:, 6, b * LOGITS:(b + 1) * LOGITS], lgT[0:LOGITS, b * P:(b + 1) * P],
                                              ident[0:LOGITS, 0:LOGITS])
            ins.then_inc(sem("f_lg_T"), 1)
            pe.wait_ge(sem("f_gate"), f_count(f, "gate", CHUNKS))
            pe.wait_ge(sem("f_lg"), f_count(f, "lg", 1))
            for a in range(4):
                ins = nc.tensor.matmul(ps[:, 4 + a, :], zero_w[:], zero_x[:], start=True, stop=False, skip_group_check=True)
            ins.then_inc(sem("f_down_done"), 1)
            for i in range(S_TILES - 2):
                f_down_pe(pe, f, i, i % 2)
                f_up_pe(pe, f, i + 2, i % 2)
            f_down_pe(pe, f, S_TILES - 2, 0)
            pe.wait_ge(sem("f_coef"), f_count(f, "coef", 1))
            pe.wait_ge(sem("f_silu"), f_count(f, "silu", CHUNKS * S_TILES))
            for i in range(BLOCKS):
                ins = nc.tensor.transpose(ps[:, i // 4, (i % 4) * P:(i % 4 + 1) * P],
                                          cexp[:, i].rearrange("p e r -> p (e r)"), ident)
            ins.then_inc(sem("f_coefT"), 1)
            f_down_pe(pe, f, S_TILES - 1, 1)
            pe.wait_ge(sem("f_coef_ready"), f_count(f, "coef_ready", 1))
            f_up_pe(pe, f, S_TILES, 0)
            with pe.Fori(S_TILES // 2, F_TILES // 2 - 1) as i2:
                for p in range(2):
                    f_up_pe(pe, f, 2 * i2 + p + 1, 1 - p)
                    f_down_pe(pe, f, 2 * i2 + p, p)
            f_up_pe(pe, f, F_TILES - 1, 1)
            f_down_pe(pe, f, F_TILES - 2, 0)
            f_down_pe(pe, f, F_TILES - 1, 1, True)

        def f_logits_pe(pe, s, c):
            for k in range(KT):
                ins = mm3(ps[:, 4 + 2 * s + c, :], at(rw, slice(None), k, s), at(xn, slice(None), k, cols(c)), k == 0, k == KT - 1)
            return ins

        def f_up_pe(pe, f, i, p, chunks=range(CHUNKS)):
            pe.wait_ge(sem("f_gu_split"), f_count(f, "gu_split", i + 1))
            for c in chunks:
                if not (isinstance(i, int) and i == 0):
                    pe.wait_ge(sem("f_h"), f_count(f, "h", 2 * i + c - 1))
                for s in range(2):
                    for k in range(KT):
                        ins = mm3(ps[:, 2 * s + c, :], at(fgu, slice(None), p, k, s), at(xn, slice(None), k, cols(c)),
                                  k == 0, k == KT - 1)
                ins.then_inc(sem("f_up_done"), 1)

        def f_down_pe(pe, f, i, p, last=False):
            pe.wait_ge(sem("f_d_split"), f_count(f, "d_split", i + 1))
            for c in range(CHUNKS):
                pe.wait_ge(sem("f_h_split"), f_count(f, "h_split", 2 * i + c + 1))
                for m in range(KT):
                    ins = mm3(ps[:, 4 + 2 * c + m, :], at(fd, slice(None), p, slice(m * P, (m + 1) * P)),
                              at(fh, slice(None), p, cols(c)), False, False)
                if last or c == CHUNKS - 1:
                    ins.then_inc(sem("f_down_done"), 1)

        def f_act(act, n, f):
            for c in range(CHUNKS):
                act.wait_ge(sem("f_gate_logits"), f_count(f, "gate_logits", c + 1))
                nc.scalar.activation(coef_s[:, cols(c)], ps[:, 4 + c, :], ACT.Sigmoid).then_inc(sem("f_gate"), 1)
            for i in range(S_TILES):
                if i == S_TILES - 1:
                    f_hidden_act(act, f, i, i % 2, False, False)
                else:
                    f_hidden_act(act, f, i, i % 2, True, i >= F_LATE_D, 0 < i <= F_LATE_D)
                if i == 1:
                    act.wait_ge(sem("f_shift"), f_count(f, "shift", 1))
                    nc.scalar.activation(pr[:], pr[:], ACT.Exp).then_inc(sem("f_exp"), 1)
            act.wait_ge(sem("f_coefT"), f_count(f, "coefT", 1))
            nc.scalar.copy(coef_r[:].rearrange("p (a n) -> p a n", a=2), ps[:, 0:2, :]).then_inc(sem("f_coef_ready"), 1)
            f_down_weights_act(act, f, S_TILES, 0)
            f_up_weights_act(act, f, S_TILES + 1, 1)
            with act.Fori(S_TILES // 2, F_TILES // 2 - 1) as i2:
                for p in range(2):
                    f_hidden_act(act, f, 2 * i2 + p, p, True, True)
            f_hidden_act(act, f, F_TILES - 2, 0, False, True)
            f_hidden_act(act, f, F_TILES - 1, 1, False, False)

        def f_prepare_act(act, f):
            act.wait_ge(sem("f_rw_loaded"), f_count(f, "rw_loaded", 16))
            split_hi(at(rw, slice(None)), rw_raw[:], "f_rw_hi")
            f_prepare_gu_act(act, f, 0)

        def f_prepare_rest_act(act, f):
            f_prepare_gu_act(act, f, 1)
            split_hi(at(fd, slice(None), 0), raw_d(0), "f_d_hi")

        def f_prepare_gu_act(act, f, p):
            act.wait_ge(sem(f"f_w_loaded{p}"), f_count(f, f"w_loaded{p}", 16))
            split_hi(at(fgu, slice(None), p), raw_gu(p), "f_gu_hi")

        def f_hidden_act(act, f, i, p, more_gu, more_d, own_d=False):
            for c in range(CHUNKS):
                act.wait_ge(sem("f_up_done"), f_count(f, "up_done", 2 * i + c + 1))
                nc.scalar.activation(f_s[:, c], ps[:, c, :], ACT.Silu).then_inc(sem("f_silu"), 1)
            if own_d:
                f_down_weights_act(act, f, i, p)
            for c in range(CHUNKS):
                act.wait_ge(sem("f_h"), f_count(f, "h", 2 * i + c + 1))
                split_hi(at(fh, slice(None), p, cols(c)), f_h[:, c], "f_h_hi")
            if more_d:
                f_down_weights_act(act, f, i + 1, 1 - p)
            if more_gu:
                f_up_weights_act(act, f, i + 2, p)

        def f_up_weights_act(act, f, i, p):
            act.wait_ge(sem(f"f_w_loaded{p}"), f_count(f, f"w_loaded{p}", 8 * i + 16 - 8 * p))
            split_hi(at(fgu, slice(None), p), raw_gu(p), "f_gu_hi")

        def f_down_weights_act(act, f, i, p):
            act.wait_ge(sem("f_down_done"), f_count(f, "down_done", i))
            split_hi(at(fd, slice(None), p), raw_d(p), "f_d_hi")

        def raw_gu(p):
            return fw_raw[:, p, 0:KT * 2 * P].rearrange("p (k s m) -> p k s m", k=KT, s=2)

        def raw_d(p):
            return fw_raw[:, p, KT * 2 * P:]

        def f_pool(pool, n, f):
            split_lo(pool, at(rw, slice(None)), rw_raw[:], "f_rw_hi", f_count(f, "rw_hi", 1), "f_rw")
            for p in range(2):
                f_split_gu_pool(pool, f, p, p)
            f_split_d_pool(pool, f, 0, 0)
            pool.wait_ge(sem("f_gate"), f_count(f, "gate", CHUNKS))
            for i in range(S_TILES):
                f_hidden_pool(pool, f, i, i % 2, coef_s, True, i >= F_LATE_D, 0 < i <= F_LATE_D)
            pool.wait_ge(sem("f_coef_ready"), f_count(f, "coef_ready", 1))
            with pool.Fori(S_TILES // 2, F_TILES // 2 - 1) as i2:
                for p in range(2):
                    f_hidden_pool(pool, f, 2 * i2 + p, p, coef_r, True, True)
            f_hidden_pool(pool, f, F_TILES - 2, 0, coef_r, False, True)
            f_hidden_pool(pool, f, F_TILES - 1, 1, coef_r, False, False)

        def f_split_gu_pool(pool, f, i, p):
            split_lo(pool, at(fgu, slice(None), p), raw_gu(p), "f_gu_hi", f_count(f, "gu_hi", i + 1), "f_gu_split")

        def f_split_d_pool(pool, f, i, p):
            split_lo(pool, at(fd, slice(None), p), raw_d(p), "f_d_hi", f_count(f, "d_hi", i + 1), "f_d_split")

        def f_hidden_pool(pool, f, i, p, coef, more_gu, more_d, own_d=False):
            for c in range(CHUNKS):
                pool.wait_ge(sem("f_silu"), f_count(f, "silu", 2 * i + c + 1))
                nc.gpsimd.tensor_tensor(f_sc[:, c], f_s[:, c], coef[:, cols(c)], ALU.mult).then_inc(sem("f_sc"), 1)
            if own_d:
                f_split_d_pool(pool, f, i, p)
            if more_d:
                f_split_d_pool(pool, f, i + 1, 1 - p)
            if more_gu:
                f_split_gu_pool(pool, f, i + 2, p)

        def f_dve(dve, n, f):
            step = counter(dve, "f_dve_step", f_count(f, "dve_step", 0))
            nc.vector.memset(r_keep[:], 1.0).then_inc(sem("f_keep"), 1)
            dve.wait_ge(sem("f_keep"), f_count(f, "keep", 1))
            nc.vector.memset(r_keep[:, :, 0], 0.0).then_inc(sem("f_keep"), 1)
            for i in range(S_TILES):
                f_hidden_dve(dve, f, i, i % 2)
                if i == 0:
                    for c in range(CHUNKS):
                        dve.wait_ge(sem("f_logits"), f_count(f, "logits", c + 1))
                        nc.vector.tensor_copy(lgT[0:LOGITS, cols(c)], ps[0:LOGITS, 6 + c, :]).then_inc(sem("f_lgT"), 1)
                    dve.wait_ge(sem("f_lg_T"), f_count(f, "lg_T", 1))
                    nc.vector.tensor_copy(lg[:], ps[:, 6, 0:BLOCKS * LOGITS].rearrange("p (i e) -> p i e", e=LOGITS)
                                          ).then_inc(sem("f_lg"), 1)
                    dve.wait_ge(sem("f_lg"), f_count(f, "lg", 1))
                    step(nc.vector.tensor_reduce(r_mx[:], lg[:, :, 0:EXPERTS], AX_X, ALU.max))
                    nc.vector.tensor_tensor(pr[:], lg[:, :, 0:EXPERTS], r_mx[:, :, None].broadcast_to(R_WIDE),
                                            ALU.subtract).then_inc(sem("f_shift"), 1)
                if i == 2:
                    f_route_dve(dve, f, step)
            with dve.Fori(S_TILES // 2, F_TILES // 2) as i2:
                for p in range(2):
                    f_hidden_dve(dve, f, 2 * i2 + p, p)
            for c in range(CHUNKS):
                dve.wait_ge(sem("f_down_done"), f_count(f, "down_done", F_TILES + 1 + c))
                for m in range(KT):
                    nc.vector.tensor_tensor(x[:, m, cols(c)], x[:, m, cols(c)], ps[:, 4 + 2 * c + m, :],
                                            ALU.add).then_inc(sem(f"x_updated{n + 1}"), 1)

        R_WIDE = [P, BLOCKS, EXPERTS]

        def f_route_dve(dve, f, step):
            dve.wait_ge(sem("f_exp"), f_count(f, "exp", 1))
            dve.wait_ge(sem("f_keep"), f_count(f, "keep", 2))
            step(nc.vector.tensor_reduce(r_sum[:], pr[:], AX_X, ALU.add))
            step(nc.vector.reciprocal(r_sum[:], r_sum[:]))
            step(nc.vector.tensor_tensor(pr[:], pr[:], r_sum[:, :, None].broadcast_to(R_WIDE), ALU.mult))
            for b in range(BLOCKS):
                ins = nc.vector.max(out=r_top[:, b], in_=pr[:, b])
            step(ins)
            least = r_top[:, :, TOP_K - 1:TOP_K].broadcast_to(R_WIDE)
            nc.vector.tensor_tensor(r_gt[:], pr[:], least, ALU.is_gt)
            step(nc.vector.tensor_tensor(r_eq[:], pr[:], least, ALU.is_equal))
            nc.vector.tensor_reduce(r_cnt[:], r_gt[:], AX_X, ALU.add)
            step(nc.vector.tensor_tensor_scan(flat(r_before), flat(r_keep), flat(r_eq), 0.0, ALU.mult, ALU.add))
            step(nc.vector.tensor_tensor(r_before[:], r_before[:], r_cnt[:, :, None].broadcast_to(R_WIDE), ALU.add))
            step(nc.vector.scalar_tensor_tensor(r_eq[:], r_before[:], TOP_K + 0.5, r_eq[:], ALU.is_lt, ALU.mult))
            step(nc.vector.tensor_tensor(r_gt[:], r_gt[:], r_eq[:], ALU.add))
            step(nc.vector.tensor_tensor(pr[:], pr[:], r_gt[:], ALU.mult))
            nc.vector.tensor_copy(cexp[:], pr[:, :, :, None].broadcast_to([P, BLOCKS, EXPERTS, ROWS_E])).then_inc(sem("f_coef"), 1)

        def flat(t):
            return t[:].rearrange("p i e -> p (i e)")

        def f_hidden_dve(dve, f, i, p):
            for c in range(CHUNKS):
                dve.wait_ge(sem("f_sc"), f_count(f, "sc", 2 * i + c + 1))
                nc.vector.tensor_tensor(f_h[:, c], f_sc[:, c], ps[:, 2 + c, :], ALU.mult).then_inc(sem("f_h"), 1)
                dve.wait_ge(sem("f_h_hi"), f_count(f, "h_hi", 2 * i + c + 1))
                nc.vector.tensor_tensor(fh[1][:, p, cols(c)], f_h[:, c], f32(fh[0][:, p, cols(c)]),
                                        ALU.subtract).then_inc(sem("f_h_split"), 1)

        def f_sp(sp, n, f):
            x_final(sp, n, CHUNKS - 1)
            sp.dma_start(rw_raw[:], router_w).then_inc(sem("f_rw_loaded"), 16)
            for p in range(2):
                sp.dma_start(fw_raw[:, p], ffn_w[p * P:(p + 1) * P, :]).then_inc(sem(f"f_w_loaded{p}"), 16)
            with sp.Fori(0, F_TILES // 2 - 1) as i2:
                for p in range(2):
                    sp.wait_ge(sem("f_d_split"), f_count(f, "d_split", 2 * i2 + p + 1))
                    sp.dma_start(fw_raw[:, p], ffn_w[bass.ds(i2 * (2 * P) + (2 + p) * P, P), :]).then_inc(sem(f"f_w_loaded{p}"), 16)

        def b_pe(pe):
            pe.wait_ge(sem("b_bg_w"), 1)
            for c in range(CHUNKS):
                normed(pe, 2, c)
                for s in range(2):
                    for k in range(KT):
                        ins = mm3(ps[:, 4 + 2 * s + c, :], at(wbg, slice(None), k, s), at(xn, slice(None), k, cols(c)),
                                  k == 0, k == KT - 1)
                ins.then_inc(sem("b_bg_done"), 1)
            b_make_pe(pe, 0, 0, B_MAKE[:-1])
            pe.wait_ge(sem("b_cum"), 1)
            cum_transpose_pe(bg_cum, 7).then_inc(sem("b_cumT"), 1)
            b_make_pe(pe, 0, 0, B_MAKE[-1:])
            with pe.Fori(0, B_HEADS // 2 - 1) as h2:
                b_head_pe(pe, 2 * h2, 0, False)
                b_head_pe(pe, 2 * h2 + 1, 1, False)
            b_head_pe(pe, B_HEADS - 2, 0, False)
            b_head_pe(pe, B_HEADS - 1, 1, True)

        B_MAKE = ("fold", "qk0", "qk1", "values", "conv0", "conv1")

        FOLD_BANK = 3

        def b_bank(pe, h, slot):
            first = isinstance(h, int) and h == 0
            if slot < 2:
                if not first:
                    pe.wait_ge(sem("b_conv_y"), 4 * h - 1)
            elif slot < 4:
                pe.wait_ge(sem("q_read"), 4 * h + slot - 1)
            elif first and slot == 7:
                pe.wait_ge(sem("b_bg_read"), 2 * BATCH)
            elif slot < 6 if first else slot >= 6:
                pe.wait_ge(sem("q_read"), 4 * h + 3 + slot % 2)
            return b_slot(h, slot)

        def b_slot(h, slot):
            first = isinstance(h, int) and h == 0
            return ps[:, ((1, 0, 1, 0) + ((1, 0, 3, 5) if first else (6, 7, 1, 0)))[slot], :]

        def b_make_pe(pe, h, p, parts):
            for part in parts:
                if part == "fold":
                    pe.wait_ge(sem("wvo_split"), h + 1)
                    if not (isinstance(h, int) and h == 0):
                        pe.wait_ge(sem("v_split"), 4 * h)
                    o = ps[:, FOLD_BANK, :]
                    for k in range(KT):
                        for d in range(B_VT):
                            ins = mm3(o[:, k * DM:(k + 1) * DM], at(wvo, slice(None), 0, d, slice(k * P, (k + 1) * P)),
                                      at(wvo, slice(None), 1, d), k == 0 and d == 0, k == KT - 1 and d == B_VT - 1)
                    ins.then_inc(sem("b_fold_done"), 1)
                elif part in ("qk0", "qk1"):
                    s = int(part[-1])
                    if s == 0:
                        pe.wait_ge(sem("wqk_split"), h + 1)
                    for c in range(CHUNKS):
                        o = b_bank(pe, h, 2 * s + c)
                        for k in range(KT):
                            ins = mm3(o, at(wqk, slice(None), k, s), at(xn, slice(None), k, cols(c)), k == 0, k == KT - 1)
                        ins.then_inc(sem("b_proj_done"), 1)
                elif part == "values":
                    pe.wait_ge(sem("fold_split"), h + 1)
                    for i in range(BLOCKS // 2):
                        o = b_bank(pe, h, 4 + i)
                        for t in range(2):
                            tok = slice((2 * i + t) * P, (2 * i + t + 1) * P)
                            for k in range(KT):
                                ins = mm3(o[:, t * DM:(t + 1) * DM], at(xn, slice(None), k, tok), at(fold, slice(None), k),
                                          t == 0 and k == 0, t == 1 and k == KT - 1)
                        ins.then_inc(sem("b_v_done"), 1)
                else:
                    s = int(part[-1])
                    if s == 0:
                        pe.wait_ge(sem("wconv_split"), h + 1)
                        pe.wait_ge(sem("wsum_split"), h + 1)
                    pe.wait_ge(sem("qpad_split"), 4 * h + 2 * s + 2)
                    pe.wait_ge(sem("qsum_split"), 4 * h + 2 * s + 2)
                    for c in range(CHUNKS):
                        if s == 1:
                            pe.wait_ge(sem("b_conv_y"), 4 * h + c + 1)
                        elif isinstance(h, int) and h == 0:
                            pe.wait_ge(sem("v_split"), 2)
                        elif c == 0:
                            pe.wait_ge(sem("v_split"), 4 * h + 4)
                        else:
                            pe.wait_ge(sem("b_m_done"), BATCH * h - 1)
                        b_conv_pe(p, s, c).then_inc(sem("b_conv_done"), 1)

        def conv_banks(c):
            a, bc = ps[:, 2 * c, 0:2 * (PAIRS + 2)], ps[:, 1 + 3 * c, :]
            return (a.rearrange("p (b t) -> p b t", t=PAIRS + 2),
                    *(v.rearrange("p (b t) -> p b t", t=PAIRS) for v in (bc[:, 0:2 * PAIRS], bc[:, 2 * PAIRS:])))

        def b_conv_pe(p, s, c):
            a, b, cc = conv_banks(c)

            def inputs(plane, first, n):
                return at(planes, slice(None), s, slice(2 * c, 2 * c + 2), plane, slice(first, first + n))
            for j in range(2):
                mm3(a, at(wconv[p], slice(None), s, 2 * j), inputs(1, j, PAIRS + 2), j == 0, j == 1)
            for j in range(2):
                mm3(b, at(wconv[p], slice(None), s, 2 * j + 1), inputs(0, 1 + j, PAIRS), j == 0, False)
            for j in range(2):
                ins = mm3(cc, at(wsum[p], slice(None), s, j), inputs(2, 1 + j, PAIRS), False, j == 1)
            return ins

        def b_score_pe(pe, h, p, b, last):
            l0, u = b * SEQ, b % 2
            if b >= 2:
                pe.wait_ge(sem("b_m_done"), BATCH * h + b - 1)
            if b == 0:
                pe.wait_ge(sem("b_conv_y"), 4 * h + 4)
                pe.wait_ge(sem("b_pieces"), PIECES)
            if b == 1 and not last:
                pe.wait_ge(sem("fold_split"), h + 2)
            d, s = ps[:, 2 + u, :], ps[:, 4 + u, :]
            if b % 2 == 0:
                pe.wait_ge(sem("qk_split"), 4 * h + 3 + b // 2)
            lhs = rows_b[:, bass.ds(h, 1)].broadcast_to([P, P])
            nc.tensor.matmul(d[:, 0:TRI], lhs, pieces_b[:, b, :], start=True, stop=True, skip_group_check=True).then_inc(sem("b_d_done"), 1)
            mm3(first_m(s), at(qk[p], slice(None), 1, slice(l0, l0 + P)), halves(at(qk[p], slice(None), 0, slice(l0, l0 + SEQ))), True, False)
            mm3(s[:, P:2 * P], at(qk[p], slice(None), 1, slice(l0 + P, l0 + SEQ)),
                at(qk[p], slice(None), 0, slice(l0 + P, l0 + SEQ)), False).then_inc(sem("b_s_done"), 1)

        def b_value_pe(pe, h, p, b, last):
            u = b % 2
            pe.wait_ge(sem("b_m_split"), BATCH * h + b + 1)
            if b == 0:
                pe.wait_ge(sem("v_split"), 4 * h + 4)
            if b >= 2:
                pe.wait_ge(sem("x_updated3"), BATCH * h + b - 1)
            elif not last:
                pe.wait_ge(sem("v_split"), 4 * h + 5 + b)
            o, ms = ps[:, 6 + u, :], at(ms_b, slice(None), u)
            for d in range(KT):
                dv = slice(d * P, (d + 1) * P)
                mm3(half_view(o[:, d * SEQ:(d + 1) * SEQ]), at(vtok[p], slice(None), 2 * b, dv), tuple(first_m(v) for v in ms),
                    d == 0, False)
                ins = mm3(o[:, d * SEQ + P:(d + 1) * SEQ], at(vtok[p], slice(None), 2 * b + 1, dv),
                          at(ms, slice(None), slice(P, 2 * P)), False, d == KT - 1)
            ins.then_inc(sem("b_o_done"), 1)

        def b_head_pe(pe, h, p, last):
            make = (lambda *parts: None) if last else (lambda *parts: b_make_pe(pe, h + 1, 1 - p, parts))
            make("fold", "qk0", "qk1")
            b_score_pe(pe, h, p, 0, last)
            b_score_pe(pe, h, p, 1, last)
            make("values")
            b_value_pe(pe, h, p, 0, last)
            b_score_pe(pe, h, p, 2, last)
            b_score_pe(pe, h, p, 3, last)
            b_value_pe(pe, h, p, 1, last)
            make("conv0", "conv1")
            b_value_pe(pe, h, p, 2, last)
            b_value_pe(pe, h, p, 3, last)

        def b_prepare_act(act):
            act.wait_ge(sem("wbg_loaded"), 16)
            split_hi(at(wbg, slice(None)), wbg_raw[:], "wbg_hi")
            b_weights_act(act, "wqk", 0, 0)

        def b_prepare_rest_act(act):
            b_weights_act(act, "wvo", 0, 0)

        def b_act(act):
            act.wait_ge(sem("b_params"), 16)
            for c in range(CHUNKS):
                act.wait_ge(sem("b_bg_done"), c + 1)
                for b in range(2 * c, 2 * c + 2):
                    nc.scalar.activation(bg_z[of_batch(b), 0], ps[of_batch(b), 4 + c, (b % 2) * SEQ:(b % 2 + 1) * SEQ],
                                         ACT.Identity, bias=bpar[of_batch(b), 0:1]).then_inc(sem("b_bg_read"), 1)
                if c == 0:
                    b_weights_act(act, "wconv", 0, 0)
            act.wait_ge(sem("qpad_zero"), 4)
            b_make_act(act, 0, 0, B_MAKE[:3])
            act.wait_ge(sem("b_abs"), 1)
            nc.scalar.activation(bg_e[:], bg_e[:], ACT.Exp, scale=-1.0).then_inc(sem("b_exp"), 1)
            act.wait_ge(sem("b_exp"), 1)
            nc.scalar.activation(bg_e[:], bg_e[:], ACT.Ln, bias=1.0).then_inc(sem("b_ln"), 1)
            act.wait_ge(sem("v_split"), 2)
            for i in range(2, BLOCKS // 2):
                b_values_act(act, 0, 0, i)
            for name in ("wvo", "wqk"):
                b_weights_act(act, name, 1, 1)
            b_make_act(act, 0, 0, ["conv0"])
            act.wait_ge(sem("b_cumT"), 1)
            ncum_act(ncum_b, 7).then_inc(sem("b_ncum"), 1)
            b_weights_act(act, "wconv", 1, 1)
            b_make_act(act, 0, 0, ["conv1"])
            act.wait_ge(sem("b_ncum"), 1)
            with act.Fori(0, B_HEADS // 2 - 1) as h2:
                b_head_act(act, 2 * h2, 0, False, True)
                b_head_act(act, 2 * h2 + 1, 1, False, True)
            b_head_act(act, B_HEADS - 2, 0, False, False)
            b_head_act(act, B_HEADS - 1, 1, True, False)

        def b_make_act(act, h, p, parts):
            for part in parts:
                if part == "fold":
                    act.wait_ge(sem("b_fold_done"), h + 1)
                    nc.scalar.copy(fold[0][:], ps[:, FOLD_BANK, :].rearrange("p (k m) -> p k m", k=KT)).then_inc(sem("fold_hi"), 1)
                elif part in ("qk0", "qk1"):
                    s = int(part[-1])
                    for c in range(CHUNKS):
                        n = 4 * h + 2 * s + c
                        act.wait_ge(sem("b_proj_done"), n + 1)
                        if not (isinstance(h, int) and h == 0 and s == 0):
                            act.wait_ge(sem("qpad_split"), n - 1)
                        nc.scalar.copy(q32[:, c], ps[:, (1 + c) % 2, :].rearrange("p (b t r) -> p b r t", r=2, t=PAIRS)
                                       ).then_inc(sem("q_read"), 1)
                    for c in range(CHUNKS):
                        n = 4 * h + 2 * s + c
                        act.wait_ge(sem("q_read"), n + 1)
                        nc.scalar.copy(planes[0][:, s, 2 * c:2 * c + 2, 0:2, 2:2 + PAIRS], q32[:, c]).then_inc(sem("qpad_hi"), 1)
                        act.wait_ge(sem("qsum"), n + 1)
                        nc.scalar.copy(planes[0][:, s, 2 * c:2 * c + 2, 2, 2:2 + PAIRS], qsum[:, c]).then_inc(sem("qsum_hi"), 1)
                elif part == "values":
                    for i in range(BLOCKS // 2):
                        b_values_act(act, h, p, i)
                else:
                    s = int(part[-1])
                    for c in range(CHUNKS):
                        act.wait_ge(sem("b_conv_y"), 4 * h + 2 * s + c + 1)
                        if not (isinstance(h, int) and h == 0 and s == 0):
                            act.wait_ge(sem("qk_split"), 4 * h + 2 * s + c - 1)
                        nc.scalar.activation(qf[:, c], conv_y[:, c].rearrange("p b t r -> p (b t r)"), ACT.Silu,
                                             bias=conv_bias[:, p, s:s + 1]).then_inc(sem("b_silu"), 1)
                    if s == 0:
                        for c in range(CHUNKS):
                            act.wait_ge(sem("b_silu"), 4 * h + c + 1)
                            split_hi(at(qk[p], slice(None), 0, cols(c)), qf[:, c], "qk_hi")
                    else:
                        if isinstance(h, int) and h == B_HEADS - 1:
                            b_k_hi_act(act, h, p)
                        nc.scalar.activation(warm[:], mean_w[:, 0:1], ACT.Exp)

        def b_values_act(act, h, p, i):
            act.wait_ge(sem("b_v_done"), 4 * h + i + 1)
            nc.scalar.copy(vtok[p][0][:, 2 * i:2 * i + 2], b_slot(h, 4 + i).rearrange("p (t v) -> p t v", t=2)
                           ).then_inc(sem("v_hi"), 1)

        def b_weights_act(act, name, h, p):
            act.wait_ge(sem(f"{name}_loaded"), 16 * h + 16)
            if name == "wconv":
                nc.scalar.copy(conv_bias[:, p], wconv_raw_all[:, CONVW:])
            split_hi(at(B_SPLIT[name][p], slice(None)), B_RAW[name][:], f"{name}_hi")
            if name == "wconv":
                act.wait_ge(sem("wsum"), h + 1)
                split_hi(at(wsum[p], slice(None)), wsum_raw[:], "wsum_hi")

        def b_split_act(act, h, b):
            act.wait_ge(sem("b_m_done"), BATCH * h + b + 1)
            if b >= 2:
                act.wait_ge(sem("b_o_done"), BATCH * h + b - 1)
            split_hi(at(ms_b, slice(None), b % 2), m_b[:, b % 2, :], "b_m_hi")

        def b_score_act(act, h, b):
            act.wait_ge(sem("b_bounded"), BATCH * h + b + 1)
            nc.scalar.activation(e_b[:, b % 2], e_b[:, b % 2], ACT.Exp).then_inc(sem("b_e_done"), 1)

        def b_head_act(act, h, p, last, weights):
            make = (lambda *parts: None) if last else (lambda *parts: b_make_act(act, h + 1, 1 - p, parts))
            if not last:
                make("fold")
                b_k_hi_act(act, h, p)
                make("qk0", "qk1")
            values = (lambda i: None) if last else (lambda i: b_values_act(act, h + 1, 1 - p, i))
            values(0)
            b_score_act(act, h, 0)
            values(1)
            b_split_act(act, h, 0)
            b_score_act(act, h, 1)
            values(2)
            b_split_act(act, h, 1)
            values(3)
            if weights:
                for name in ("wqk", "wvo"):
                    b_weights_act(act, name, h + 2, p)
            b_score_act(act, h, 2)
            b_split_act(act, h, 2)
            b_score_act(act, h, 3)
            b_split_act(act, h, 3)
            if weights:
                b_weights_act(act, "wconv", h + 2, p)
            make("conv0", "conv1")

        def b_k_hi_act(act, h, p):
            for c in range(CHUNKS):
                act.wait_ge(sem("b_silu"), 4 * h + 2 + c + 1)
                split_hi(at(qk[p], slice(None), 1, cols(c)), qf[:, c], "qk_hi")

        def b_dve(dve):
            step = counter(dve, "b_dve_step")
            for s in range(2):
                nc.vector.memset(f32(planes[s][:, :, :, :, 0:2]), 0.0).then_inc(sem("qpad_zero"), 1)
                nc.vector.memset(f32(planes[s][:, :, :, :, 2 + PAIRS:]), 0.0).then_inc(sem("qpad_zero"), 1)
            step(nc.vector.memset(bg_ones[:], 1.0))
            step(nc.vector.memset(pieces_b[:], 0.0))
            dve.wait_ge(sem("b_params"), 16)
            for c in range(CHUNKS):
                dve.wait_ge(sem("b_bg_done"), c + 1)
                for b in range(2 * c, 2 * c + 2):
                    nc.vector.tensor_scalar(bg_z[of_batch(b), 1], ps[of_batch(b), 6 + c, (b % 2) * SEQ:(b % 2 + 1) * SEQ],
                                            bpar[of_batch(b), 1:2], None, ALU.add).then_inc(sem("b_bg_read"), 1)
            dve.wait_ge(sem("b_bg_read"), 2 * BATCH)
            nc.vector.scalar_tensor_tensor(bg_e[:], bg_z[:], -1.0, bg_z[:], ALU.mult, ALU.max).then_inc(sem("b_abs"), 1)
            b_make_dve(dve, 0, 0, B_MAKE[:3])
            for i in range(2):
                dve.wait_ge(sem("b_v_done"), i + 1)
                nc.vector.tensor_copy(vtok[0][0][:, 2 * i:2 * i + 2], b_slot(0, 4 + i).rearrange("p (t v) -> p t v", t=2)
                                      ).then_inc(sem("v_hi"), 1)
                b_values_dve(dve, 0, 0, i)
            dve.wait_ge(sem("b_ln"), 1)
            step(nc.vector.scalar_tensor_tensor(bg_z[:], bg_z[:], 0.0, bg_e[:], ALU.min, ALU.subtract))
            nc.vector.tensor_tensor_scan(bg_cum[:], bg_ones[:], bg_z[:, 0], 0.0, ALU.mult, ALU.add).then_inc(sem("b_cum"), 1)
            dve.wait_ge(sem("b_cum"), 1)
            step(nc.vector.tensor_tensor(bg_z[:, 1], bg_z[:, 1], bg_cum[:], ALU.add))
            b_make_dve(dve, 0, 0, ["conv0"])
            for i in range(2, BLOCKS // 2):
                b_values_dve(dve, 0, 0, i)
            split_pieces(dve, step, pieces_b, bg_z[:, 1], bg_p, "b_pieces", [0, 1])
            b_make_dve(dve, 0, 0, ["conv1"])
            split_pieces(dve, step, pieces_b, bg_z[:, 1], bg_p, "b_pieces", [2])
            with dve.Fori(0, B_HEADS // 2 - 1) as h2:
                b_head_dve(dve, 2 * h2, 0, False)
                b_head_dve(dve, 2 * h2 + 1, 1, False)
            b_head_dve(dve, B_HEADS - 2, 0, False)
            b_head_dve(dve, B_HEADS - 1, 1, True)

        def b_make_dve(dve, h, p, parts):
            for part in parts:
                if part == "fold":
                    dve.wait_ge(sem("fold_hi"), h + 1)
                    nc.vector.tensor_tensor(fold[1][:], ps[:, FOLD_BANK, :].rearrange("p (k m) -> p k m", k=KT), f32(fold[0][:]),
                                            ALU.subtract).then_inc(sem("fold_split"), 1)
                elif part in ("qk0", "qk1"):
                    s = int(part[-1])
                    for c in range(CHUNKS):
                        n = 4 * h + 2 * s + c
                        if not (isinstance(h, int) and h == 0 and s == 0):
                            dve.wait_ge(sem("qsum_split"), n - 1)
                        dve.wait_ge(sem("q_read"), n + 1)
                        nc.vector.tensor_tensor(qsum[:, c], q32[:, c, :, 0], q32[:, c, :, 1], ALU.add).then_inc(sem("qsum"), 1)
                        dve.wait_ge(sem("qpad_hi"), n + 1)
                        at_ = (slice(None), s, slice(2 * c, 2 * c + 2), slice(0, 2), slice(2, 2 + PAIRS))
                        nc.vector.tensor_tensor(planes[1][at_], q32[:, c], f32(planes[0][at_]), ALU.subtract).then_inc(sem("qpad_split"), 1)
                elif part == "values":
                    for i in range(BLOCKS // 2):
                        b_values_dve(dve, h, p, i)
                else:
                    s = int(part[-1])
                    for c in range(CHUNKS):
                        n = 4 * h + 2 * s + c
                        a, b, cc = conv_banks(c)
                        if not (isinstance(h, int) and h == 0 and s == 0):
                            dve.wait_ge(sem("b_silu"), n - 1)
                        dve.wait_ge(sem("b_conv_done"), n + 1)
                        y = conv_y[:, c]
                        nc.vector.tensor_copy(y[:, :, :, 0], b).then_inc(sem("b_conv_c"), 1)
                        dve.wait_ge(sem("b_conv_c"), 2 * n + 1)
                        nc.vector.tensor_tensor(y[:, :, :, 1], cc, y[:, :, :, 0], ALU.subtract).then_inc(sem("b_conv_c"), 1)
                        dve.wait_ge(sem("b_conv_c"), 2 * n + 2)
                        nc.vector.tensor_tensor(y[:, :, :, 0], y[:, :, :, 0], a[:, :, 0:PAIRS], ALU.add)
                        nc.vector.tensor_tensor(y[:, :, :, 1], y[:, :, :, 1], a[:, :, 1:1 + PAIRS], ALU.subtract).then_inc(sem("b_conv_y"), 1)

        def b_values_dve(dve, h, p, i):
            dve.wait_ge(sem("v_hi"), 4 * h + i + 1)
            at_ = (slice(None), slice(2 * i, 2 * i + 2))
            nc.vector.tensor_tensor(vtok[p][1][at_], b_slot(h, 4 + i).rearrange("p (t v) -> p t v", t=2),
                                    f32(vtok[p][0][at_]), ALU.subtract).then_inc(sem("v_split"), 1)

        def b_exponents_dve(dve, h, b):
            dve.wait_ge(sem("b_d_done"), BATCH * h + b + 1)
            dve.wait_ge(sem("b_ncum"), 1)
            exponents_dve(e_b[:, b % 2], ps[:, 2 + b % 2, :], ncum_b, b, h).then_inc(sem("b_bounded"), 1)

        def b_score_dve(dve, h, b):
            dve.wait_ge(sem("b_s_done"), BATCH * h + b + 1)
            dve.wait_ge(sem("b_e_done"), BATCH * h + b + 1)
            if b >= 2:
                dve.wait_ge(sem("b_m_split"), BATCH * h + b - 1)
            nc.vector.tensor_tensor(m_b[:, b % 2, :], ps[:, 4 + b % 2, 0:TRI], e_b[:, b % 2, :],
                                    ALU.mult).then_inc(sem("b_m_done"), 1)

        def b_value_dve(dve, h, b):
            dve.wait_ge(sem("b_o_done"), BATCH * h + b + 1)
            at_ = (slice(None), slice(None), slice(b * SEQ, (b + 1) * SEQ))
            nc.vector.tensor_tensor(x[at_], x[at_], ps[:, 6 + b % 2, :].rearrange("p (d l) -> p d l", d=KT),
                                    ALU.add).then_inc(sem("x_updated3"), 1)

        def b_head_dve(dve, h, p, last):
            make = (lambda *parts: None) if last else (lambda *parts: b_make_dve(dve, h + 1, 1 - p, parts))
            make("fold", "qk0", "qk1")
            for b in range(2):
                b_exponents_dve(dve, h, b)
            for b in range(2):
                b_score_dve(dve, h, b)
                if not last:
                    b_values_dve(dve, h + 1, 1 - p, b)
            if not last:
                for i in range(2, BLOCKS // 2):
                    b_values_dve(dve, h + 1, 1 - p, i)
            b_value_dve(dve, h, 0)
            for b in range(2, BATCH):
                b_exponents_dve(dve, h, b)
            for b in range(2, BATCH):
                b_score_dve(dve, h, b)
            make("conv0")
            b_value_dve(dve, h, 1)
            make("conv1")
            b_value_dve(dve, h, 2)
            b_value_dve(dve, h, 3)

        def b_pool(pool):
            split_lo(pool, at(wbg, slice(None)), wbg_raw[:], "wbg_hi", 1, "b_bg_w")
            b_weights_pool(pool, "wqk", 0, 0)
            b_wsum_pool(pool, 0)
            for name in ("wvo", "wconv"):
                b_weights_pool(pool, name, 0, 0)
            for s in range(2):
                b_qsum_pool(pool, 0, s)
            for name in ("wvo", "wqk"):
                b_weights_pool(pool, name, 1, 1)
            b_wsum_pool(pool, 1)
            b_conv_pool(pool, 0, 0, 0)
            b_weights_pool(pool, "wconv", 1, 1)
            b_conv_pool(pool, 0, 0, 1)
            with pool.Fori(0, B_HEADS // 2 - 1) as h2:
                b_head_pool(pool, 2 * h2, 0, True, True)
                b_head_pool(pool, 2 * h2 + 1, 1, True, True)
            b_head_pool(pool, B_HEADS - 2, 0, True, False)
            b_head_pool(pool, B_HEADS - 1, 1, False, False)

        def b_weights_pool(pool, name, h, p):
            split_lo(pool, at(B_SPLIT[name][p], slice(None)), B_RAW[name][:], f"{name}_hi", h + 1, f"{name}_split")
            if name == "wconv":
                split_lo(pool, at(wsum[p], slice(None)), wsum_raw[:], "wsum_hi", h + 1, "wsum_split")

        def b_wsum_pool(pool, h):
            pool.wait_ge(sem("wconv_loaded"), 16 * h + 16)
            taps = wconv_raw.rearrange("p s (j r) m -> p s j r m", r=2)
            nc.gpsimd.tensor_tensor(wsum_raw[:], taps[:, :, :, 0], taps[:, :, :, 1], ALU.add).then_inc(sem("wsum"), 1)

        def b_qsum_pool(pool, h, s):
            for c in range(CHUNKS):
                split_lo(pool, at(planes, slice(None), s, slice(2 * c, 2 * c + 2), 2, slice(2, 2 + PAIRS)), qsum[:, c],
                         "qsum_hi", 4 * h + 2 * s + c + 1, "qsum_split")

        def b_conv_pool(pool, h, p, s):
            for c in range(CHUNKS):
                split_lo(pool, at(qk[p], slice(None), s, cols(c)), qf[:, c], "qk_hi", 4 * h + 2 * s + c + 1, "qk_split")

        def b_score_pool(pool, h, b):
            split_lo(pool, at(ms_b, slice(None), b % 2), m_b[:, b % 2, :], "b_m_hi", BATCH * h + b + 1, "b_m_split")

        def b_head_pool(pool, h, p, make, weights):
            if make:
                b_qsum_pool(pool, h + 1, 0)
                b_qsum_pool(pool, h + 1, 1)
            b_score_pool(pool, h, 0)
            b_score_pool(pool, h, 1)
            if weights:
                b_wsum_pool(pool, h + 2)
                b_weights_pool(pool, "wqk", h + 2, p)
            b_score_pool(pool, h, 2)
            b_score_pool(pool, h, 3)
            if weights:
                b_weights_pool(pool, "wvo", h + 2, p)
            if make:
                b_conv_pool(pool, h + 1, 1 - p, 0)
            if weights:
                b_weights_pool(pool, "wconv", h + 2, p)
            if make:
                b_conv_pool(pool, h + 1, 1 - p, 1)

        B_RAW = dict(wqk=wqk_raw, wvo=wvo_raw, wconv=wconv_raw)
        B_SPLIT = dict(wqk=(wqk, wqk), wvo=(wvo, wvo), wconv=wconv)

        B_PARTS = (("wqk", wqk_raw, b_qk), ("wvo", wvo_raw, b_vo), ("wconv", wconv_raw_all, b_conv))

        def b_sp(sp):
            x_final(sp, 2, CHUNKS - 1)
            sp.dma_start(bpar[:], b_par).then_inc(sem("b_params"), 16)
            sp.dma_start(wbg_raw[:], b_bg).then_inc(sem("wbg_loaded"), 16)
            for name, raw, src in B_PARTS:
                sp.dma_start(raw[:], src[0:P, :]).then_inc(sem(f"{name}_loaded"), 16)
            for name, raw, src in B_PARTS:
                sp.wait_ge(sem(f"{name}_split"), 1)
                sp.dma_start(raw[:], src[P:2 * P, :]).then_inc(sem(f"{name}_loaded"), 16)
            with sp.Fori(0, B_HEADS - 2) as h:
                for name, raw, src in B_PARTS:
                    sp.wait_ge(sem(f"{name}_split"), h + 2)
                    sp.dma_start(raw[:], src[bass.ds(h * P + 2 * P, P), :]).then_inc(sem(f"{name}_loaded"), 16)

        block = ctx.enter_context(nc.Block())

        @block.sync
        def _(sp):
            for c in range(CHUNKS):
                sp.dma_start(x[:, :, cols(c)], xT[:, :, cols(c)]).then_inc(sem(f"x_loaded{c}"), 16)
            sp.dma_start(const[:], consts).then_inc(sem("consts_loaded"), 16)
            a_sp(sp)
            f_sp(sp, 1, 0)
            b_sp(sp)
            f_sp(sp, 3, 1)
            x_final(sp, 4, CHUNKS - 1)
            sp.dma_start(out, x[:]).then_inc(sem("out_stored"), 16)
            sp.wait_ge(sem("out_stored"), 16)

        @block.gpsimd
        def _(pool):
            a_pool(pool)
            f_pool(pool, 1, 0)
            b_pool(pool)
            f_pool(pool, 3, 1)

        @block.scalar
        def _(act):
            norm_act(act, 0, a_prepare_act, a_prepare_rest_act)
            a_act(act)
            norm_act(act, 1, lambda act: f_prepare_act(act, 0), lambda act: f_prepare_rest_act(act, 0))
            f_act(act, 1, 0)
            norm_act(act, 2, b_prepare_act, b_prepare_rest_act)
            b_act(act)
            norm_act(act, 3, lambda act: f_prepare_act(act, 1), lambda act: f_prepare_rest_act(act, 1))
            f_act(act, 3, 1)

        @block.vector
        def _(dve):
            nc.vector.memset(mean_w[:], 1.0 / DM).then_inc(sem("mean_made"), 1)
            nc.vector.memset(ones_w[:], 1.0).then_inc(sem("ones_made"), 1)
            a_early_dve(dve)
            dve.wait_ge(sem("consts_loaded"), 16)
            nc.vector.memset(zero_w[:], 0.0)
            nc.vector.memset(zero_x[:], 0.0)
            nc.vector.tensor_copy(rows_b[:], const[:, 3 * P:3 * P + 32])
            norm_dve(dve, 0)
            a_dve(dve)
            norm_dve(dve, 1)
            f_dve(dve, 1, 0)
            norm_dve(dve, 2)
            b_dve(dve)
            norm_dve(dve, 3)
            f_dve(dve, 3, 1)

        @block.tensor
        def _(pe):
            norm_pe(pe, 0)
            a_pe(pe)
            norm_pe(pe, 1)
            f_pe(pe, 1, 0)
            norm_pe(pe, 2)
            b_pe(pe)
            norm_pe(pe, 3)
            f_pe(pe, 3, 1)


def _constants():
    i = np.arange(P)
    c = np.zeros((P, N_CONST), np.float32)
    c[:, 0:P] = np.eye(P)
    c[:, P:2 * P] = np.where(i[None, :] >= i[:, None], BOUND, MASKED)
    c[:, 2 * P:3 * P] = BOUND
    c[:, 3 * P:3 * P + 32] = (i[:, None] % 32 == np.arange(32)[None, :]) & (i[:, None] < 96)
    return c


def _feature_major(w):
    return w.T.reshape(KT, P, w.shape[0]).transpose(1, 0, 2)


def _layout(i):
    c = np.ascontiguousarray
    i = {k: np.asarray(v) for k, v in i.items()}
    w = i["L0_attn_a_W_in"]
    hn = A_HEADS * A_STATE
    bc = w[2 * A_INNER:2 * A_INNER + 2 * hn].reshape(2, A_HEADS, A_STATE, KT, P)
    vg = w[:2 * A_INNER].reshape(2, A_TILES, P, KT, P)
    par = [i["L0_attn_a_conv_w"].reshape(A_TILES, P, A_TAPS).transpose(1, 0, 2).reshape(P, -1),
           i["L0_attn_a_conv_b"].reshape(A_TILES, P).T, i["L0_attn_a_D_param"].reshape(A_TILES, P).T,
           np.tile(i["L0_attn_a_A_log"], 4)[:, None], np.tile(i["L0_attn_a_dt_bias"], 4)[:, None]]
    a_wo = np.zeros((A_TILES + 1, P, DM), np.float32)
    a_wo[1:] = i["L0_attn_a_W_out"].T.reshape(A_TILES, P, DM)

    gu = np.zeros((F_TILES, 2, P, DM), np.float32)
    dn = np.zeros((F_TILES, P, DM), np.float32)
    sg = i["L0_ffn_shared_gate_up_w"].reshape(2, S_HIDDEN, DM)
    sd = i["L0_ffn_shared_down_w"].T
    for t in range(S_TILES):
        n = min(P, S_HIDDEN - t * P)
        gu[t, :, :n] = sg[:, t * P:t * P + n]
        dn[t, :n] = sd[t * P:t * P + n]
    gu[S_TILES:] = i["L0_ffn_w13"].reshape(EXPERTS, 2, R_TILES, ROWS_E, DM).transpose(2, 1, 0, 3, 4).reshape(R_TILES, 2, P, DM)
    dn[S_TILES:] = i["L0_ffn_w2"].reshape(EXPERTS, DM, R_TILES, ROWS_E).transpose(2, 0, 3, 1).reshape(R_TILES, P, DM)
    gu = gu.reshape(F_TILES, 2, P, KT, P).transpose(0, 4, 3, 1, 2).reshape(F_TILES, P, KT * 2 * P)
    rw = np.zeros((2, P, DM), np.float32)
    rw[0] = i["L0_ffn_sgate_w"]
    rw[1, :EXPERTS] = i["L0_ffn_gate_w"]

    qk = np.stack([i["L0_attn_b_Wq"], i["L0_attn_b_Wk"]]).reshape(2, B_HEADS, B_KD, KT, P)
    v = i["L0_attn_b_Wv"].reshape(B_HEADS, B_VT, P, DM).transpose(0, 2, 1, 3)
    cv = np.stack([i["L0_attn_b_Wq_conv"], i["L0_attn_b_Wk_conv"]]).reshape(2, B_HEADS, B_KD, P, B_TAPS)
    cb = np.stack([i["L0_attn_b_bq_conv"], i["L0_attn_b_bk_conv"]], axis=1)
    wo = i["L0_attn_b_Wo"].reshape(DM, B_HEADS, B_VT, P).transpose(1, 3, 2, 0)
    reps = P // B_HEADS
    bg = np.stack([np.tile(i["L0_attn_b_Wb"], (reps, 1)), np.tile(i["L0_attn_b_Wg"], (reps, 1))])
    bpar = [np.tile(i["L0_attn_b_bb"], reps)[:, None], np.tile(i["L0_attn_b_bg"], reps)[:, None]]
    return dict(
        xT=c(i["L0_attn_a_x"].reshape(TOKENS, KT, P).transpose(2, 1, 0)),
        consts=_constants(),
        a_vg=c(vg.transpose(4, 1, 3, 0, 2)),
        a_dt=c(_feature_major(np.tile(w[2 * A_INNER + 2 * hn:], (4, 1)))),
        a_heads=c(bc.transpose(1, 4, 3, 0, 2)).reshape(A_HEADS * P, KT * 2 * P),
        a_wo=a_wo.reshape(-1, DM),
        a_par=c(np.concatenate(par, axis=1)),
        ffn_w=c(np.concatenate([gu, dn], axis=2)).reshape(F_TILES * P, KT * 2 * P + DM),
        router_w=c(rw.reshape(2, P, KT, P).transpose(3, 2, 0, 1)),
        b_qk=c(qk.transpose(1, 4, 3, 0, 2)).reshape(B_HEADS * P, QKW),
        b_vo=c(np.stack([v, wo], axis=2)).reshape(B_HEADS * P, VOW),
        b_conv=c(np.concatenate([cv.transpose(1, 3, 0, 4, 2).reshape(B_HEADS * P, CONVW), cb], axis=1)),
        b_bg=c(bg.reshape(2, P, KT, P).transpose(3, 2, 0, 1)),
        b_par=c(np.concatenate(bpar, axis=1)),
    )


def kernel(**inputs):
    import concourse.bacc as bacc
    from concourse.bass_utils import run_bass_kernel_spmd

    arrays = _layout(inputs)
    nc = bacc.Bacc("TRN2", target_bir_lowering=False, num_devices=1)
    args = [nc.dram_tensor(k, a.shape, F32, kind="ExternalInput").ap() for k, a in arrays.items()]
    out = nc.dram_tensor("out", (P, KT, TOKENS), F32, kind="ExternalOutput").ap()
    build_layer(nc, *args, out)
    result = run_bass_kernel_spmd(nc, [arrays], core_ids=[0]).results[0]["out"]
    return np.ascontiguousarray(result.transpose(2, 1, 0)).reshape(BATCH, SEQ, DM)
```
